# Optimizing a Trainium2 kernel written in Bass

```python
import numpy as np
import jax
import jax.numpy as jnp

def _softmax(x, axis=-1):
    return jax.nn.softmax(x, axis=axis)

def _gelu(x):
    return jax.nn.gelu(x, approximate=True)

def _silu(x):
    return jax.nn.silu(x)

def _sigmoid(x):
    return jax.nn.sigmoid(x)

def _layernorm(x, axis=-1, eps=1e-05):
    m = jnp.mean(x, axis=axis, keepdims=True)
    v = jnp.var(x, axis=axis, keepdims=True)
    return (x - m) / jnp.sqrt(v + eps)

def _scatter_add(tgt, idx, src, axis=0):
    return tgt.at[idx].add(src)

def _segment_sum(src, seg, n):
    return jax.ops.segment_sum(src, seg, n)
kernel_name = 'mk_xattn_ffn_d1_seqx_r8_db6857'

def setup_inputs(seed: int=0):
    np.random.seed(seed)
    _w = jnp.asarray

    def _rec_inputs():
        import jax
        import jax.numpy as jnp
        _rk = jax.random.key(seed)
        x = -0.0002928 + 1 * jax.random.normal(jax.random.fold_in(_rk, 1), (8, 256, 128), jnp.float32)
        _lenS = 256 - jax.random.randint(jax.random.fold_in(_rk, 7), (8,), 0, max(1, 256 // 4) + 1, jnp.int32)
        _lenS2 = 256 - jax.random.randint(jax.random.fold_in(_rk, 8), (8,), 0, max(1, 256 // 4) + 1, jnp.int32)
        _ctx_1024P = jax.random.normal(jax.random.fold_in(_rk, 11), (8, 16, 128), jnp.float32)
        _ctx_1024c = jax.random.dirichlet(jax.random.fold_in(_rk, 511), 0.3 * jnp.ones((16,), jnp.float32), (8, 256))
        _ctx_1024t = jnp.einsum('bsk,bkd->bsd', _ctx_1024c, _ctx_1024P)
        _ctx_1024t = _ctx_1024t * jax.lax.rsqrt(jnp.mean(jnp.square(_ctx_1024t)) + 1e-12) * 0.953939
        ctx_1024 = -1.39393e-06 + 0.999914 * (_ctx_1024t + 0.3 * jax.random.normal(jax.random.fold_in(_rk, 611), (8, 256, 128), jnp.float32))
        return (x, ctx_1024)
    x, ctx_1024 = _rec_inputs()

    def _L0_xattn_setup():
        import jax, jax.numpy as jnp
        import numpy as np
        D_MODEL = 128
        NUM_HEADS = 16
        HEAD_DIM = D_MODEL // NUM_HEADS

        def _split_heads(x):
            B, S, D = x.shape
            return x.reshape(B, S, NUM_HEADS, HEAD_DIM).transpose(0, 2, 1, 3)
        key = jax.random.key(seed)
        ks = jax.random.split(key, 11)
        B, S, D = (2, 256, D_MODEL)
        scale = 1.0 / np.sqrt(D)
        inp = {'q': jax.random.normal(ks[0], (B, S, D), dtype=jnp.float32), 'k': jax.random.normal(ks[1], (B, S, D), dtype=jnp.float32), 'v': jax.random.normal(ks[2], (B, S, D), dtype=jnp.float32), 'Wq': jax.random.normal(ks[3], (D, D), dtype=jnp.float32) * scale, 'bq': jnp.zeros((D,), dtype=jnp.float32), 'Wk': jax.random.normal(ks[4], (D, D), dtype=jnp.float32) * scale, 'bk': jnp.zeros((D,), dtype=jnp.float32), 'Wv': jax.random.normal(ks[5], (D, D), dtype=jnp.float32) * scale, 'bv': jnp.zeros((D,), dtype=jnp.float32), 'Wo': jax.random.normal(ks[6], (D, D), dtype=jnp.float32) * scale, 'bo': jnp.zeros((D,), dtype=jnp.float32)}
        return inp
    _L0_xattn_all = _L0_xattn_setup()
    _L0_xattn_in = {k: v for k, v in _L0_xattn_all.items() if k in ('Wq', 'bq', 'Wk', 'bk', 'Wv', 'bv', 'Wo', 'bo')}
    del _L0_xattn_all

    def _L0_ffn_setup():
        import jax, jax.numpy as jnp
        import numpy as np
        S, B, D = (128, 2, 128)
        E, TOPK = (15, 3)
        F = 128
        FS = 256

        def _uinit(k, shape, out_dim):
            std = out_dim ** (-0.5)
            return jax.random.uniform(k, shape, jnp.float32, -std, std)
        key = jax.random.key(seed)
        ks = jax.random.split(key, 10)
        return {'x': jax.random.normal(ks[0], (S, B, D), jnp.float32), 'gate_w': jax.random.normal(ks[1], (E, D), jnp.float32) * D ** (-0.5), 'fc1_w': _uinit(ks[2], (E, 2 * F, D), 2 * F), 'fc1_b': _uinit(ks[3], (E, 2 * F), 2 * F), 'geglu_mult': jnp.ones((E, F), jnp.float32), 'fc2_w': _uinit(ks[4], (E, D, F), D), 'fc2_b': _uinit(ks[5], (E, D), D), 's_fc1_w': _uinit(ks[6], (2 * FS, D), 2 * FS), 's_fc1_b': _uinit(ks[7], (2 * FS,), 2 * FS), 's_geglu_mult': jnp.ones((FS,), jnp.float32), 's_fc2_w': _uinit(ks[8], (D, FS), D), 's_fc2_b': _uinit(ks[9], (D,), D)}
    _L0_ffn_all = _L0_ffn_setup()
    _L0_ffn_in = {k: v for k, v in _L0_ffn_all.items() if k in ('gate_w', 'fc1_w', 'fc1_b', 'geglu_mult', 'fc2_w', 'fc2_b', 's_fc1_w', 's_fc1_b', 's_geglu_mult', 's_fc2_w', 's_fc2_b')}
    del _L0_ffn_all
    return {'x': x, 'ctx_1024': ctx_1024, 'L0_xattn_Wq': _L0_xattn_in['Wq'], 'L0_xattn_bq': _L0_xattn_in['bq'], 'L0_xattn_Wk': _L0_xattn_in['Wk'], 'L0_xattn_bk': _L0_xattn_in['bk'], 'L0_xattn_Wv': _L0_xattn_in['Wv'], 'L0_xattn_bv': _L0_xattn_in['bv'], 'L0_xattn_Wo': _L0_xattn_in['Wo'], 'L0_xattn_bo': _L0_xattn_in['bo'], 'L0_ffn_gate_w': _L0_ffn_in['gate_w'], 'L0_ffn_fc1_w': _L0_ffn_in['fc1_w'], 'L0_ffn_fc1_b': _L0_ffn_in['fc1_b'], 'L0_ffn_geglu_mult': _L0_ffn_in['geglu_mult'], 'L0_ffn_fc2_w': _L0_ffn_in['fc2_w'], 'L0_ffn_fc2_b': _L0_ffn_in['fc2_b'], 'L0_ffn_s_fc1_w': _L0_ffn_in['s_fc1_w'], 'L0_ffn_s_fc1_b': _L0_ffn_in['s_fc1_b'], 'L0_ffn_s_geglu_mult': _L0_ffn_in['s_geglu_mult'], 'L0_ffn_s_fc2_w': _L0_ffn_in['s_fc2_w'], 'L0_ffn_s_fc2_b': _L0_ffn_in['s_fc2_b']}

def reference(x, ctx_1024, L0_xattn_Wq, L0_xattn_bq, L0_xattn_Wk, L0_xattn_bk, L0_xattn_Wv, L0_xattn_bv, L0_xattn_Wo, L0_xattn_bo, L0_ffn_gate_w, L0_ffn_fc1_w, L0_ffn_fc1_b, L0_ffn_geglu_mult, L0_ffn_fc2_w, L0_ffn_fc2_b, L0_ffn_s_fc1_w, L0_ffn_s_fc1_b, L0_ffn_s_geglu_mult, L0_ffn_s_fc2_w, L0_ffn_s_fc2_b):
    import jax
    import jax.numpy as jnp

    def _L0_xattn_ref(q, k, v, Wq, bq, Wk, bk, Wv, bv, Wo, bo):
        import jax, jax.numpy as jnp
        import numpy as np
        D_MODEL = 128
        NUM_HEADS = 16
        HEAD_DIM = D_MODEL // NUM_HEADS

        def _split_heads(x):
            B, S, D = x.shape
            return x.reshape(B, S, NUM_HEADS, HEAD_DIM).transpose(0, 2, 1, 3)
        B, S, D = q.shape
        qh = _split_heads(q @ Wq.T + bq)
        kh = _split_heads(k @ Wk.T + bk)
        vh = _split_heads(v @ Wv.T + bv)
        scores = jnp.einsum('bhqd,bhkd->bhqk', qh, kh) / jnp.sqrt(jnp.asarray(HEAD_DIM, dtype=qh.dtype))
        causal = jnp.tril(jnp.ones((S, S), dtype=bool))
        scores = jnp.where(causal[None, None], scores, -jnp.inf)
        attn = jax.nn.softmax(scores, axis=-1)
        out = jnp.einsum('bhqk,bhkd->bhqd', attn, vh)
        out = out.transpose(0, 2, 1, 3).reshape(B, S, D)
        return out @ Wo.T + bo

    def _L0_ffn_ref(x, gate_w, fc1_w, fc1_b, geglu_mult, fc2_w, fc2_b, s_fc1_w, s_fc1_b, s_geglu_mult, s_fc2_w, s_fc2_b):
        import jax, jax.numpy as jnp
        import numpy as np
        S, B, D = (128, 2, 128)
        E, TOPK = (15, 3)
        F = 128
        FS = 256

        def _uinit(k, shape, out_dim):
            std = out_dim ** (-0.5)
            return jax.random.uniform(k, shape, jnp.float32, -std, std)
        s, b, d = x.shape
        xt = x.reshape(-1, d)
        T = xt.shape[0]
        logits = xt @ gate_w.T
        scores = jax.nn.softmax(logits, axis=-1)
        topk_w, topk_idx = jax.lax.top_k(scores, TOPK)
        topk_w = topk_w / (jnp.sum(topk_w, axis=-1, keepdims=True) + 1e-20)
        comb = jnp.zeros((T, E), xt.dtype).at[jnp.arange(T)[:, None], topk_idx].add(topk_w)
        h = jnp.einsum('td,efd->etf', xt, fc1_w) + fc1_b[:, None, :]
        xh, g = (h[..., :F], h[..., F:])
        a = jax.nn.gelu(g, approximate=False) * xh * geglu_mult[:, None, :]
        yexp = jnp.einsum('etf,edf->etd', a, fc2_w) + fc2_b[:, None, :]
        y = jnp.einsum('etd,te->td', yexp, comb)
        hs = xt @ s_fc1_w.T + s_fc1_b
        xs, gs = (hs[..., :FS], hs[..., FS:])
        as_ = jax.nn.gelu(gs, approximate=False) * xs * s_geglu_mult
        ys = as_ @ s_fc2_w.T + s_fc2_b
        return (y + ys).reshape(s, b, d)
    x = x + _L0_xattn_ref(_layernorm(x, axis=-1), ctx_1024, ctx_1024, L0_xattn_Wq, L0_xattn_bq, L0_xattn_Wk, L0_xattn_bk, L0_xattn_Wv, L0_xattn_bv, L0_xattn_Wo, L0_xattn_bo)
    x = x + _L0_ffn_ref(_layernorm(x, axis=-1), L0_ffn_gate_w, L0_ffn_fc1_w, L0_ffn_fc1_b, L0_ffn_geglu_mult, L0_ffn_fc2_w, L0_ffn_fc2_b, L0_ffn_s_fc1_w, L0_ffn_s_fc1_b, L0_ffn_s_geglu_mult, L0_ffn_s_fc2_w, L0_ffn_s_fc2_b)
    return x

_drawn_inputs = setup_inputs


def setup_inputs(seed=0):
    import zlib

    import numpy as np

    out = dict(_drawn_inputs(seed))
    spreads = {'L0_xattn_bq': (0.0, 0.363),
     'L0_xattn_bk': (0.0, 0.8),
     'L0_xattn_bv': (0.0, 0.1),
     'L0_xattn_bo': (0.0, 0.1),
     'L0_ffn_geglu_mult': (1.0, 0.6),
     'L0_ffn_s_geglu_mult': (1.0, 0.6)}
    factors = {'L0_ffn_fc1_b': 8.0, 'L0_ffn_s_fc1_b': 8.0}
    for name, (base, spread) in spreads.items():
        noise = np.random.default_rng([zlib.crc32(name.encode()), seed]).standard_normal(out[name].shape)
        drawn = base * np.exp(spread * noise) if base else spread * noise
        out[name] = jnp.asarray(drawn.astype(out[name].dtype))
    for name, factor in factors.items():
        out[name] = (out[name] * factor).astype(out[name].dtype)
    return out
```

```python
from contextlib import ExitStack

import numpy as np

import concourse.bass as bass
from concourse import mybir

F32 = mybir.dt.float32
BF16 = mybir.dt.bfloat16
ACT = mybir.ActivationFunctionType
ALU = mybir.AluOpType
AX = mybir.AxisListType

P = 128
BATCHES, SEQ, D = 8, 256, 128
HEADS = 16
HD = D // HEADS
QT = SEQ // P
TILES = BATCHES * QT
E, TOPK, F, FS = 15, 3, 128, 256
SHARED = FS // F
EA = E + SHARED
SCALE = float(HD) ** -0.5
EPS = 1e-5
MASKED = -3.0e38
BANK = 512
GROUPS = 12
BURSTS = 6
TOPW = E + 1 + 8

Q_ROWS = [(0, 0, 3), (3, 0, 2), (5, 0, 1)]
K_ROWS = [(0, 0, 1), (1, 0, 1), (2, 0, 1), (3, 1, 1), (4, 1, 1), (5, 2, 1)]
QX_ROWS = [(0, 0, 2), (2, 0, 1)]
KX_ROWS = [(0, 0, 1), (1, 0, 1), (2, 1, 1)]
M_ROW = 6 * HD
S_SLOTS = [(0, 2), (2, 4), (4, 6), (6, 8), (8, 10), (10, 11), (11, 12)] + [(12, 12)] * 5


class Batch:

    def __init__(self, c, turn=None):
        self.c, self.turn = c, turn

    def __add__(self, n):
        return Batch(self.c + n, self.turn)

    @property
    def real(self):
        return 0 <= self.c < BATCHES

    @property
    def par(self):
        return self.c % 2

    def val(self, per, k):
        v = per * self.c + k
        return v if self.turn is None else self.turn * (2 * per) + v

    def half(self, per, k):
        v = per * (self.c // 2) + k
        return v if self.turn is None else self.turn * per + v

    def tile(self, width):
        v = self.c * width
        return v if self.turn is None else self.turn * (2 * width) + v


def steps(eng, step):
    for c in range(-3, 1):
        step(Batch(c))
    with eng.Fori(0, 2) as turn:
        step(Batch(1, turn))
        step(Batch(2, turn))
    for c in range(5, BATCHES + 1):
        step(Batch(c))


def head_of(r, i, j):
    return 8 * r + 2 * j + i


def build(nc, ins, out):
    with ExitStack() as ctx:
        def sb(name, shape, dt=F32):
            return ctx.enter_context(nc.sbuf_tensor(name, shape, dt))

        def ps(name):
            return ctx.enter_context(nc.psum_tensor(name, [P, BANK], F32))

        def sem(name):
            return ctx.enter_context(nc.semaphore(name))

        s_bank = [ps("s_bank0"), ps("s_bank1")]
        t_bank = [ps("t_bank0"), ps("t_bank1")]
        o_bank = [ps("o_bank0"), ps("o_bank1")]
        m_bank = [ps("m_bank0"), ps("m_bank1")]

        parts_dram = nc.dram_tensor("parts_dram", [2, 2, 3, P, SEQ], BF16).ap()

        ident = sb("ident", [P, P])
        identb = sb("identb", [P, P], BF16)
        mask_s = sb("mask_s", [P, P], BF16)
        mask_t = sb("mask_t", [P, P], BF16)
        half = sb("half", [P, 2])
        eps = sb("eps", [P, 2])
        flag = sb("flag", [P, 1])
        wq = sb("wq", [D, D])
        wk = sb("wk", [D, D])
        wv = sb("wv", [D, D])
        wo = sb("wo", [D, D])
        bq = sb("bq", [P, 1])
        bk = sb("bk", [P, 1])
        bv = sb("bv", [P, QT, D])
        bo = sb("bo", [P, QT, D])
        gate = sb("gate", [D, E])
        w1 = sb("w1", [D, EA, 2 * F])
        b1 = sb("b1", [F, EA, 2])
        w2 = sb("w2", [F, EA, D])
        mult = sb("mult", [F, EA])
        b2 = sb("b2", [32, D])

        x_all = sb("x_all", [P, TILES, D])
        x1_all = sb("x1_all", [P, TILES, D])
        x1nT_all = sb("x1nT_all", [D, TILES * P])
        ctxT = [sb(f"ctxT{i}", [D, SEQ]) for i in range(2)]
        stats1 = sb("stats1", [P, QT, 6])
        mv1 = sb("mv1", [P, QT, 2])
        ve1 = sb("ve1", [P, QT])
        rstd1 = sb("rstd1", [P, QT])
        xn = sb("xn", [P, QT, D])
        xnT = sb("xnT", [D, SEQ])
        qk32 = sb("qk32", [P, 2, SEQ])
        rest = sb("rest", [P, 2, SEQ])
        parts = [sb(f"parts{i}", [P, 3, 2, SEQ], BF16) for i in range(2)]
        qx = [sb(f"qx{i}", [P, HEADS, SEQ], BF16) for i in range(2)]
        kx = [sb(f"kx{i}", [P, HEADS, SEQ], BF16) for i in range(2)]
        qy = [sb(f"qy{i}", [P, HEADS, SEQ], BF16) for i in range(2)]
        ky = [sb(f"ky{i}", [P, HEADS, SEQ], BF16) for i in range(2)]
        negm = sb("negm", [P, QT, HEADS])
        mrest = sb("mrest", [P, QT, HEADS])
        zero32 = sb("zero32", [P, QT, HEADS])
        mparts = sb("mparts", [P, QT, P], BF16)
        mT = sb("mT", [3 * HEADS, SEQ], BF16)
        vaug = [sb(f"vaug{i}", [P, QT, HEADS, 32]) for i in range(2)]
        probs = sb("probs", [P, 4, BANK])
        o_sb = sb("o_sb", [P, BANK])
        rden = sb("rden", [P, QT * 2 * 4, 2])
        on = sb("on", [P, QT, D])
        onT = sb("onT", [D, SEQ])
        stats2 = sb("stats2", [P, QT, 6])
        mv2 = sb("mv2", [P, QT, 2])
        ve2 = sb("ve2", [P, QT])
        rstd2 = sb("rstd2", [P, QT])
        x1n = sb("x1n", [P, QT, D])
        x1nT = sb("x1nT", [D, SEQ])
        logits = sb("logits", [P, TILES, E + 1])

        x_in = sem("x_in")
        x_rest_in = sem("x_rest_in")
        ctx_in = [sem("ctx_in0"), sem("ctx_in1")]
        attn_w_in = sem("attn_w_in")
        ffn_w_in = sem("ffn_w_in")
        parts_out = [sem("parts_out0"), sem("parts_out1")]
        x_load = [sem("x_load0"), sem("x_load1")]
        y_load = [sem("y_load0"), sem("y_load1")]
        m_load = [sem("m_load0"), sem("m_load1")]
        x_zeroed = sem("x_zeroed")
        y_zeroed = sem("y_zeroed")
        v_ones = sem("v_ones")
        const_zero = sem("const_zero")
        consts = sem("consts")
        half_ready = sem("half_ready")
        ky_zero = sem("ky_zero")
        flag_set = sem("flag_set")
        mcut = sem("mcut")
        ln1_stats = sem("ln1_stats")
        ln1_mv = sem("ln1_mv")
        ln1_ve = sem("ln1_ve")
        ln1_rstd = sem("ln1_rstd")
        xn_ready = sem("xn_ready")
        xb_ready = sem("xb_ready")
        xnT_done = sem("xnT_done")
        xnT_evac = sem("xnT_evac")
        qk_done = sem("qk_done")
        qk_evac = sem("qk_evac")
        v_done = sem("v_done")
        v_evac = sem("v_evac")
        hi_ready = sem("hi_ready")
        mid_ready = sem("mid_ready")
        lo_ready = sem("lo_ready")
        rest_ready = sem("rest_ready")
        s_done = sem("s_done")
        s_reduced = sem("s_reduced")
        msplit = sem("msplit")
        mT_done = sem("mT_done")
        mT_evac = sem("mT_evac")
        t_done = sem("t_done")
        exp_done = sem("exp_done")
        av_done = sem("av_done")
        o_evac = sem("o_evac")
        oT_done = sem("oT_done")
        recip_done = sem("recip_done")
        norm_done = sem("norm_done")
        onT_done = sem("onT_done")
        onT_evac = sem("onT_evac")
        wo_done = sem("wo_done")
        x1_ready = sem("x1_ready")
        ln2_stats = sem("ln2_stats")
        ln2_mv = sem("ln2_mv")
        ln2_ve = sem("ln2_ve")
        ln2_rstd = sem("ln2_rstd")
        x1n_ready = sem("x1n_ready")
        x1nT_done = sem("x1nT_done")
        x1nT_evac = sem("x1nT_evac")
        gate_done = sem("gate_done")
        gate_evac = sem("gate_evac")

        lmax = sb("lmax", [P, TILES])
        probs_e = sb("probs_e", [P, TILES, TOPW])
        zsum = sb("zsum", [P, TILES])
        zinv = sb("zinv", [P, TILES])
        top8 = sb("top8", [P, TILES, 8])
        marked = sb("marked", [P, TILES, TOPW])
        wsum = sb("wsum", [P, TILES])
        winv = sb("winv", [P, TILES])
        comb = sb("comb", [P, TILES, EA])
        combT = sb("combT", [32, TILES, P])
        gelu = sb("gelu", [P, 3, SEQ])
        act_ = sb("act_", [P, 3, SEQ])
        seq = sem("gate_math")
        exp_gate = sem("exp_gate")
        comb_ready = sem("comb_ready")
        w2_scaled = sem("w2_scaled")
        combT_done = sem("combT_done")
        combT_evac = sem("combT_evac")
        bias_done = sem("bias_done")
        bias_added = sem("bias_added")
        h_done = sem("h_done")
        gelu_done = sem("gelu_done")
        a_ready = sem("a_ready")
        y_done = sem("y_done")
        y_added = sem("y_added")
        out_done = sem("out_done")
        h_bank = s_bank + t_bank
        y_bank = o_bank + m_bank

        def rows(dram, par, which, first, n):
            return dram[par, which, first:first + n].rearrange("r (d h) t -> (r d) (h t)", h=HEADS)

        block = ctx.enter_context(nc.Block())

        @block.sync
        def _(sp):
            x_v = ins["x"].rearrange("b (j p) d -> p (b j) d", p=P)
            sp.dma_start(x_all[:, 0:QT, :], x_v[:, 0:QT, :]).then_inc(x_in, 16)
            sp.dma_start(wq[:], ins["WqT"]).then_inc(attn_w_in, 16)
            sp.dma_start(wk[:], ins["WkT"]).then_inc(attn_w_in, 16)
            sp.dma_start(bq[:], ins["bq"]).then_inc(attn_w_in, 16)
            sp.dma_start(bk[:], ins["bk"]).then_inc(attn_w_in, 16)
            sp.dma_start(wv[:], ins["WvT"]).then_inc(attn_w_in, 16)
            for t in range(QT):
                sp.dma_start(bv[:, t, :], ins["bv"].partition_broadcast(P)).then_inc(attn_w_in, 16)
                sp.dma_start(bo[:, t, :], ins["bo"].partition_broadcast(P)).then_inc(attn_w_in, 16)
            sp.dma_start(wo[:], ins["WoT"]).then_inc(attn_w_in, 16)
            sp.dma_start(gate[:], ins["gateT"]).then_inc(attn_w_in, 16)
            sp.dma_start(x_all[:, QT:, :], x_v[:, QT:, :]).then_inc(x_rest_in, 16)

            def store_part(par, r):
                sp.dma_start(parts_dram[par, :, r].rearrange("k p t -> p k t"),
                             parts[par][:, r]).then_inc(parts_out[par], 16)

            def load(dst, which, table, par, done):
                for row, first, n in table:
                    sp.dma_start(dst[row * HD:(row + n) * HD].rearrange("p h t -> p (h t)"),
                                 rows(parts_dram, par, which, first, n)).then_inc(done, 16)

            def step(b):
                if (b + 1).real:
                    c, par = b + 1, (b + 1).par
                    if (b + -1).real:
                        sp.wait_ge(t_done, (b + -1).val(GROUPS, GROUPS))
                    else:
                        sp.wait_ge(y_zeroed, 4)
                    sp.wait_ge(parts_out[par], c.half(48, 48))
                    load(qy[par], 0, Q_ROWS, par, y_load[par])
                    load(ky[par], 1, K_ROWS, par, y_load[par])
                if (b + 3).real:
                    if (b + 1).real:
                        sp.wait_ge(v_done, (b + 1).val(1, 1))
                    sp.dma_start(ctxT[(b + 3).par][:], ins["ctxT"][:, bass.ds((b + 3).tile(SEQ), SEQ)]
                                 ).then_inc(ctx_in[(b + 3).par], 16)
                if (b + 2).real:
                    c, par = b + 2, (b + 2).par
                    sp.wait_ge(hi_ready, c.val(1, 1))
                    store_part(par, 0)
                    sp.wait_ge(mid_ready, c.val(1, 1))
                    store_part(par, 1)
                    sp.wait_ge(parts_out[par], c.half(48, 32))
                    if not b.real:
                        sp.wait_ge(x_zeroed, 4)
                    load(qx[par], 0, QX_ROWS, par, x_load[par])
                    load(kx[par], 1, KX_ROWS, par, x_load[par])
                    sp.wait_ge(lo_ready, c.val(1, 1))
                    store_part(par, 2)
                if b.c == -1:
                    sp.dma_start(w1[:], ins["w1T"]).then_inc(ffn_w_in, 16)
                    sp.dma_start(w2[:], ins["w2T"]).then_inc(ffn_w_in, 16)
                    sp.dma_start(b1[:], ins["b1"]).then_inc(ffn_w_in, 16)
                    sp.dma_start(mult[:], ins["mult"]).then_inc(ffn_w_in, 16)
                    sp.dma_start(b2[0:E, :], ins["b2"]).then_inc(ffn_w_in, 16)
                    sp.dma_start(b2[E:E + 1, :], ins["sb2"]).then_inc(ffn_w_in, 16)

            steps(sp, step)
            out_v = out.rearrange("b (j p) d -> p (b j) d", p=P)
            with sp.Fori(0, BATCHES) as c:
                sp.wait_ge(y_added, EA * QT * c + EA * QT + 1)
                sp.dma_start(out_v[:, bass.ds(c * QT, QT), :], x1_all[:, bass.ds(c * QT, QT), :]).then_inc(out_done, 16)
            sp.wait_ge(out_done, 16 * BATCHES)

        @block.tensor
        def _(pe):
            mm = nc.tensor.matmul

            def s_group(b, g):
                bank = s_bank[g % 2]
                n = GROUPS * b.c + g
                if g == 0:
                    pe.wait_ge(x_load[b.par], b.half(80, 80))
                if n >= 2:
                    pe.wait_ge(s_reduced, b.val(GROUPS, g - 1))
                if g < 4:
                    heads, keys, tile = range(4 * g, 4 * g + 4), P, 0
                else:
                    heads, keys, tile = range(2 * (g - 4), 2 * (g - 4) + 2), 2 * P, 1
                view = bank[:].rearrange("p (h k) -> p h k", k=keys)
                mm(view[:, :, keys - P:], identb[:], mask_s[:, None, :].to_broadcast([P, len(heads), P]),
                   start=True, stop=True)
                for k, h in enumerate(heads):
                    last = mm(view[:, k, :], qx[b.par][:, h, tile * P:(tile + 1) * P], kx[b.par][:, h, 0:keys],
                              start=False, stop=True, skip_group_check=True)
                last.then_inc(s_done, 1)

            def t_group(b, g):
                bank = t_bank[g % 2]
                if g == 0:
                    pe.wait_ge(y_load[b.par], b.half(144, 144))
                    pe.wait_ge(m_load[b.par], b.half(16, 16))
                if GROUPS * b.c + g >= 2:
                    pe.wait_ge(exp_done, b.val(GROUPS, g - 1))
                if g < 8:
                    r, i, jj = g // 4, g // 2 % 2, g % 2
                    heads = [head_of(r, i, 2 * jj + k) for k in range(2)]
                    queries, key0 = slice(0, 2 * P), 0
                else:
                    r, i = (g - 8) // 2, g % 2
                    heads = [head_of(r, i, j) for j in range(4)]
                    queries, key0 = slice(P, 2 * P), P
                view = bank[:].rearrange("p (h q) -> p h q", h=len(heads))
                mm(view[:, :, 0:P], identb[:], mask_t[:, None, :].to_broadcast([P, len(heads), P]),
                   start=True, stop=True)
                for k, h in enumerate(heads):
                    last = mm(view[:, k, :], ky[b.par][:, h, key0:key0 + P], qy[b.par][:, h, queries],
                              start=False, stop=True, skip_group_check=True)
                last.then_inc(t_done, 1)

            def av_burst(b, m):
                if m == 0:
                    pe.wait_ge(v_evac, b.val(2, 2))
                pe.wait_ge(exp_done, b.val(GROUPS, 2 * m + 2))
                bank = o_bank[b.par]
                for k in range(4 if m < 4 else 8):
                    if m < 4:
                        r, i, j, kt, q0 = m // 2, m % 2, k, 0, 0
                        src = probs[:, (2 * m + k // 2) % 4, (k % 2) * 2 * P:(k % 2 + 1) * 2 * P]
                    else:
                        r, i, j, kt, q0 = m - 4, k // 4, k % 4, 1, P
                        src = probs[:, (2 * m + i) % 4, j * P:(j + 1) * P]
                    last = mm(bank[32 * j:32 * j + 32, r * SEQ + q0:(r + 1) * SEQ],
                              vaug[b.par][:, kt, head_of(r, i, j), :], src,
                              start=(m == 0), stop=True, skip_group_check=True)
                last.then_inc(av_done, 1)

            def xn_transposes(b):
                pe.wait_ge(xn_ready, b.val(QT, QT))
                if (b + -2).real:
                    pe.wait_ge(mT_evac, (b + -2).val(1, 1))
                for t in range(QT):
                    last = nc.tensor.transpose(m_bank[0][:, t * P:(t + 1) * P], xn[:, t, :], ident[:])
                last.then_inc(xnT_done, 1)

            def qk_proj(b):
                if (b + -2).real:
                    pe.wait_ge(v_evac, (b + -2).val(2, 2))
                pe.wait_ge(xnT_evac, b.val(1, 1))
                pe.wait_ge(ctx_in[b.par], b.half(16, 16))
                mm(m_bank[1][:, 0:SEQ], wq[:], xnT[:], start=True, stop=True)
                mm(m_bank[1][:, SEQ:2 * SEQ], wk[:], ctxT[b.par][:], start=True, stop=True).then_inc(qk_done, 1)

            def v_proj(b):
                if (b + 1).real:
                    pe.wait_ge(qk_evac, (b + 1).val(2, 2))
                else:
                    pe.wait_ge(gate_evac, (b + -3).val(1, 1))
                for t in range(QT):
                    last = mm(m_bank[1][:, t * D:(t + 1) * D], ctxT[b.par][:, t * P:(t + 1) * P], wv[:],
                              start=True, stop=True)
                last.then_inc(v_done, 1)

            def o_transposes(b):
                pe.wait_ge(o_evac, b.val(1, 1))
                if (b + 3).real:
                    pe.wait_ge(xnT_evac, (b + 3).val(1, 1))
                elif (b + 1).real:
                    pe.wait_ge(mT_evac, (b + 1).val(1, 1))
                else:
                    pe.wait_ge(onT_evac, (b + -1).val(1, 1))
                for t in range(QT):
                    for r in range(2):
                        last = nc.tensor.transpose(m_bank[0][:, (2 * t + r) * P:(2 * t + r + 1) * P],
                                                   o_sb[:, r * SEQ + t * P:r * SEQ + (t + 1) * P], ident[:])
                last.then_inc(oT_done, 1)

            def on_transposes(b):
                pe.wait_ge(norm_done, b.val(1, 1))
                for t in range(QT):
                    last = nc.tensor.transpose(m_bank[0][:, t * P:(t + 1) * P], on[:, t, :], ident[:])
                last.then_inc(onT_done, 1)

            def out_proj(b):
                pe.wait_ge(onT_evac, b.val(1, 1))
                if (b + 2).real:
                    pe.wait_ge(v_evac, (b + 2).val(2, 2))
                elif (b + -1).real:
                    pe.wait_ge(gate_evac, (b + -1).val(1, 1))
                for t in range(QT):
                    last = mm(m_bank[1][:, t * D:(t + 1) * D], onT[:, t * P:(t + 1) * P], wo[:],
                              start=True, stop=True)
                last.then_inc(wo_done, 1)

            def m_transposes(b):
                pe.wait_ge(msplit, b.val(1, 1))
                if (b + -2).real:
                    pe.wait_ge(onT_evac, (b + -2).val(1, 1))
                elif (b + 1).real:
                    pe.wait_ge(xnT_evac, (b + 1).val(1, 1))
                dst = m_bank[0][:].bitcast(BF16)
                for t in range(QT):
                    last = nc.tensor.transpose(dst[:, t * P:(t + 1) * P], mparts[:, t, :], identb[:])
                last.then_inc(mT_done, 1)

            def x1n_transposes(b):
                pe.wait_ge(x1n_ready, b.val(QT, QT))
                for t in range(QT):
                    last = nc.tensor.transpose(m_bank[1][:, t * P:(t + 1) * P], x1n[:, t, :], ident[:])
                last.then_inc(x1nT_done, 1)

            def gate_logits(b):
                pe.wait_ge(x1nT_evac, b.val(2, 2))
                for t in range(QT):
                    last = mm(m_bank[1][:, 16 * t:16 * t + E], x1nT[:, t * P:(t + 1) * P], gate[:],
                              start=True, stop=True)
                last.then_inc(gate_done, 1)

            pe.wait_ge(consts, 4)
            pe.wait_ge(attn_w_in, 16 * 11)

            def step(b):
                for slot in range(GROUPS):
                    if (b + 1).real:
                        for g in range(*S_SLOTS[slot]):
                            s_group(b + 1, g)
                    if b.real:
                        t_group(b, slot)
                    if slot == 0 and (b + 2).real:
                        xn_transposes(b + 2)
                    if slot == 2 and (b + 2).real:
                        qk_proj(b + 2)
                    if slot == 3 and (b + -1).real:
                        o_transposes(b + -1)
                    if slot == 4 and (b + 1).real:
                        v_proj(b + 1)
                    if slot == 6 and (b + -1).real:
                        on_transposes(b + -1)
                    if slot == 8 and (b + -1).real:
                        out_proj(b + -1)
                    if slot == 9 and (b + 1).real:
                        m_transposes(b + 1)
                    if slot == 10 and (b + -1).real:
                        x1n_transposes(b + -1)
                    if slot == 11 and (b + -1).real:
                        gate_logits(b + -1)
                    if slot == 1 and (b + -1).real:
                        av_burst(b + -1, BURSTS - 1)
                    if slot % 2 and slot >= 3 and b.real:
                        av_burst(b, (slot - 3) // 2)

            steps(pe, step)

            pe.wait_ge(comb_ready, 1)
            for t in range(TILES):
                last = nc.tensor.transpose(h_bank[t // 4][0:EA, (t % 4) * P:(t % 4 + 1) * P], comb[:, t, :], ident[:])
                if t % 4 == 3:
                    last.then_inc(combT_done, 1)
            pe.wait_ge(ffn_w_in, 16 * 6)
            for t in range(TILES):
                if t % 4 == 0:
                    pe.wait_ge(combT_evac, t // 4 + 1)
                last = mm(y_bank[t // 4][:, (t % 4) * P:(t % 4 + 1) * P], combT[0:E + 1, t, :], b2[0:E + 1, :],
                          start=True, stop=True)
                if t % 4 == 3:
                    last.then_inc(bias_done, 1)
            pe.wait_ge(w2_scaled, EA)
            pe.wait_ge(bias_added, 4)

            with pe.Fori(0, BATCHES) as c:
                for e in range(EA + 2):
                    if e < EA:
                        pe.wait_ge(a_ready, EA * c + 1 + max(0, e - 3))
                        xc = x1nT_all[:, bass.ds(c * SEQ, SEQ)]
                        mm(h_bank[e % 4][:, 0:SEQ], w1[:, e, 0:F], xc, start=True, stop=True)
                        mm(h_bank[e % 4][:, SEQ:], w1[:, e, F:], xc, start=True, stop=True).then_inc(h_done, 1)
                    if e >= 2:
                        k = e - 2
                        pe.wait_ge(a_ready, EA * c + 1 + k + 1)
                        pe.wait_ge(y_added, EA * QT * c + 1 + QT * max(0, k - 3))
                        for t in range(QT):
                            last = mm(y_bank[k % 4][:, t * P:(t + 1) * P], act_[:, k % 3, t * P:(t + 1) * P], w2[:, k, :],
                                      start=True, stop=True)
                        last.then_inc(y_done, 1)

        @block.scalar
        def _(act):
            act.wait_ge(attn_w_in, 16 * 11)

            def step(b):
                for slot in range(GROUPS):
                    if b.real:
                        g = slot
                        act.wait_ge(t_done, b.val(GROUPS, g + 1))
                        if g >= 4:
                            act.wait_ge(av_done, b.val(BURSTS, (g - 4) // 2 + 1))
                        elif (b + -1).real:
                            act.wait_ge(av_done, b.val(BURSTS, (g - 4) // 2 + 1))
                        nc.scalar.activation(probs[:, g % 4, :], t_bank[g % 2][:], ACT.Exp,
                                             scale=SCALE).then_inc(exp_done, 1)
                    if slot == 0 and (b + 2).real:
                        act.wait_ge(xnT_done, (b + 2).val(1, 1))
                        if (b + 1).real:
                            act.wait_ge(qk_done, (b + 1).val(1, 1))
                        nc.scalar.activation(xnT[:], m_bank[0][:, 0:SEQ], ACT.Identity).then_inc(xnT_evac, 1)
                    if slot == 2 and (b + 2).real:
                        act.wait_ge(qk_done, (b + 2).val(1, 1))
                        if (b + 1).real:
                            act.wait_ge(rest_ready, (b + 1).val(1, 1))
                        for k, bias in enumerate((bq, bk)):
                            nc.scalar.activation(qk32[:, k, :], m_bank[1][:, k * SEQ:(k + 1) * SEQ], ACT.Identity,
                                                 bias=bias[:]).then_inc(qk_evac, 1)
                    if slot == 2 and (b + -1).real:
                        act.wait_ge(av_done, (b + -1).val(BURSTS, BURSTS))
                        nc.scalar.activation(o_sb[:], o_bank[(b + -1).par][:], ACT.Identity).then_inc(o_evac, 1)
                    if slot == 6 and (b + -1).real:
                        act.wait_ge(onT_done, (b + -1).val(1, 1))
                        nc.scalar.activation(onT[:], m_bank[0][:, 0:SEQ], ACT.Identity).then_inc(onT_evac, 1)
                    if slot == 9 and (b + 1).real:
                        act.wait_ge(mT_done, (b + 1).val(1, 1))
                        if b.real:
                            act.wait_ge(m_load[b.par], b.half(16, 16))
                        nc.scalar.activation(mT[:], m_bank[0][:].bitcast(BF16)[0:3 * HEADS, 0:SEQ],
                                             ACT.Identity).then_inc(mT_evac, 1)
                        act.wait_ge(mT_evac, (b + 1).val(1, 1))
                        if (b + -1).real:
                            act.wait_ge(t_done, (b + -1).val(GROUPS, GROUPS))
                        else:
                            act.wait_ge(y_zeroed, 4)
                        act.dma_start(qy[(b + 1).par][M_ROW:M_ROW + 3].rearrange("p h t -> p (h t)"),
                                      mT[:]).then_inc(m_load[(b + 1).par], 16)
                    if slot == 10 and (b + -1).real:
                        act.wait_ge(x1nT_done, (b + -1).val(1, 1))
                        for dst in (x1nT[:], x1nT_all[:, bass.ds((b + -1).tile(SEQ), SEQ)]):
                            nc.scalar.activation(dst, m_bank[1][:, 0:SEQ], ACT.Identity).then_inc(x1nT_evac, 1)

            steps(act, step)

            act.wait_ge(seq, 2)
            nc.scalar.activation(probs_e[:, :, 0:E], probs_e[:, :, 0:E], ACT.Exp).then_inc(exp_gate, 1)
            for k in range(4):
                act.wait_ge(combT_done, k + 1)
                nc.scalar.activation(combT[0:EA, 4 * k:4 * k + 4, :],
                                     h_bank[k][0:EA, :].rearrange("p (t q) -> p t q", t=4), ACT.Identity).then_inc(combT_evac, 1)
            with act.Fori(0, BATCHES) as c:
                for e in range(EA):
                    act.wait_ge(h_done, EA * c + e + 1)
                    act.wait_ge(a_ready, EA * c + 1 + max(0, e - 2))
                    nc.scalar.activation(gelu[:, e % 3, :], h_bank[e % 4][:, SEQ:], ACT.Gelu,
                                         bias=b1[:, e, 1:2]).then_inc(gelu_done, 1)

        @block.vector
        def _(dve):
            ones_pair = float(np.uint32(0x3F803F80).view(np.float32))
            for i in range(2):
                flat = ky[i][:].rearrange("p h t -> p (h t)").bitcast(F32)
                nc.vector.memset(flat, 0.0).then_inc(ky_zero, 1)
                dve.wait_ge(ky_zero, i + 1)
                nc.vector.memset(flat[32:64], ones_pair).then_inc(y_zeroed, 1)
            nc.vector.memset(probs_e[:], -1.0).then_inc(ky_zero, 1)

            def reduce(b, g):
                dve.wait_ge(s_done, b.val(GROUPS, g + 1))
                if g == 0 and (b + -1).real:
                    dve.wait_ge(msplit, (b + -1).val(1, 1))
                if g < 4:
                    dst, keys = negm[:, 0, 4 * g:4 * g + 4], P
                else:
                    dst, keys = negm[:, 1, 2 * (g - 4):2 * (g - 4) + 2], 2 * P
                nc.vector.tensor_reduce(dst, s_bank[g % 2][:].rearrange("p (h k) -> p h k", k=keys), AX.X, ALU.max,
                                        negate=True).then_inc(s_reduced, 1)

            def held_by(sem_, value):
                dve.wait_ge(sem_, value)
                nc.vector.memset(flag[:], 0.0).then_inc(flag_set, 1)

            def layer_norm_stats(src, stats, mv, s_stats, s_mv, b, guard):
                held_by(*guard)
                for t in range(QT):
                    nc.vector.bn_stats(stats[:, t, :], src[t]).then_inc(s_stats, 1)
                held_by(s_stats, b.val(QT, QT))
                for t in range(QT):
                    nc.vector.bn_aggr(mv[:, t, :], stats[:, t, :]).then_inc(s_mv, 1)

            def tiles_of(arr, b):
                return [arr[:, bass.ds(b.tile(QT) + t, 1), :].rearrange("p o d -> p (o d)") for t in range(QT)]

            def step(b):
                for slot in range(GROUPS):
                    if (b + 1).real:
                        for g in range(*S_SLOTS[slot]):
                            reduce(b + 1, g)
                    if slot == 3 and (b + 2).real:
                        par = (b + 2).par
                        dve.wait_ge(qk_evac, (b + 2).val(2, 2))
                        if b.real:
                            dve.wait_ge(parts_out[par], b.half(48, 48))
                        nc.vector.tensor_copy(parts[par][:, 0], qk32[:]).then_inc(hi_ready, 1)
                    if slot == 4 and (b + -1).real:
                        c = b + -1
                        dve.wait_ge(oT_done, c.val(1, 1))
                        view = m_bank[0][:].rearrange("p (g w) -> p g w", w=32)
                        nc.vector.reciprocal(rden[:], view[:, :, 2 * HD:4 * HD:HD]).then_inc(recip_done, 1)
                        dve.wait_ge(recip_done, c.val(1, 1))
                        nc.vector.tensor_tensor(
                            on[:].rearrange("p t (g i d) -> p (t g) i d", i=2, d=HD),
                            view[:, :, 0:2 * HD].rearrange("p g (i d) -> p g i d", d=HD),
                            rden[:, :, :, None].to_broadcast([P, QT * 8, 2, HD]), ALU.mult).then_inc(norm_done, 1)
                    if slot == 5 and (b + 1).real:
                        c = b + 1
                        dve.wait_ge(v_done, c.val(1, 1))
                        if (b + -1).real:
                            dve.wait_ge(av_done, (b + -1).val(BURSTS, BURSTS))
                        else:
                            dve.wait_ge(v_ones, 6)
                        for i in range(2):
                            nc.vector.tensor_tensor(
                                vaug[c.par][:].rearrange("p t (g i) w -> p (t g) (i w)", i=2)[:, :, i * 40:i * 40 + HD],
                                m_bank[1][:, 0:QT * D].rearrange("p (g i d) -> p g i d", i=2, d=HD)[:, :, i, :],
                                bv[:].rearrange("p t (g i d) -> p (t g) i d", i=2, d=HD)[:, :, i, :],
                                ALU.add).then_inc(v_evac, 1)
                    if slot == 6 and (b + 2).real:
                        par = (b + 2).par
                        dve.wait_ge(rest_ready, (b + 2).val(1, 1))
                        nc.vector.tensor_copy(parts[par][:, 1], rest[:]).then_inc(mid_ready, 1)
                    if slot == 7 and (b + 3).real:
                        c = b + 3
                        first = (x_in, 16) if c.c == 0 else (x_rest_in, 16)
                        layer_norm_stats(tiles_of(x_all, c), stats1, mv1, ln1_stats, ln1_mv, c, first)
                    if slot == 8 and (b + 3).real:
                        c = b + 3
                        dve.wait_ge(ln1_rstd, c.val(1, 1))
                        if (b + 2).real:
                            dve.wait_ge(xnT_done, (b + 2).val(1, 1))
                        for t, src in enumerate(tiles_of(x_all, c)):
                            nc.vector.tensor_scalar(xn[:, t, :], src, mv1[:, t, 0:1], rstd1[:, t:t + 1],
                                                    ALU.subtract, ALU.mult).then_inc(xn_ready, 1)
                    if slot == 9 and (b + -1).real:
                        c = b + -1
                        dve.wait_ge(wo_done, c.val(1, 1))
                        dve.wait_ge(xb_ready, c.val(1, 1))
                        nc.vector.tensor_tensor(
                            x1_all[:, bass.ds(c.tile(QT), QT), :], m_bank[1][:, 0:QT * D].rearrange("p (t d) -> p t d", d=D),
                            x_all[:, bass.ds(c.tile(QT), QT), :], ALU.add).then_inc(x1_ready, 1)
                        layer_norm_stats(tiles_of(x1_all, c), stats2, mv2, ln2_stats, ln2_mv, c,
                                         (x1_ready, c.val(1, 1)))
                    if slot == 10 and (b + -1).real:
                        c = b + -1
                        dve.wait_ge(ln2_rstd, c.val(1, 1))
                        for t, src in enumerate(tiles_of(x1_all, c)):
                            nc.vector.tensor_scalar(x1n[:, t, :], src, mv2[:, t, 0:1], rstd2[:, t:t + 1],
                                                    ALU.subtract, ALU.mult).then_inc(x1n_ready, 1)
                    if slot == 11 and (b + -1).real:
                        c = b + -1
                        dve.wait_ge(gate_done, c.val(1, 1))
                        nc.vector.tensor_copy(logits[:, bass.ds(c.tile(QT), QT), 0:E],
                                              m_bank[1][:, 0:32].rearrange("p (t e) -> p t e", e=16)[:, :, 0:E]
                                              ).then_inc(gate_evac, 1)

            steps(dve, step)

            sq = [0]

            def chained(ins_):
                ins_.then_inc(seq, 1)
                sq[0] += 1
                dve.wait_ge(seq, sq[0])

            def wide(v, w):
                return v[:, :, None].to_broadcast([P, TILES, w])

            pe_ = probs_e[:, :, 0:E]
            dve.wait_ge(gate_evac, BATCHES)
            chained(nc.vector.tensor_reduce(lmax[:], logits[:, :, 0:E], AX.X, ALU.max))
            chained(nc.vector.tensor_tensor(pe_, logits[:, :, 0:E], wide(lmax, E), ALU.subtract))
            dve.wait_ge(ffn_w_in, 16 * 6)
            for e in range(EA):
                nc.vector.tensor_scalar(w2[:, e, :], w2[:, e, :], mult[:, e:e + 1], None, ALU.mult).then_inc(w2_scaled, 1)
            dve.wait_ge(exp_gate, 1)
            chained(nc.vector.tensor_reduce(zsum[:], pe_, AX.X, ALU.add))
            chained(nc.vector.reciprocal(zinv[:], zsum[:]))
            chained(nc.vector.tensor_tensor(pe_, pe_, wide(zinv, E), ALU.mult))
            for t in range(TILES):
                last = nc.vector.max(top8[:, t, :], probs_e[:, t, :])
            chained(last)
            chained(nc.vector.memset(top8[:, :, TOPK:], -1.0))
            for t in range(TILES):
                last = nc.vector.match_replace(marked[:, t, :], top8[:, t, :], probs_e[:, t, :], -2.0)
            chained(last)
            chained(nc.vector.tensor_scalar(marked[:], marked[:], -2.0, None, ALU.is_equal))
            chained(nc.vector.tensor_tensor(marked[:, :, 0:E], marked[:, :, 0:E], pe_, ALU.mult))
            chained(nc.vector.tensor_reduce(wsum[:], marked[:, :, 0:E], AX.X, ALU.add))
            chained(nc.vector.tensor_scalar(wsum[:], wsum[:], 1e-20, None, ALU.add))
            chained(nc.vector.reciprocal(winv[:], wsum[:]))
            chained(nc.vector.memset(comb[:, :, E:], 1.0))
            nc.vector.tensor_tensor(comb[:, :, 0:E], marked[:, :, 0:E], wide(winv, E), ALU.mult).then_inc(comb_ready, 1)
            dve.wait_ge(comb_ready, 1)
            for k in range(4):
                dve.wait_ge(bias_done, k + 1)
                nc.vector.tensor_tensor(x1_all[:, 4 * k:4 * k + 4, :], y_bank[k][:].rearrange("p (t d) -> p t d", t=4),
                                        x1_all[:, 4 * k:4 * k + 4, :], ALU.add).then_inc(bias_added, 1)
            dve.wait_ge(bias_added, 4)
            nc.vector.memset(lmax[:], 0.0).then_inc(a_ready, 1)
            nc.vector.memset(zsum[:], 0.0).then_inc(y_added, 1)

            with dve.Fori(0, BATCHES) as c:
                for e in range(EA + 2):
                    if e < EA:
                        dve.wait_ge(gelu_done, EA * c + e + 1)
                        dve.wait_ge(y_done, EA * c + max(e - 2, 0)) if e > 2 else None
                        nc.vector.scalar_tensor_tensor(out=act_[:, e % 3, :], in0=h_bank[e % 4][:, 0:SEQ],
                                                       scalar=b1[:, e, 0:1], in1=gelu[:, e % 3, :], op0=ALU.add,
                                                       op1=ALU.mult).then_inc(a_ready, 1)
                    if e >= 2:
                        k = e - 2
                        dve.wait_ge(y_done, EA * c + k + 1)
                        for t in range(QT):
                            dve.wait_ge(y_added, EA * QT * c + 1 + max(0, QT * k + t - 1))
                            tile = x1_all[:, bass.ds(c * QT + t, 1), :].rearrange("p o d -> p (o d)")
                            w = comb[:, bass.ds(c * QT + t, 1), k:k + 1].rearrange("p o d -> p (o d)")
                            nc.vector.scalar_tensor_tensor(out=tile, in0=y_bank[k % 4][:, t * P:(t + 1) * P], scalar=w,
                                                           in1=tile, op0=ALU.mult, op1=ALU.add).then_inc(y_added, 1)

        @block.gpsimd
        def _(pool):
            g = nc.gpsimd
            for k, m in enumerate((ident, identb)):
                g.memset(m[:], 0.0).then_inc(const_zero, 1)
                pool.wait_ge(const_zero, k + 1)
                g.affine_select(out=m[:], in_=m[:], compare_op=ALU.not_equal, fill=1.0, base=0,
                                pattern=[[-1, P]], channel_multiplier=1).then_inc(consts, 1)
            for k, (m, step_, mult_) in enumerate(((mask_s, -1, 1), (mask_t, 1, -1))):
                g.memset(m[:], 0.0).then_inc(const_zero, 1)
                pool.wait_ge(const_zero, k + 3)
                g.affine_select(out=m[:], in_=m[:], compare_op=ALU.is_ge, fill=MASKED, base=0,
                                pattern=[[step_, P]], channel_multiplier=mult_).then_inc(consts, 1)
            g.memset(half[:], -0.5).then_inc(half_ready, 1)
            g.memset(eps[:], EPS).then_inc(half_ready, 1)
            g.memset(zero32[:], 0.0).then_inc(half_ready, 1)
            g.memset(mparts[:], 0.0).then_inc(half_ready, 1)
            for m in (qx[0], kx[0], qx[1], kx[1]):
                g.memset(m[:].rearrange("p h t -> p (h t)").bitcast(F32), 0.0).then_inc(x_zeroed, 1)
            pool.wait_ge(half_ready, 4)

            def rstd(b, mv, ve, out_, s_mv, s_ve, s_out):
                pool.wait_ge(s_mv, b.val(QT, QT))
                g.tensor_tensor(ve[:], mv[:, :, 1], eps[:], ALU.add).then_inc(s_ve, 1)
                pool.wait_ge(s_ve, b.val(1, 1))
                g.tensor_tensor(out_[:], ve[:], half[:], ALU.pow).then_inc(s_out, 1)

            def cut(r):
                return mparts[:, :, r * HEADS:(r + 1) * HEADS]

            def step(b):
                if b.c == -3:
                    for i in range(2):
                        g.memset(qy[i][:].rearrange("p h t -> p (h t)").bitcast(F32), 0.0).then_inc(y_zeroed, 1)
                        g.memset(vaug[i][:], 0.0).then_inc(v_ones, 1)
                    pool.wait_ge(v_ones, 2)
                    for i in range(2):
                        for k in range(2):
                            v = vaug[i][:].rearrange("p t (g i) w -> p (t g) (i w)", i=2)
                            g.memset(v[:, :, k * 40 + 2 * HD:k * 40 + 2 * HD + 1], 1.0).then_inc(v_ones, 1)
                if (b + 2).real:
                    c = b + 2
                    par = c.par
                    pool.wait_ge(hi_ready, c.val(1, 1))
                    g.tensor_tensor(rest[:], qk32[:], parts[par][:, 0], ALU.subtract).then_inc(rest_ready, 1)
                    pool.wait_ge(mid_ready, c.val(1, 1))
                    g.tensor_tensor(parts[par][:, 2], rest[:], parts[par][:, 1], ALU.subtract).then_inc(lo_ready, 1)
                if (b + 3).real:
                    c = b + 3
                    rstd(c, mv1, ve1, rstd1, ln1_mv, ln1_ve, ln1_rstd)
                if (b + 1).real:
                    c = b + 1
                    pool.wait_ge(s_reduced, c.val(GROUPS, GROUPS))
                    if b.real:
                        pool.wait_ge(mT_done, b.val(1, 1))
                    g.tensor_tensor(cut(0), negm[:], zero32[:], ALU.add).then_inc(mcut, 1)
                    pool.wait_ge(mcut, c.val(3, 1))
                    g.tensor_tensor(mrest[:], negm[:], cut(0), ALU.subtract).then_inc(mcut, 1)
                    pool.wait_ge(mcut, c.val(3, 2))
                    g.tensor_tensor(cut(1), mrest[:], zero32[:], ALU.add).then_inc(mcut, 1)
                    pool.wait_ge(mcut, c.val(3, 3))
                    g.tensor_tensor(cut(2), mrest[:], cut(1), ALU.subtract).then_inc(msplit, 1)
                if (b + 1).real:
                    c = b + 1
                    xs = x_all[:, bass.ds(c.tile(QT), QT), :]
                    pool.wait_ge(xn_ready, c.val(QT, QT))
                    g.tensor_tensor(xs, xs, bo[:], ALU.add).then_inc(xb_ready, 1)
                if (b + -1).real:
                    rstd(b + -1, mv2, ve2, rstd2, ln2_mv, ln2_ve, ln2_rstd)

            pool.wait_ge(attn_w_in, 16 * 11)
            steps(pool, step)


_HOST = {
    "x": lambda a: a["x"],
    "ctxT": lambda a: a["ctx_1024"].reshape(BATCHES * SEQ, D).T,
    "WqT": lambda a: by_dim(a["L0_xattn_Wq"]).T,
    "WkT": lambda a: by_dim(a["L0_xattn_Wk"]).T,
    "WvT": lambda a: a["L0_xattn_Wv"].T,
    "WoT": lambda a: a["L0_xattn_Wo"].T,
    "bq": lambda a: by_dim(a["L0_xattn_bq"].reshape(D, 1)),
    "bk": lambda a: by_dim(a["L0_xattn_bk"].reshape(D, 1)),
    "bv": lambda a: a["L0_xattn_bv"].reshape(1, D),
    "bo": lambda a: a["L0_xattn_bo"].reshape(1, D),
    "gateT": lambda a: a["L0_ffn_gate_w"].T,
    "w1T": lambda a: _stack(a["L0_ffn_fc1_w"].reshape(E, 2, F, D), a["L0_ffn_s_fc1_w"].reshape(2, SHARED, F, D)
                            .transpose(1, 0, 2, 3)).transpose(3, 0, 1, 2).reshape(D, EA, 2 * F),
    "b1": lambda a: _stack(a["L0_ffn_fc1_b"].reshape(E, 2, F), a["L0_ffn_s_fc1_b"].reshape(2, SHARED, F)
                           .transpose(1, 0, 2)).transpose(2, 0, 1),
    "w2T": lambda a: _stack(a["L0_ffn_fc2_w"], a["L0_ffn_s_fc2_w"].reshape(D, SHARED, F).transpose(1, 0, 2))
    .transpose(2, 0, 1),
    "mult": lambda a: _stack(a["L0_ffn_geglu_mult"], a["L0_ffn_s_geglu_mult"].reshape(SHARED, F)).T,
    "b2": lambda a: a["L0_ffn_fc2_b"],
    "sb2": lambda a: a["L0_ffn_s_fc2_b"].reshape(1, D),
}


def by_dim(w):
    return w.reshape(HEADS, HD, -1).transpose(1, 0, 2).reshape(D, -1)


def _stack(a, b):
    return np.concatenate([a, b], axis=0)


def kernel(**inputs):
    import concourse.bacc as bacc
    from concourse.bass_utils import run_bass_kernel_spmd

    given = {k: np.asarray(v) for k, v in inputs.items()}
    nc = bacc.Bacc("TRN2", target_bir_lowering=False, num_devices=1)
    arrays, ins = {}, {}
    for name, lay in _HOST.items():
        arrays[f"in_{name}"] = np.ascontiguousarray(lay(given))
        ins[name] = nc.dram_tensor(f"in_{name}", arrays[f"in_{name}"].shape, F32, kind="ExternalInput").ap()
    out = nc.dram_tensor("out", (BATCHES, SEQ, D), F32, kind="ExternalOutput").ap()
    build(nc, ins, out)
    r = run_bass_kernel_spmd(nc, [arrays], core_ids=[0])
    return r.results[0]["out"]
```

```python
from contextlib import ExitStack

import numpy as np

import concourse.bass as bass
from concourse import mybir

F32 = mybir.dt.float32
BF16 = mybir.dt.bfloat16
I32 = mybir.dt.int32
U32 = mybir.dt.uint32
ACT = mybir.ActivationFunctionType
ALU = mybir.AluOpType
AX = mybir.AxisListType

P = 128
BATCHES, SEQ, D = 8, 256, 128
HEADS = 16
HD = D // HEADS
QT = SEQ // P
TILES = BATCHES * QT
E, TOPK, F, FS = 15, 3, 128, 256
SHARED = FS // F
EA = E + SHARED
SCALE = float(HD) ** -0.5
EPS = 1e-5
MASKED = -3.0e38
BANK = 512
GROUPS = 12
BURSTS = 6
TOPW = E + 1 + 8

T = BATCHES * SEQ
ROW = D + 2
REGION = T + P
UNIT = REGION // P
UNROLL = 4
SLOT_TILES = -(-(T * TOPK // P + E - 1) // UNROLL) * UNROLL
ROW_GROUPS = SLOT_TILES // UNROLL
CHUNKS = 4
ROUNDS = [(0, 8), (8, 12), (12, 16)]
ROUND_AT = {5: 0, 7: 1}
DISPATCH_AT = {6: (0, 10), 7: (10, 24), 8: (24, 36)}
IOTAS = 9
TABLES = 3
NOBODY = 1.0e6

Q_ROWS = [(0, 0, 3), (3, 0, 2), (5, 0, 1)]
K_ROWS = [(0, 0, 1), (1, 0, 1), (2, 0, 1), (3, 1, 1), (4, 1, 1), (5, 2, 1)]
QX_ROWS = [(0, 0, 2), (2, 0, 1)]
KX_ROWS = [(0, 0, 1), (1, 0, 1), (2, 1, 1)]
M_ROW = 6 * HD
S_SLOTS = [(0, 2), (2, 4), (4, 6), (6, 8), (8, 10), (10, 11), (11, 12)] + [(12, 12)] * 5


class Batch:

    def __init__(self, c, turn=None):
        self.c, self.turn = c, turn

    def __add__(self, n):
        return Batch(self.c + n, self.turn)

    @property
    def real(self):
        return 0 <= self.c < BATCHES

    @property
    def par(self):
        return self.c % 2

    def val(self, per, k):
        v = per * self.c + k
        return v if self.turn is None else self.turn * (2 * per) + v

    def half(self, per, k):
        v = per * (self.c // 2) + k
        return v if self.turn is None else self.turn * per + v

    def tile(self, width):
        v = self.c * width
        return v if self.turn is None else self.turn * (2 * width) + v


def steps(eng, step):
    for c in range(-3, 1):
        step(Batch(c))
    with eng.Fori(0, 2) as turn:
        step(Batch(1, turn))
        step(Batch(2, turn))
    for c in range(5, BATCHES + 1):
        step(Batch(c))


class Group(Batch):

    def __add__(self, n):
        return Group(self.c + n, self.turn)

    @property
    def real(self):
        return 0 <= self.c < ROW_GROUPS


def group_steps(eng, step, first, full):
    turns = (ROW_GROUPS - 1 - full) // 2
    for c in range(first, full):
        step(Group(c))
    with eng.Fori(0, turns) as turn:
        step(Group(full, turn))
        step(Group(full + 1, turn))
    for c in range(full + 2 * turns, ROW_GROUPS + 1):
        step(Group(c))


def head_of(r, i, j):
    return 8 * r + 2 * j + i


def build(nc, ins, out):
    with ExitStack() as ctx:
        def sb(name, shape, dt=F32):
            return ctx.enter_context(nc.sbuf_tensor(name, shape, dt))

        def ps(name):
            return ctx.enter_context(nc.psum_tensor(name, [P, BANK], F32))

        def sem(name):
            return ctx.enter_context(nc.semaphore(name))

        s_bank = [ps("s_bank0"), ps("s_bank1")]
        t_bank = [ps("t_bank0"), ps("t_bank1")]
        o_bank = [ps("o_bank0"), ps("o_bank1")]
        m_bank = [ps("m_bank0"), ps("m_bank1")]

        parts_dram = nc.dram_tensor("parts_dram", [2, 2, 3, P, SEQ], BF16).ap()
        slots_dram = nc.dram_tensor("slots_dram", [(E + 1) * REGION, ROW], F32).ap()
        y_dram = nc.dram_tensor("y_dram", [TOPK * T, D], F32).ap()

        ident = sb("ident", [P, P])
        identb = sb("identb", [P, P], BF16)
        mask_s = sb("mask_s", [P, P], BF16)
        mask_t = sb("mask_t", [P, P], BF16)
        half = sb("half", [P, 2])
        eps = sb("eps", [P, 2])
        flag = sb("flag", [P, 1])
        wq = sb("wq", [D, D])
        wk = sb("wk", [D, D])
        wv = sb("wv", [D, D])
        wo = sb("wo", [D, D])
        bq = sb("bq", [P, 1])
        bk = sb("bk", [P, 1])
        bv = sb("bv", [P, QT, D])
        bo = sb("bo", [P, QT, D])
        gate = sb("gate", [D, E])
        w1 = sb("w1", [D, EA, 2 * F])
        b1 = sb("b1", [F, EA, 2])
        w2 = sb("w2", [F, EA, D])
        mult = sb("mult", [F, EA])
        b1_row = sb("b1_row", [P, E + 1, 2 * F])
        b2_row = sb("b2_row", [P, E + 1, D])
        before = sb("before", [P, P], BF16)
        upto = sb("upto", [P, P], BF16)
        ones = sb("ones", [P, P], BF16)
        ones32 = sb("ones32", [1, P])
        place0 = sb("place0", [P, E])
        full = sb("full", [P, SEQ // HEADS])
        tile_no = sb("tile_no", [P, SLOT_TILES])
        own = sb("own", [P, 1])
        pad_rows = sb("pad_rows", [P, ROW])

        x_all = sb("x_all", [P, TILES, D])
        x1_all = sb("x1_all", [P, TILES, D])
        x1nT_all = sb("x1nT_all", [D, TILES * P])
        ctxT = [sb(f"ctxT{i}", [D, SEQ]) for i in range(2)]
        stats1 = sb("stats1", [P, QT, 6])
        mv1 = sb("mv1", [P, QT, 2])
        ve1 = sb("ve1", [P, QT])
        rstd1 = sb("rstd1", [P, QT])
        xn = sb("xn", [P, QT, D])
        xnT = sb("xnT", [D, SEQ])
        qk32 = sb("qk32", [P, 2, SEQ])
        rest = sb("rest", [P, 2, SEQ])
        parts = [sb(f"parts{i}", [P, 3, 2, SEQ], BF16) for i in range(2)]
        qk_max = sb("qk_max", [P, 4, HEADS, SEQ], BF16)
        qx = [qk_max[:, i] for i in range(2)]
        kx = [qk_max[:, 2 + i] for i in range(2)]
        qy = [sb(f"qy{i}", [P, HEADS, SEQ], BF16) for i in range(2)]
        ky = [sb(f"ky{i}", [P, HEADS, SEQ], BF16) for i in range(2)]
        negm = sb("negm", [P, QT, HEADS])
        mrest = sb("mrest", [P, QT, HEADS])
        zero32 = sb("zero32", [P, QT, HEADS])
        mparts = sb("mparts", [P, QT, P], BF16)
        mT = sb("mT", [3 * HEADS, SEQ], BF16)
        vaug = [sb(f"vaug{i}", [P, QT, HEADS, 32]) for i in range(2)]
        probs = sb("probs", [P, 4, BANK])
        o_sb = sb("o_sb", [P, BANK])
        rden = sb("rden", [P, QT * 2 * 4, 2])
        on = sb("on", [P, QT, D])
        onT = sb("onT", [D, SEQ])
        stats2 = sb("stats2", [P, QT, 6])
        mv2 = sb("mv2", [P, QT, 2])
        ve2 = sb("ve2", [P, QT])
        rstd2 = sb("rstd2", [P, QT])
        x1n = sb("x1n", [P, QT, D])
        x1nT = sb("x1nT", [D, SEQ])
        logits = sb("logits", [P, TILES, E + 1])

        x_in = sem("x_in")
        x_rest_in = sem("x_rest_in")
        ctx_in = [sem("ctx_in0"), sem("ctx_in1")]
        attn_w_in = sem("attn_w_in")
        ffn_w_in = sem("ffn_w_in")
        parts_out = [sem("parts_out0"), sem("parts_out1")]
        x_load = [sem("x_load0"), sem("x_load1")]
        y_load = [sem("y_load0"), sem("y_load1")]
        m_load = [sem("m_load0"), sem("m_load1")]
        x_zeroed = sem("x_zeroed")
        y_zeroed = sem("y_zeroed")
        v_ones = sem("v_ones")
        const_zero = sem("const_zero")
        consts = sem("consts")
        half_ready = sem("half_ready")
        ky_zero = sem("ky_zero")
        flag_set = sem("flag_set")
        mcut = sem("mcut")
        ln1_stats = sem("ln1_stats")
        ln1_mv = sem("ln1_mv")
        ln1_ve = sem("ln1_ve")
        ln1_rstd = sem("ln1_rstd")
        xn_ready = sem("xn_ready")
        xb_ready = sem("xb_ready")
        xnT_done = sem("xnT_done")
        xnT_evac = sem("xnT_evac")
        qk_done = sem("qk_done")
        qk_evac = sem("qk_evac")
        v_done = sem("v_done")
        v_evac = sem("v_evac")
        hi_ready = sem("hi_ready")
        mid_ready = sem("mid_ready")
        lo_ready = sem("lo_ready")
        rest_ready = sem("rest_ready")
        s_done = sem("s_done")
        s_reduced = sem("s_reduced")
        msplit = sem("msplit")
        mT_done = sem("mT_done")
        mT_evac = sem("mT_evac")
        t_done = sem("t_done")
        exp_done = sem("exp_done")
        av_done = sem("av_done")
        o_evac = sem("o_evac")
        oT_done = sem("oT_done")
        recip_done = sem("recip_done")
        norm_done = sem("norm_done")
        onT_done = sem("onT_done")
        onT_evac = sem("onT_evac")
        wo_done = sem("wo_done")
        x1_ready = sem("x1_ready")
        ln2_stats = sem("ln2_stats")
        ln2_mv = sem("ln2_mv")
        ln2_ve = sem("ln2_ve")
        ln2_rstd = sem("ln2_rstd")
        x1n_ready = sem("x1n_ready")
        x1nT_done = sem("x1nT_done")
        x1nT_evac = sem("x1nT_evac")
        gate_done = sem("gate_done")
        gate_evac = sem("gate_evac")
        x1n_saved = sem("x1n_saved")

        def within(m, first, n, w):
            flat = m[:].rearrange("p h t -> p (h t)").bitcast(F32)
            return flat[:, first:first + n * w].rearrange("p (n w) -> p n w", w=w)

        lmax = sb("lmax", [P, TILES])
        probs_e = sb("probs_e", [P, TILES, TOPW])
        zsum = sb("zsum", [P, TILES])
        zinv = sb("zinv", [P, TILES])
        top8 = sb("top8", [P, TILES, 8])
        marked = sb("marked", [P, TILES, TOPW])
        wsum = sb("wsum", [P, TILES])
        winv = sb("winv", [P, TILES])
        comb = sb("comb", [P, TILES, E])
        rows_all = sb("rows_all", [P, TILES, ROW])
        mask_e = sb("mask_e", [P, TILES, E], BF16)
        place = sb("place", [P, TILES, E])
        top_place = sb("top_place", [P, TILES, 8])
        to_slot = sb("to_slot", [P, TILES, TOPK], I32)
        picked = sb("picked", [P, TILES, TOPK, E])
        weight = sb("weight", [P, TILES, TOPK])
        tile_ge = sb("tile_ge", [E, P // HD])
        n_tiles = sb("n_tiles", [E, 1])
        n_tiles_b = sb("n_tiles_b", [E, 1], BF16)
        skip = sb("skip", [E, 1])
        ends = sb("ends", [E, 1])
        passed = sb("passed", [E, 2, SLOT_TILES], BF16)
        tile_e = sb("tile_e", [P, SLOT_TILES], I32)
        tile_row = sb("tile_row", [P, SLOT_TILES])
        tile_row_i = sb("tile_row_i", [P, SLOT_TILES], I32)
        slot_row = sb("slot_row", [P, SLOT_TILES])
        pad_at = sb("pad_at", [P, 16], I32)
        gelu = within(qy[0], 0, 4, SEQ)
        act_ = within(qy[0], 4 * SEQ, 4, SEQ)
        slots = [within(qy[1], i * UNROLL * ROW, UNROLL, ROW) for i in range(2)]
        hb = within(ky[1], UNROLL * D, UNROLL, 2 * F)
        sxT = [within(ky[0], 0, UNROLL, P), within(ky[1], UNROLL * (D + 2 * F), UNROLL, P)]
        ge = within(ky[0], UNROLL * P, UNROLL, F)
        ae = within(ky[0], 2 * UNROLL * P, UNROLL, F)
        aeT = within(ky[0], 3 * UNROLL * P, UNROLL, P)
        ye = within(ky[1], 0, UNROLL, D)
        which_k = sb("which_k", [P, UNROLL])
        home_f = sb("home_f", [P, SLOT_TILES])
        home = sb("home", [P, UNROLL], I32)
        held = sb("held", [P, SLOT_TILES])
        held_dve = sb("held_dve", [P, 4])
        seq = sem("gate_math")
        less_max = sem("less_max")
        exp_gate = sem("exp_gate")
        w2_scaled = sem("w2_scaled")
        iotas = sem("iotas")
        mask_ready = sem("mask_ready")
        ranked = sem("ranked")
        rank_read = sem("rank_read")
        offs_ready = sem("offs_ready")
        tiles_counted = sem("tiles_counted")
        n_ready = sem("n_ready")
        ends_done = sem("ends_done")
        passed_ready = sem("passed_ready")
        tiles_known = sem("tiles_known")
        tables_ready = sem("tables_ready")
        dispatched = sem("dispatched")
        padded = sem("padded")
        sh_h_done = sem("sh_h_done")
        sh_gelu = sem("sh_gelu")
        sh_a = sem("sh_a")
        sh_y_done = sem("sh_y_done")
        sh_added = sem("sh_added")
        slot_in = [[sem(f"slot_in{i}{u}") for u in range(UNROLL)] for i in range(2)]
        x_turned = sem("x_turned")
        sxT_evac = sem("sxT_evac")
        h_done = sem("h_done")
        hb_ready = sem("hb_ready")
        ge_done = sem("ge_done")
        a_done = sem("a_done")
        aT_done = sem("aT_done")
        aT_evac = sem("aT_evac")
        y_done = sem("y_done")
        home_step = sem("home_step")
        y_ready = sem("y_ready")
        y_taken = sem("y_taken")
        scattered = [sem(f"scattered{u}") for u in range(UNROLL)]
        y_in = [sem(f"y_in{c}") for c in range(CHUNKS)]
        combined = sem("combined")
        weights_ready = sem("weights_ready")
        weighed = sem("weighed")
        added = sem("added")
        out_done = sem("out_done")
        h_bank = s_bank + t_bank
        y_all = qk_max[:].rearrange("p n h t -> p (n h t)").bitcast(F32).rearrange(
            "p (k t d) -> p k t d", t=TILES, d=D)[:, 0:TOPK]

        def reg_values(src, engine, top, why):
            return nc.values_load_multi_w_load_instructions(src, engines=[engine], min_val=0, max_val=top,
                                                            skip_runtime_bounds_check_because=why)[1]

        class Experts:

            def __init__(self, engine):
                self.engine, self.held = engine, {}

            def of(self, g):
                if (g.c, g.turn is None) not in self.held:
                    self.held[g.c, g.turn is None] = reg_values(
                        tile_e[0:1, bass.ds(g.val(UNROLL, 0), UNROLL)], self.engine, E, "counts at most E ends")
                return self.held[g.c, g.turn is None]

        def rows(dram, par, which, first, n):
            return dram[par, which, first:first + n].rearrange("r (d h) t -> (r d) (h t)", h=HEADS)

        block = ctx.enter_context(nc.Block())

        @block.sync
        def _(sp):
            x_v = ins["x"].rearrange("b (j p) d -> p (b j) d", p=P)
            sp.dma_start(x_all[:, 0:QT, :], x_v[:, 0:QT, :]).then_inc(x_in, 16)
            sp.dma_start(wq[:], ins["WqT"]).then_inc(attn_w_in, 16)
            sp.dma_start(wk[:], ins["WkT"]).then_inc(attn_w_in, 16)
            sp.dma_start(bq[:], ins["bq"]).then_inc(attn_w_in, 16)
            sp.dma_start(bk[:], ins["bk"]).then_inc(attn_w_in, 16)
            sp.dma_start(wv[:], ins["WvT"]).then_inc(attn_w_in, 16)
            for t in range(QT):
                sp.dma_start(bv[:, t, :], ins["bv"].partition_broadcast(P)).then_inc(attn_w_in, 16)
                sp.dma_start(bo[:, t, :], ins["bo"].partition_broadcast(P)).then_inc(attn_w_in, 16)
            sp.dma_start(wo[:], ins["WoT"]).then_inc(attn_w_in, 16)
            sp.dma_start(gate[:], ins["gateT"]).then_inc(attn_w_in, 16)
            sp.dma_start(x_all[:, QT:, :], x_v[:, QT:, :]).then_inc(x_rest_in, 16)

            def store_part(par, r):
                sp.dma_start(parts_dram[par, :, r].rearrange("k p t -> p k t"),
                             parts[par][:, r]).then_inc(parts_out[par], 16)

            def load(dst, which, table, par, done):
                for row, first, n in table:
                    sp.dma_start(dst[row * HD:(row + n) * HD].rearrange("p h t -> p (h t)"),
                                 rows(parts_dram, par, which, first, n)).then_inc(done, 16)

            def step(b):
                if (b + 1).real:
                    c, par = b + 1, (b + 1).par
                    if (b + -1).real:
                        sp.wait_ge(t_done, (b + -1).val(GROUPS, GROUPS))
                    else:
                        sp.wait_ge(y_zeroed, 4)
                    sp.wait_ge(parts_out[par], c.half(48, 48))
                    load(qy[par], 0, Q_ROWS, par, y_load[par])
                    load(ky[par], 1, K_ROWS, par, y_load[par])
                if (b + 3).real:
                    if (b + 1).real:
                        sp.wait_ge(v_done, (b + 1).val(1, 1))
                    sp.dma_start(ctxT[(b + 3).par][:], ins["ctxT"][:, bass.ds((b + 3).tile(SEQ), SEQ)]
                                 ).then_inc(ctx_in[(b + 3).par], 16)
                if (b + 2).real:
                    c, par = b + 2, (b + 2).par
                    sp.wait_ge(hi_ready, c.val(1, 1))
                    store_part(par, 0)
                    sp.wait_ge(mid_ready, c.val(1, 1))
                    store_part(par, 1)
                    sp.wait_ge(parts_out[par], c.half(48, 32))
                    if not b.real:
                        sp.wait_ge(x_zeroed, 4)
                    load(qx[par], 0, QX_ROWS, par, x_load[par])
                    load(kx[par], 1, KX_ROWS, par, x_load[par])
                    sp.wait_ge(lo_ready, c.val(1, 1))
                    store_part(par, 2)
                if b.c == -1:
                    sp.dma_start(w1[:], ins["w1T"]).then_inc(ffn_w_in, 16)
                    sp.dma_start(w2[:], ins["w2T"]).then_inc(ffn_w_in, 16)
                    sp.dma_start(b1[:], ins["b1"]).then_inc(ffn_w_in, 16)
                    sp.dma_start(mult[:], ins["mult"]).then_inc(ffn_w_in, 16)
                    sp.dma_start(b1_row[:].rearrange("p e f -> p (e f)"),
                                 ins["b1_row"].partition_broadcast(P)).then_inc(ffn_w_in, 16)
                    sp.dma_start(b2_row[:].rearrange("p e f -> p (e f)"),
                                 ins["b2_row"].partition_broadcast(P)).then_inc(ffn_w_in, 16)

            steps(sp, step)

            sp.wait_ge(iotas, IOTAS)
            sp.dma_start(slots_dram[E * REGION:E * REGION + P, :], pad_rows[:]).then_inc(padded, 16)
            sp.wait_ge(tables_ready, TABLES)
            at = reg_values(pad_at[0:1, 0:E], mybir.EngineType.SP, E * REGION, "a region has room for its rows")
            for e in range(E):
                sp.dma_start(slots_dram[bass.ds(at[e], P), :], pad_rows[:]).then_inc(padded, 16)
            sp.wait_ge(padded, 16 * (E + 1))
            sp.wait_ge(dispatched, 16 * TILES * TOPK)

            def load_group(g):
                row = reg_values(tile_row_i[0:1, bass.ds(g.val(UNROLL, 0), UNROLL)], mybir.EngineType.SP, E * REGION,
                                 "the last region's first row is the maximum")
                if (g + -2).real:
                    sp.wait_ge(home_step, (g + -2).val(3, 3))
                for u in range(UNROLL):
                    sp.dma_start(slots[g.par][:, u, :], slots_dram[bass.ds(row[u], P), :]).then_inc(slot_in[g.par][u], 16)

            load_group(Group(0))
            load_group(Group(1))
            with sp.Fori(0, ROW_GROUPS // 2 - 1) as turn:
                load_group(Group(2, turn))
                load_group(Group(3, turn))
            for u in range(UNROLL):
                sp.wait_ge(scattered[u], 16 * ROW_GROUPS)
            y_v = y_dram.rearrange("(k t p) d -> p k t d", k=TOPK, p=P)
            n = TILES // CHUNKS
            for c in range(CHUNKS):
                for k in range(TOPK):
                    sp.dma_start(y_all[:, k, c * n:(c + 1) * n, :], y_v[:, k, c * n:(c + 1) * n, :]).then_inc(y_in[c], 16)
            out_v = out.rearrange("b (j p) d -> p (b j) d", p=P)
            for c in range(CHUNKS):
                sp.wait_ge(combined, c + 1)
                sp.dma_start(out_v[:, c * n:(c + 1) * n, :], x1_all[:, c * n:(c + 1) * n, :]).then_inc(out_done, 16)
            sp.wait_ge(out_done, 16 * CHUNKS)

        @block.tensor
        def _(pe):
            mm = nc.tensor.matmul

            def s_group(b, g):
                bank = s_bank[g % 2]
                n = GROUPS * b.c + g
                if g == 0:
                    pe.wait_ge(x_load[b.par], b.half(80, 80))
                if n >= 2:
                    pe.wait_ge(s_reduced, b.val(GROUPS, g - 1))
                if g < 4:
                    heads, keys, tile = range(4 * g, 4 * g + 4), P, 0
                else:
                    heads, keys, tile = range(2 * (g - 4), 2 * (g - 4) + 2), 2 * P, 1
                view = bank[:].rearrange("p (h k) -> p h k", k=keys)
                mm(view[:, :, keys - P:], identb[:], mask_s[:, None, :].to_broadcast([P, len(heads), P]),
                   start=True, stop=True)
                for k, h in enumerate(heads):
                    last = mm(view[:, k, :], qx[b.par][:, h, tile * P:(tile + 1) * P], kx[b.par][:, h, 0:keys],
                              start=False, stop=True, skip_group_check=True)
                last.then_inc(s_done, 1)

            def t_group(b, g):
                bank = t_bank[g % 2]
                if g == 0:
                    pe.wait_ge(y_load[b.par], b.half(144, 144))
                    pe.wait_ge(m_load[b.par], b.half(16, 16))
                if GROUPS * b.c + g >= 2:
                    pe.wait_ge(exp_done, b.val(GROUPS, g - 1))
                if g < 8:
                    r, i, jj = g // 4, g // 2 % 2, g % 2
                    heads = [head_of(r, i, 2 * jj + k) for k in range(2)]
                    queries, key0 = slice(0, 2 * P), 0
                else:
                    r, i = (g - 8) // 2, g % 2
                    heads = [head_of(r, i, j) for j in range(4)]
                    queries, key0 = slice(P, 2 * P), P
                view = bank[:].rearrange("p (h q) -> p h q", h=len(heads))
                mm(view[:, :, 0:P], identb[:], mask_t[:, None, :].to_broadcast([P, len(heads), P]),
                   start=True, stop=True)
                for k, h in enumerate(heads):
                    last = mm(view[:, k, :], ky[b.par][:, h, key0:key0 + P], qy[b.par][:, h, queries],
                              start=False, stop=True, skip_group_check=True)
                last.then_inc(t_done, 1)

            def av_burst(b, m):
                if m == 0:
                    pe.wait_ge(v_evac, b.val(2, 2))
                pe.wait_ge(exp_done, b.val(GROUPS, 2 * m + 2))
                bank = o_bank[b.par]
                for k in range(4 if m < 4 else 8):
                    if m < 4:
                        r, i, j, kt, q0 = m // 2, m % 2, k, 0, 0
                        src = probs[:, (2 * m + k // 2) % 4, (k % 2) * 2 * P:(k % 2 + 1) * 2 * P]
                    else:
                        r, i, j, kt, q0 = m - 4, k // 4, k % 4, 1, P
                        src = probs[:, (2 * m + i) % 4, j * P:(j + 1) * P]
                    last = mm(bank[32 * j:32 * j + 32, r * SEQ + q0:(r + 1) * SEQ],
                              vaug[b.par][:, kt, head_of(r, i, j), :], src,
                              start=(m == 0), stop=True, skip_group_check=True)
                last.then_inc(av_done, 1)

            def xn_transposes(b):
                pe.wait_ge(xn_ready, b.val(QT, QT))
                if (b + -2).real:
                    pe.wait_ge(mT_evac, (b + -2).val(1, 1))
                for t in range(QT):
                    last = nc.tensor.transpose(m_bank[0][:, t * P:(t + 1) * P], xn[:, t, :], ident[:])
                last.then_inc(xnT_done, 1)

            def qk_proj(b):
                if (b + -2).real:
                    pe.wait_ge(v_evac, (b + -2).val(2, 2))
                pe.wait_ge(xnT_evac, b.val(1, 1))
                pe.wait_ge(ctx_in[b.par], b.half(16, 16))
                mm(m_bank[1][:, 0:SEQ], wq[:], xnT[:], start=True, stop=True)
                mm(m_bank[1][:, SEQ:2 * SEQ], wk[:], ctxT[b.par][:], start=True, stop=True).then_inc(qk_done, 1)

            def v_proj(b):
                if (b + 1).real:
                    pe.wait_ge(qk_evac, (b + 1).val(2, 2))
                else:
                    pe.wait_ge(gate_evac, (b + -3).val(1, 1))
                for t in range(QT):
                    last = mm(m_bank[1][:, t * D:(t + 1) * D], ctxT[b.par][:, t * P:(t + 1) * P], wv[:],
                              start=True, stop=True)
                last.then_inc(v_done, 1)

            def o_transposes(b):
                pe.wait_ge(o_evac, b.val(1, 1))
                if (b + 3).real:
                    pe.wait_ge(xnT_evac, (b + 3).val(1, 1))
                elif (b + 1).real:
                    pe.wait_ge(mT_evac, (b + 1).val(1, 1))
                else:
                    pe.wait_ge(onT_evac, (b + -1).val(1, 1))
                for t in range(QT):
                    for r in range(2):
                        last = nc.tensor.transpose(m_bank[0][:, (2 * t + r) * P:(2 * t + r + 1) * P],
                                                   o_sb[:, r * SEQ + t * P:r * SEQ + (t + 1) * P], ident[:])
                last.then_inc(oT_done, 1)

            def on_transposes(b):
                pe.wait_ge(norm_done, b.val(1, 1))
                for t in range(QT):
                    last = nc.tensor.transpose(m_bank[0][:, t * P:(t + 1) * P], on[:, t, :], ident[:])
                last.then_inc(onT_done, 1)

            def out_proj(b):
                pe.wait_ge(onT_evac, b.val(1, 1))
                if (b + 2).real:
                    pe.wait_ge(v_evac, (b + 2).val(2, 2))
                elif (b + -1).real:
                    pe.wait_ge(gate_evac, (b + -1).val(1, 1))
                for t in range(QT):
                    last = mm(m_bank[1][:, t * D:(t + 1) * D], onT[:, t * P:(t + 1) * P], wo[:],
                              start=True, stop=True)
                last.then_inc(wo_done, 1)

            def m_transposes(b):
                pe.wait_ge(msplit, b.val(1, 1))
                if (b + -2).real:
                    pe.wait_ge(onT_evac, (b + -2).val(1, 1))
                elif (b + 1).real:
                    pe.wait_ge(xnT_evac, (b + 1).val(1, 1))
                dst = m_bank[0][:].bitcast(BF16)
                for t in range(QT):
                    last = nc.tensor.transpose(dst[:, t * P:(t + 1) * P], mparts[:, t, :], identb[:])
                last.then_inc(mT_done, 1)

            def x1n_transposes(b):
                pe.wait_ge(x1n_ready, b.val(QT, QT))
                for t in range(QT):
                    last = nc.tensor.transpose(m_bank[1][:, t * P:(t + 1) * P], x1n[:, t, :], ident[:])
                last.then_inc(x1nT_done, 1)

            def gate_logits(b):
                pe.wait_ge(x1nT_evac, b.val(2, 2))
                for t in range(QT):
                    last = mm(m_bank[1][:, 16 * t:16 * t + E], x1nT[:, t * P:(t + 1) * P], gate[:],
                              start=True, stop=True)
                last.then_inc(gate_done, 1)

            def rank(r):
                t0, t1 = ROUNDS[r]
                view = s_bank[0][:, 0:(t1 - t0) * E].rearrange("p (t e) -> p t e", e=E)
                pe.wait_ge(mask_ready, r + 1)
                last = mm(view, before[:], mask_e[:, t0:t1, :], start=True, stop=True)
                for t in range(t1 - 1):
                    lo = max(t + 1, t0)
                    last = mm(view[:, lo - t0:, :], ones[:], mask_e[:, t:t + 1, :].to_broadcast([P, t1 - lo, E]),
                              start=False, stop=True, skip_group_check=True)
                last.then_inc(ranked, 1)

            pe.wait_ge(consts, 4)
            pe.wait_ge(attn_w_in, 16 * 11)

            def step(b):
                if b.c - 1 in ROUND_AT and (b + 1).real:
                    pe.wait_ge(rank_read, ROUND_AT[b.c - 1] + 1)
                for slot in range(GROUPS):
                    if (b + 1).real:
                        for g in range(*S_SLOTS[slot]):
                            s_group(b + 1, g)
                    if b.real:
                        t_group(b, slot)
                    if slot == 0 and (b + 2).real:
                        xn_transposes(b + 2)
                    if slot == 2 and (b + 2).real:
                        qk_proj(b + 2)
                    if slot == 3 and (b + -1).real:
                        o_transposes(b + -1)
                    if slot == 4 and (b + 1).real:
                        v_proj(b + 1)
                    if slot == 6 and (b + -1).real:
                        on_transposes(b + -1)
                    if slot == 8 and (b + -1).real:
                        out_proj(b + -1)
                    if slot == 9 and (b + 1).real:
                        m_transposes(b + 1)
                    if slot == 10 and (b + -1).real:
                        x1n_transposes(b + -1)
                    if slot == 11 and (b + -1).real:
                        gate_logits(b + -1)
                    if slot == 11 and b.c in ROUND_AT:
                        rank(ROUND_AT[b.c])
                    if slot == 1 and (b + -1).real:
                        av_burst(b + -1, BURSTS - 1)
                    if slot % 2 and slot >= 3 and b.real:
                        av_burst(b, (slot - 3) // 2)

            steps(pe, step)

            rank(len(ROUNDS) - 1)
            for t in range(TILES):
                mm(m_bank[1][0:E, 0:16], mask_e[:, t, :], ones[:, 0:16], start=(t == 0), stop=(t == TILES - 1))
            for t in range(TILES):
                last = mm(m_bank[1][:, 16:16 + E], ones[:], mask_e[:, t, :], start=False, stop=True,
                          skip_group_check=True)
            last.then_inc(tiles_counted, 1)
            pe.wait_ge(n_ready, 1)
            mm(o_bank[0][0:E, 0:16], upto[0:E, 0:E], n_tiles_b[:].to_broadcast([E, 16]), start=True, stop=True
               ).then_inc(ends_done, 1)
            pe.wait_ge(passed_ready, 1)
            mm(o_bank[1][:, 0:2 * SLOT_TILES], ones[0:E, :], passed[:].rearrange("p a j -> p (a j)"),
               start=True, stop=True).then_inc(tiles_known, 1)

            pe.wait_ge(ffn_w_in, 16 * 6)
            pe.wait_ge(w2_scaled, EA)
            pe.wait_ge(tables_ready, TABLES)
            with pe.Fori(0, BATCHES // 2) as i:
                for k in range(2):
                    xc = x1nT_all[:, bass.ds((2 * i + k) * SEQ, SEQ)]
                    for h in range(SHARED):
                        n = 2 * k + h
                        pe.wait_ge(sh_a, 4 * i + 1)
                        mm(h_bank[n][:, 0:SEQ], w1[:, E + h, 0:F], xc, start=True, stop=True)
                        mm(h_bank[n][:, SEQ:], w1[:, E + h, F:], xc, start=True, stop=True).then_inc(sh_h_done, 1)
                for k in range(2):
                    pe.wait_ge(sh_a, 4 * i + 2 * k + 3)
                    pe.wait_ge(sh_added, 2 * i + k + 1)
                    for t in range(QT):
                        yb = o_bank[k][:, t * P:(t + 1) * P]
                        mm(yb, ones32[:], b2_row[0:1, E, :], start=True, stop=False)
                        for h in range(SHARED):
                            last = mm(yb, act_[:, 2 * k + h, t * P:(t + 1) * P], w2[:, E + h, :],
                                      start=False, stop=(h == SHARED - 1))
                    last.then_inc(sh_y_done, 1)

            pe.wait_ge(sh_added, 2 + BATCHES)

            experts = Experts(mybir.EngineType.PE)

            def step(g):
                now, prev, nxt = g, g + -1, g + 1

                def turn_x(u):
                    if nxt.real:
                        pe.wait_ge(slot_in[nxt.par][u], nxt.half(16, 16))
                        nc.tensor.transpose(m_bank[0][:, u * P:(u + 1) * P], slots[nxt.par][:, u, 0:D], ident[:]
                                            ).then_inc(x_turned, 1)

                def fc1(u):
                    if now.real:
                        pe.wait_ge(sxT_evac, now.val(1, 1))
                        if prev.real:
                            pe.wait_ge(hb_ready, prev.val(UNROLL, u + 1))
                        mm(h_bank[u][:, 0:2 * F], sxT[now.par][:, u, :], w1[:, bass.ds(experts.of(now)[u], 1), :].rearrange("p o f -> p (o f)"),
                           start=True, stop=True).then_inc(h_done, 1)

                def turn_a(u):
                    if prev.real:
                        pe.wait_ge(a_done, prev.val(UNROLL, u + 1))
                        nc.tensor.transpose(m_bank[1][:, (u % 2) * P:(u % 2 + 1) * P], ae[:, u, :], ident[:]
                                            ).then_inc(aT_done, 1)

                def fc2(u):
                    if prev.real:
                        pe.wait_ge(aT_evac, prev.val(2, u // 2 + 1))
                        if (prev + -1).real and u % 2 == 0:
                            pe.wait_ge(y_taken, (prev + -1).val(UNROLL, u + 2))
                        mm(o_bank[u // 2][:, (u % 2) * D:(u % 2 + 1) * D], aeT[:, u, :],
                           w2[:, bass.ds(experts.of(prev)[u], 1), :].rearrange("p o f -> p (o f)"), start=True, stop=True
                           ).then_inc(y_done, 1)

                turn_a(0)
                turn_a(1)
                fc1(0)
                fc1(1)
                for u in range(UNROLL):
                    turn_x(u)
                if prev.real:
                    experts.of(prev)
                fc1(2)
                fc2(0)
                fc2(1)
                turn_a(2)
                turn_a(3)
                fc1(3)
                fc2(2)
                fc2(3)

            group_steps(pe, step, -1, 2)

        @block.scalar
        def _(act):
            act.wait_ge(attn_w_in, 16 * 11)

            def exp_round(r):
                t0, t1 = ROUNDS[r]
                act.wait_ge(less_max, r + 1)
                nc.scalar.activation(probs_e[:, t0:t1, 0:E], probs_e[:, t0:t1, 0:E], ACT.Exp).then_inc(exp_gate, 1)

            def step(b):
                for slot in range(GROUPS):
                    if b.real:
                        g = slot
                        act.wait_ge(t_done, b.val(GROUPS, g + 1))
                        if g >= 4:
                            act.wait_ge(av_done, b.val(BURSTS, (g - 4) // 2 + 1))
                        elif (b + -1).real:
                            act.wait_ge(av_done, b.val(BURSTS, (g - 4) // 2 + 1))
                        nc.scalar.activation(probs[:, g % 4, :], t_bank[g % 2][:], ACT.Exp,
                                             scale=SCALE).then_inc(exp_done, 1)
                    if slot == 8 and b.c in ROUND_AT:
                        exp_round(ROUND_AT[b.c])
                    if slot == 0 and (b + 2).real:
                        act.wait_ge(xnT_done, (b + 2).val(1, 1))
                        if (b + 1).real:
                            act.wait_ge(qk_done, (b + 1).val(1, 1))
                        nc.scalar.activation(xnT[:], m_bank[0][:, 0:SEQ], ACT.Identity).then_inc(xnT_evac, 1)
                    if slot == 2 and (b + 2).real:
                        act.wait_ge(qk_done, (b + 2).val(1, 1))
                        if (b + 1).real:
                            act.wait_ge(rest_ready, (b + 1).val(1, 1))
                        for k, bias in enumerate((bq, bk)):
                            nc.scalar.activation(qk32[:, k, :], m_bank[1][:, k * SEQ:(k + 1) * SEQ], ACT.Identity,
                                                 bias=bias[:]).then_inc(qk_evac, 1)
                    if slot == 2 and (b + -1).real:
                        act.wait_ge(av_done, (b + -1).val(BURSTS, BURSTS))
                        nc.scalar.activation(o_sb[:], o_bank[(b + -1).par][:], ACT.Identity).then_inc(o_evac, 1)
                    if slot == 6 and (b + -1).real:
                        act.wait_ge(onT_done, (b + -1).val(1, 1))
                        nc.scalar.activation(onT[:], m_bank[0][:, 0:SEQ], ACT.Identity).then_inc(onT_evac, 1)
                    if slot == 9 and (b + 1).real:
                        act.wait_ge(mT_done, (b + 1).val(1, 1))
                        if b.real:
                            act.wait_ge(m_load[b.par], b.half(16, 16))
                        nc.scalar.activation(mT[:], m_bank[0][:].bitcast(BF16)[0:3 * HEADS, 0:SEQ],
                                             ACT.Identity).then_inc(mT_evac, 1)
                        act.wait_ge(mT_evac, (b + 1).val(1, 1))
                        if (b + -1).real:
                            act.wait_ge(t_done, (b + -1).val(GROUPS, GROUPS))
                        else:
                            act.wait_ge(y_zeroed, 4)
                        act.dma_start(qy[(b + 1).par][M_ROW:M_ROW + 3].rearrange("p h t -> p (h t)"),
                                      mT[:]).then_inc(m_load[(b + 1).par], 16)
                    if slot == 10 and (b + -1).real:
                        act.wait_ge(x1nT_done, (b + -1).val(1, 1))
                        for dst in (x1nT[:], x1nT_all[:, bass.ds((b + -1).tile(SEQ), SEQ)]):
                            nc.scalar.activation(dst, m_bank[1][:, 0:SEQ], ACT.Identity).then_inc(x1nT_evac, 1)
                        nc.scalar.activation(rows_all[:, bass.ds((b + -1).tile(QT), QT), 0:D], x1n[:],
                                             ACT.Identity).then_inc(x1n_saved, 1)

            steps(act, step)

            exp_round(len(ROUNDS) - 1)
            act.wait_ge(ffn_w_in, 16 * 6)
            with act.Fori(0, BATCHES // 2) as i:
                for n in range(4):
                    act.wait_ge(sh_h_done, 4 * i + n + 1)
                    act.wait_ge(sh_a, 4 * i + 1)
                    nc.scalar.activation(gelu[:, n, :], h_bank[n][:, SEQ:], ACT.Gelu,
                                         bias=b1[:, E + n % 2, 1:2]).then_inc(sh_gelu, 1)

            def step(g):
                now, prev, nxt = g, g + -1, g + 1

                def evac_x():
                    if nxt.real:
                        act.wait_ge(x_turned, nxt.val(UNROLL, UNROLL))
                        nc.scalar.activation(sxT[nxt.par], m_bank[0][:].rearrange("p (u q) -> p u q", u=UNROLL),
                                             ACT.Identity).then_inc(sxT_evac, 1)

                def gelu_e(u):
                    if now.real:
                        act.wait_ge(hb_ready, now.val(UNROLL, u + 1))
                        nc.scalar.activation(ge[:, u, :], hb[:, u, F:], ACT.Gelu).then_inc(ge_done, 1)

                def evac_a(k):
                    if prev.real:
                        act.wait_ge(aT_done, prev.val(UNROLL, 2 * k + 2))
                        if (prev + -1).real:
                            act.wait_ge(y_done, (prev + -1).val(UNROLL, 2 * k + 2))
                        nc.scalar.activation(aeT[:, 2 * k:2 * k + 2, :],
                                             m_bank[1][:, 0:2 * P].rearrange("p (u q) -> p u q", u=2),
                                             ACT.Identity).then_inc(aT_evac, 1)

                evac_a(0)
                gelu_e(0)
                gelu_e(1)
                evac_x()
                evac_a(1)
                gelu_e(2)
                gelu_e(3)

            group_steps(act, step, -1, 2)

            n = TILES // CHUNKS
            act.wait_ge(weights_ready, len(ROUNDS))
            for c in range(CHUNKS):
                act.wait_ge(y_in[c], 16 * TOPK)
                for t in range(c * n, (c + 1) * n):
                    for k in range(1, TOPK):
                        nc.scalar.activation(y_all[:, k, t, :], y_all[:, k, t, :], ACT.Copy,
                                             scale=weight[:, t, k:k + 1]).then_inc(weighed, 1)

        @block.vector
        def _(dve):
            ones_pair = float(np.uint32(0x3F803F80).view(np.float32))
            for i in range(2):
                flat = ky[i][:].rearrange("p h t -> p (h t)").bitcast(F32)
                nc.vector.memset(flat, 0.0).then_inc(ky_zero, 1)
                dve.wait_ge(ky_zero, i + 1)
                nc.vector.memset(flat[32:64], ones_pair).then_inc(y_zeroed, 1)
            nc.vector.memset(probs_e[:], -1.0).then_inc(ky_zero, 1)

            def reduce(b, g):
                dve.wait_ge(s_done, b.val(GROUPS, g + 1))
                if g == 0 and (b + -1).real:
                    dve.wait_ge(msplit, (b + -1).val(1, 1))
                if g < 4:
                    dst, keys = negm[:, 0, 4 * g:4 * g + 4], P
                else:
                    dst, keys = negm[:, 1, 2 * (g - 4):2 * (g - 4) + 2], 2 * P
                nc.vector.tensor_reduce(dst, s_bank[g % 2][:].rearrange("p (h k) -> p h k", k=keys), AX.X, ALU.max,
                                        negate=True).then_inc(s_reduced, 1)

            def held_by(sem_, value):
                dve.wait_ge(sem_, value)
                nc.vector.memset(flag[:], 0.0).then_inc(flag_set, 1)

            def layer_norm_stats(src, stats, mv, s_stats, s_mv, b, guard):
                held_by(*guard)
                for t in range(QT):
                    nc.vector.bn_stats(stats[:, t, :], src[t]).then_inc(s_stats, 1)
                held_by(s_stats, b.val(QT, QT))
                for t in range(QT):
                    nc.vector.bn_aggr(mv[:, t, :], stats[:, t, :]).then_inc(s_mv, 1)

            def tiles_of(arr, b):
                return [arr[:, bass.ds(b.tile(QT) + t, 1), :].rearrange("p o d -> p (o d)") for t in range(QT)]

            sq = [0]

            def chained(ins_):
                ins_.then_inc(seq, 1)
                sq[0] += 1
                dve.wait_ge(seq, sq[0])

            def choose(r, part):
                t0, t1 = ROUNDS[r]
                n = t1 - t0
                ts = slice(t0, t1)
                pe_, lg, top = probs_e[:, ts, 0:E], logits[:, ts, 0:E], top8[:, ts]

                def wide(v, w=E):
                    return v[:, ts, None].to_broadcast([P, n, w])

                if part == 0:
                    dve.wait_ge(gate_evac, t1 // QT)
                    chained(nc.vector.tensor_reduce(lmax[:, ts], lg, AX.X, ALU.max))
                    nc.vector.tensor_tensor(pe_, lg, wide(lmax), ALU.subtract).then_inc(less_max, 1)
                if part == 1:
                    dve.wait_ge(exp_gate, r + 1)
                    chained(nc.vector.tensor_reduce(zsum[:, ts], pe_, AX.X, ALU.add))
                    chained(nc.vector.reciprocal(zinv[:, ts], zsum[:, ts]))
                    chained(nc.vector.tensor_tensor(pe_, pe_, wide(zinv), ALU.mult))
                    for t in range(t0, t1):
                        last = nc.vector.max(top8[:, t, :], probs_e[:, t, :])
                    chained(last)
                    chained(nc.vector.memset(top[:, :, TOPK:], -1.0))
                    for t in range(t0, t1):
                        last = nc.vector.match_replace(marked[:, t, :], top8[:, t, :], probs_e[:, t, :], -2.0)
                    chained(last)
                    nc.vector.tensor_scalar(mask_e[:, ts, :], marked[:, ts, 0:E], -2.0, None, ALU.is_equal
                                            ).then_inc(mask_ready, 1)
                    dve.wait_ge(mask_ready, r + 1)
                    chained(nc.vector.tensor_scalar(marked[:, ts, :], marked[:, ts, :], -2.0, None, ALU.is_equal))
                    chained(nc.vector.tensor_tensor(pe_, marked[:, ts, 0:E], pe_, ALU.mult))
                    chained(nc.vector.tensor_reduce(wsum[:, ts], pe_, AX.X, ALU.add))
                    chained(nc.vector.tensor_scalar(wsum[:, ts], wsum[:, ts], 1e-20, None, ALU.add))
                    chained(nc.vector.reciprocal(winv[:, ts], wsum[:, ts]))
                    nc.vector.tensor_tensor(comb[:, ts, :], pe_, wide(winv), ALU.mult)
                if part == 2:
                    dve.wait_ge(ranked, r + 1)
                    dve.wait_ge(iotas, IOTAS)
                    chained(nc.vector.tensor_tensor(
                        place[:, ts, :], s_bank[0][:, 0:n * E].rearrange("p (t e) -> p t e", e=E),
                        place0[:, None, :].to_broadcast([P, n, E]), ALU.add))
                    nc.vector.memset(held_dve[:, r:r + 1], 0.0).then_inc(rank_read, 1)
                    chained(nc.vector.tensor_tensor(place[:, ts, :], place[:, ts, :], marked[:, ts, 0:E], ALU.mult))
                    for t in range(t0, t1):
                        last = nc.vector.max(top_place[:, t, :], place[:, t, :])
                    chained(last)
                    nc.vector.tensor_scalar(rows_all[:, ts, D + 1:], top_place[:, ts, 1:2], -1.0, None, ALU.add)
                    nc.vector.tensor_scalar(to_slot[:, ts, :], top_place[:, ts, 0:TOPK], -1.0, None, ALU.add
                                            ).then_inc(offs_ready, 1)
                    chained(nc.vector.tensor_tensor(
                        picked[:, ts], place[:, ts, None, :].to_broadcast([P, n, TOPK, E]),
                        top_place[:, ts, 0:TOPK, None].to_broadcast([P, n, TOPK, E]), ALU.is_equal))
                    chained(nc.vector.tensor_tensor(
                        picked[:, ts], picked[:, ts], comb[:, ts, None, :].to_broadcast([P, n, TOPK, E]), ALU.mult))
                    nc.vector.tensor_reduce(weight[:, ts, :], picked[:, ts], AX.X, ALU.add).then_inc(weights_ready, 1)

            def step(b):
                for slot in range(GROUPS):
                    if (b + 1).real:
                        for g in range(*S_SLOTS[slot]):
                            reduce(b + 1, g)
                    if slot == 3 and (b + 2).real:
                        par = (b + 2).par
                        dve.wait_ge(qk_evac, (b + 2).val(2, 2))
                        if b.real:
                            dve.wait_ge(parts_out[par], b.half(48, 48))
                        nc.vector.tensor_copy(parts[par][:, 0], qk32[:]).then_inc(hi_ready, 1)
                    if slot == 4 and (b + -1).real:
                        c = b + -1
                        dve.wait_ge(oT_done, c.val(1, 1))
                        view = m_bank[0][:].rearrange("p (g w) -> p g w", w=32)
                        nc.vector.reciprocal(rden[:], view[:, :, 2 * HD:4 * HD:HD]).then_inc(recip_done, 1)
                        dve.wait_ge(recip_done, c.val(1, 1))
                        nc.vector.tensor_tensor(
                            on[:].rearrange("p t (g i d) -> p (t g) i d", i=2, d=HD),
                            view[:, :, 0:2 * HD].rearrange("p g (i d) -> p g i d", d=HD),
                            rden[:, :, :, None].to_broadcast([P, QT * 8, 2, HD]), ALU.mult).then_inc(norm_done, 1)
                    if slot == 5 and (b + 1).real:
                        c = b + 1
                        dve.wait_ge(v_done, c.val(1, 1))
                        if (b + -1).real:
                            dve.wait_ge(av_done, (b + -1).val(BURSTS, BURSTS))
                        else:
                            dve.wait_ge(v_ones, 6)
                        for i in range(2):
                            nc.vector.tensor_tensor(
                                vaug[c.par][:].rearrange("p t (g i) w -> p (t g) (i w)", i=2)[:, :, i * 40:i * 40 + HD],
                                m_bank[1][:, 0:QT * D].rearrange("p (g i d) -> p g i d", i=2, d=HD)[:, :, i, :],
                                bv[:].rearrange("p t (g i d) -> p (t g) i d", i=2, d=HD)[:, :, i, :],
                                ALU.add).then_inc(v_evac, 1)
                    if slot == 6 and (b + 2).real:
                        par = (b + 2).par
                        dve.wait_ge(rest_ready, (b + 2).val(1, 1))
                        nc.vector.tensor_copy(parts[par][:, 1], rest[:]).then_inc(mid_ready, 1)
                    if slot == 7 and (b + 3).real:
                        c = b + 3
                        first = (x_in, 16) if c.c == 0 else (x_rest_in, 16)
                        layer_norm_stats(tiles_of(x_all, c), stats1, mv1, ln1_stats, ln1_mv, c, first)
                    if slot == 8 and (b + 3).real:
                        c = b + 3
                        dve.wait_ge(ln1_rstd, c.val(1, 1))
                        if (b + 2).real:
                            dve.wait_ge(xnT_done, (b + 2).val(1, 1))
                        for t, src in enumerate(tiles_of(x_all, c)):
                            nc.vector.tensor_scalar(xn[:, t, :], src, mv1[:, t, 0:1], rstd1[:, t:t + 1],
                                                    ALU.subtract, ALU.mult).then_inc(xn_ready, 1)
                    if slot == 9 and (b + -1).real:
                        c = b + -1
                        dve.wait_ge(wo_done, c.val(1, 1))
                        dve.wait_ge(xb_ready, c.val(1, 1))
                        nc.vector.tensor_tensor(
                            x1_all[:, bass.ds(c.tile(QT), QT), :], m_bank[1][:, 0:QT * D].rearrange("p (t d) -> p t d", d=D),
                            x_all[:, bass.ds(c.tile(QT), QT), :], ALU.add).then_inc(x1_ready, 1)
                        layer_norm_stats(tiles_of(x1_all, c), stats2, mv2, ln2_stats, ln2_mv, c,
                                         (x1_ready, c.val(1, 1)))
                    if slot == 10 and (b + -1).real:
                        c = b + -1
                        dve.wait_ge(ln2_rstd, c.val(1, 1))
                        if (b + -2).real:
                            dve.wait_ge(x1n_saved, (b + -2).val(1, 1))
                        for t, src in enumerate(tiles_of(x1_all, c)):
                            nc.vector.tensor_scalar(x1n[:, t, :], src, mv2[:, t, 0:1], rstd2[:, t:t + 1],
                                                    ALU.subtract, ALU.mult).then_inc(x1n_ready, 1)
                    if slot == 11 and (b + -1).real:
                        c = b + -1
                        dve.wait_ge(gate_done, c.val(1, 1))
                        nc.vector.tensor_copy(logits[:, bass.ds(c.tile(QT), QT), 0:E],
                                              m_bank[1][:, 0:32].rearrange("p (t e) -> p t e", e=16)[:, :, 0:E]
                                              ).then_inc(gate_evac, 1)
                    if b.c in ROUND_AT and slot in (7, 9, 11):
                        choose(ROUND_AT[b.c], (slot - 7) // 2)

            steps(dve, step)

            for part in range(3):
                choose(len(ROUNDS) - 1, part)

            dve.wait_ge(tiles_counted, 1)
            chained(nc.vector.tensor_tensor(tile_ge[:], m_bank[1][0:E, 0:16], full[0:E, :], ALU.is_gt))
            chained(nc.vector.tensor_reduce(n_tiles[:], tile_ge[:], AX.X, ALU.add))
            nc.vector.tensor_copy(n_tiles_b[:], n_tiles[:]).then_inc(n_ready, 1)
            nc.vector.tensor_scalar(skip[:], n_tiles[:], -1.0, float(UNIT), ALU.mult, ALU.add)
            nc.vector.scalar_tensor_tensor(out=pad_at[:, 0:E], in0=m_bank[1][:, 16:16 + E], scalar=-1.0, in1=place0[:],
                                           op0=ALU.add, op1=ALU.add).then_inc(tables_ready, 1)
            dve.wait_ge(ends_done, 1)
            chained(nc.vector.tensor_copy(ends[:], o_bank[0][0:E, 0:1]))
            nc.vector.tensor_scalar(passed[:, 0, :], tile_no[0:E, :], ends[:], None, ALU.is_ge)
            nc.vector.tensor_scalar(passed[:, 1, :], tile_no[0:E, :], ends[:], skip[:], ALU.is_ge, ALU.mult
                                    ).then_inc(passed_ready, 1)
            dve.wait_ge(tiles_known, 1)
            nc.vector.tensor_copy(tile_e[:], o_bank[1][:, 0:SLOT_TILES])
            chained(nc.vector.tensor_tensor(tile_row[:], o_bank[1][:, SLOT_TILES:2 * SLOT_TILES], tile_no[:], ALU.add))
            chained(nc.vector.tensor_scalar(tile_row[:], tile_row[:], float(E * UNIT), float(P), ALU.min, ALU.mult))
            nc.vector.tensor_copy(tile_row_i[:], tile_row[:]).then_inc(tables_ready, 1)
            nc.vector.tensor_scalar(slot_row[:], tile_row[:], own[:], None, ALU.add).then_inc(tables_ready, 1)
            dve.wait_ge(ffn_w_in, 16 * 6)
            for e in range(EA):
                nc.vector.tensor_scalar(w2[:, e, :], w2[:, e, :], mult[:, e:e + 1], None, ALU.mult).then_inc(w2_scaled, 1)
            nc.vector.memset(lmax[:, 0:1], 0.0).then_inc(sh_a, 1)
            nc.vector.memset(lmax[:, 1:2], 0.0).then_inc(sh_added, 2)

            with dve.Fori(0, BATCHES // 2) as i:
                for n in range(4):
                    dve.wait_ge(sh_gelu, 4 * i + n + 1)
                    nc.vector.scalar_tensor_tensor(out=act_[:, n, :], in0=h_bank[n][:, 0:SEQ], scalar=b1[:, E + n % 2, 0:1],
                                                   in1=gelu[:, n, :], op0=ALU.add, op1=ALU.mult).then_inc(sh_a, 1)
                for k in range(2):
                    dve.wait_ge(sh_y_done, 2 * i + k + 1)
                    tile = x1_all[:, bass.ds((2 * i + k) * QT, QT), :]
                    nc.vector.tensor_tensor(tile, o_bank[k][:, 0:QT * D].rearrange("p (t d) -> p t d", d=D), tile,
                                            ALU.add).then_inc(sh_added, 1)


            experts = Experts(mybir.EngineType.DVE)

            def step(g):
                now, prev, nxt = g, g + -1, g + 1

                def bias1(u):
                    if now.real:
                        dve.wait_ge(h_done, now.val(UNROLL, u + 1))
                        if prev.real and u == 0:
                            dve.wait_ge(a_done, prev.val(UNROLL, UNROLL))
                        nc.vector.tensor_tensor(hb[:, u, :], h_bank[u][:, 0:2 * F],
                                                b1_row[:, bass.ds(experts.of(now)[u], 1), :].rearrange("p o f -> p (o f)"),
                                                ALU.add).then_inc(hb_ready, 1)

                def geglu(u):
                    if now.real:
                        dve.wait_ge(ge_done, now.val(UNROLL, u + 1))
                        if prev.real:
                            dve.wait_ge(aT_done, prev.val(UNROLL, u + 1))
                        nc.vector.tensor_tensor(ae[:, u, :], hb[:, u, 0:F], ge[:, u, :], ALU.mult).then_inc(a_done, 1)

                def bias2(u):
                    if prev.real:
                        dve.wait_ge(y_done, prev.val(UNROLL, u // 2 * 2 + 2))
                        if (prev + -1).real:
                            dve.wait_ge(scattered[u], prev.val(16, 0))
                        nc.vector.tensor_tensor(ye[:, u, :], o_bank[u // 2][:, (u % 2) * D:(u % 2 + 1) * D],
                                                b2_row[:, bass.ds(experts.of(prev)[u], 1), :].rearrange("p o f -> p (o f)"),
                                                ALU.add).then_inc(y_taken, 1)
                        nc.vector.tensor_copy(home[:, u:u + 1], home_f[:, bass.ds(prev.val(UNROLL, u), 1)]
                                              ).then_inc(y_ready, 1)

                def home_op(k):
                    if not nxt.real:
                        return
                    at = bass.ds(nxt.val(UNROLL, 0), UNROLL)
                    if k == 0:
                        dve.wait_ge(x_turned, nxt.val(UNROLL, UNROLL))
                        if now.real:
                            dve.wait_ge(home_step, now.val(3, 3))
                        op = nc.vector.tensor_tensor(which_k[:], slots[nxt.par][:, :, D + 1], slot_row[:, at], ALU.subtract)
                    elif k == 1:
                        dve.wait_ge(home_step, nxt.val(3, 1))
                        op = nc.vector.tensor_scalar(which_k[:], which_k[:], 1.0, -1.0, ALU.min, ALU.max)
                    else:
                        dve.wait_ge(home_step, nxt.val(3, 2))
                        op = nc.vector.scalar_tensor_tensor(out=home_f[:, at], in0=which_k[:], scalar=float(T),
                                                            in1=slots[nxt.par][:, :, D], op0=ALU.mult, op1=ALU.add)
                    op.then_inc(home_step, 1)

                bias1(0)
                bias1(1)
                home_op(0)
                geglu(0)
                bias1(2)
                home_op(1)
                geglu(1)
                bias2(0)
                home_op(2)
                bias2(1)
                geglu(2)
                bias1(3)
                if nxt.real and now.par == 0:
                    experts.of(nxt)
                bias2(2)
                bias2(3)
                geglu(3)

            group_steps(dve, step, -1, 2)

            n = TILES // CHUNKS
            for c in range(CHUNKS):
                ts = slice(c * n, (c + 1) * n)
                dve.wait_ge(y_in[c], 16 * TOPK)
                for t in range(c * n, (c + 1) * n):
                    nc.vector.scalar_tensor_tensor(out=x1_all[:, t, :], in0=y_all[:, 0, t, :],
                                                   scalar=weight[:, t, 0:1], in1=x1_all[:, t, :],
                                                   op0=ALU.mult, op1=ALU.add).then_inc(added, 1)
                dve.wait_ge(weighed, 2 * n * (c + 1))
                dve.wait_ge(added, (n + 1) * c + n)
                nc.vector.tensor_tensor(x1_all[:, ts, :], x1_all[:, ts, :], y_all[:, 1, ts, :], ALU.add).then_inc(added, 1)
                dve.wait_ge(added, (n + 1) * (c + 1))
                nc.vector.tensor_tensor(x1_all[:, ts, :], x1_all[:, ts, :], y_all[:, 2, ts, :], ALU.add
                                        ).then_inc(combined, 1)

        @block.gpsimd
        def _(pool):
            g = nc.gpsimd
            for k, m in enumerate((ident, identb)):
                g.memset(m[:], 0.0).then_inc(const_zero, 1)
                pool.wait_ge(const_zero, k + 1)
                g.affine_select(out=m[:], in_=m[:], compare_op=ALU.not_equal, fill=1.0, base=0,
                                pattern=[[-1, P]], channel_multiplier=1).then_inc(consts, 1)
            for k, (m, step_, mult_) in enumerate(((mask_s, -1, 1), (mask_t, 1, -1))):
                g.memset(m[:], 0.0).then_inc(const_zero, 1)
                pool.wait_ge(const_zero, k + 3)
                g.affine_select(out=m[:], in_=m[:], compare_op=ALU.is_ge, fill=MASKED, base=0,
                                pattern=[[step_, P]], channel_multiplier=mult_).then_inc(consts, 1)
            g.memset(half[:], -0.5).then_inc(half_ready, 1)
            g.memset(eps[:], EPS).then_inc(half_ready, 1)
            g.memset(zero32[:], 0.0).then_inc(half_ready, 1)
            g.memset(mparts[:], 0.0).then_inc(half_ready, 1)
            for m in (qx[0], kx[0], qx[1], kx[1]):
                g.memset(m[:].rearrange("p h t -> p (h t)").bitcast(F32), 0.0).then_inc(x_zeroed, 1)
            pool.wait_ge(half_ready, 4)
            kw = dict(allow_small_or_imprecise_dtypes=True)
            g.memset(ones[:], 1.0).then_inc(iotas, 1)
            g.memset(ones32[:], 1.0).then_inc(iotas, 1)
            for k, (m, first) in enumerate(((before, -1), (upto, 0))):
                g.memset(m[:], 1.0).then_inc(const_zero, 1)
                pool.wait_ge(const_zero, k + 5)
                g.affine_select(out=m[:], in_=m[:], compare_op=ALU.is_ge, fill=0.0, base=first,
                                pattern=[[1, P]], channel_multiplier=-1).then_inc(iotas, 1)
            g.iota(place0[:], pattern=[[REGION, E]], base=1, channel_multiplier=0, **kw).then_inc(iotas, 1)
            g.iota(full[:], pattern=[[P, SEQ // HEADS]], base=0, channel_multiplier=0, **kw).then_inc(iotas, 1)
            g.iota(tile_no[:], pattern=[[1, SLOT_TILES]], base=0, channel_multiplier=0, **kw).then_inc(iotas, 1)
            g.iota(own[:], pattern=[[1, 1]], base=0, channel_multiplier=1, **kw).then_inc(iotas, 1)
            g.iota(rows_all[:, :, D], pattern=[[P, TILES]], base=T, channel_multiplier=1, **kw).then_inc(const_zero, 1)
            g.memset(pad_rows[:], 0.0).then_inc(const_zero, 1)
            pool.wait_ge(const_zero, 8)
            g.memset(pad_rows[:, D:D + 1], NOBODY).then_inc(iotas, 1)

            def rstd(b, mv, ve, out_, s_mv, s_ve, s_out):
                pool.wait_ge(s_mv, b.val(QT, QT))
                g.tensor_tensor(ve[:], mv[:, :, 1], eps[:], ALU.add).then_inc(s_ve, 1)
                pool.wait_ge(s_ve, b.val(1, 1))
                g.tensor_tensor(out_[:], ve[:], half[:], ALU.pow).then_inc(s_out, 1)

            def dispatch(first, end):
                for n in range(first, end):
                    t, k = divmod(n, TOPK)
                    for r, (t0, _) in enumerate(ROUNDS):
                        if n == t0 * TOPK or (n == first and t >= t0):
                            pool.wait_ge(offs_ready, r + 1)
                            pool.wait_ge(x1n_saved, ROUNDS[r][1] // QT)
                    g.indirect_dma_start(out=slots_dram, out_offset=bass.IndirectOffsetOnAxis(
                        ap=to_slot[:, t, k:k + 1].bitcast(U32), axis=0), in_=rows_all[:, t, :],
                        in_offset=None).then_inc(dispatched, 16)

            def cut(r):
                return mparts[:, :, r * HEADS:(r + 1) * HEADS]

            def step(b):
                if b.c == -3:
                    for i in range(2):
                        g.memset(qy[i][:].rearrange("p h t -> p (h t)").bitcast(F32), 0.0).then_inc(y_zeroed, 1)
                        g.memset(vaug[i][:], 0.0).then_inc(v_ones, 1)
                    pool.wait_ge(v_ones, 2)
                    for i in range(2):
                        for k in range(2):
                            v = vaug[i][:].rearrange("p t (g i) w -> p (t g) (i w)", i=2)
                            g.memset(v[:, :, k * 40 + 2 * HD:k * 40 + 2 * HD + 1], 1.0).then_inc(v_ones, 1)
                if (b + 2).real:
                    c = b + 2
                    par = c.par
                    pool.wait_ge(hi_ready, c.val(1, 1))
                    g.tensor_tensor(rest[:], qk32[:], parts[par][:, 0], ALU.subtract).then_inc(rest_ready, 1)
                    pool.wait_ge(mid_ready, c.val(1, 1))
                    g.tensor_tensor(parts[par][:, 2], rest[:], parts[par][:, 1], ALU.subtract).then_inc(lo_ready, 1)
                if (b + 3).real:
                    c = b + 3
                    rstd(c, mv1, ve1, rstd1, ln1_mv, ln1_ve, ln1_rstd)
                if (b + 1).real:
                    c = b + 1
                    pool.wait_ge(s_reduced, c.val(GROUPS, GROUPS))
                    if b.real:
                        pool.wait_ge(mT_done, b.val(1, 1))
                    g.tensor_tensor(cut(0), negm[:], zero32[:], ALU.add).then_inc(mcut, 1)
                    pool.wait_ge(mcut, c.val(3, 1))
                    g.tensor_tensor(mrest[:], negm[:], cut(0), ALU.subtract).then_inc(mcut, 1)
                    pool.wait_ge(mcut, c.val(3, 2))
                    g.tensor_tensor(cut(1), mrest[:], zero32[:], ALU.add).then_inc(mcut, 1)
                    pool.wait_ge(mcut, c.val(3, 3))
                    g.tensor_tensor(cut(2), mrest[:], cut(1), ALU.subtract).then_inc(msplit, 1)
                if (b + 1).real:
                    c = b + 1
                    xs = x_all[:, bass.ds(c.tile(QT), QT), :]
                    pool.wait_ge(xn_ready, c.val(QT, QT))
                    g.tensor_tensor(xs, xs, bo[:], ALU.add).then_inc(xb_ready, 1)
                if b.c == BATCHES:
                    rstd(b + -1, mv2, ve2, rstd2, ln2_mv, ln2_ve, ln2_rstd)
                if b.c in DISPATCH_AT:
                    dispatch(*DISPATCH_AT[b.c])
                if (b + -1).real and b.c < BATCHES:
                    rstd(b + -1, mv2, ve2, rstd2, ln2_mv, ln2_ve, ln2_rstd)

            pool.wait_ge(attn_w_in, 16 * 11)
            steps(pool, step)

            dispatch(DISPATCH_AT[BATCHES][1], TILES * TOPK)
            with pool.Fori(0, ROW_GROUPS) as i:
                for u in range(UNROLL):
                    if u % 2 == 0:
                        pool.wait_ge(y_ready, UNROLL * i + u + 2)
                        g.tensor_tensor(held[:, bass.ds(UNROLL * i + u, 1)], own[:], own[:], ALU.add)
                    g.indirect_dma_start(out=y_dram, out_offset=bass.IndirectOffsetOnAxis(
                        ap=home[:, u:u + 1].bitcast(U32), axis=0), in_=ye[:, u, :], in_offset=None,
                        bounds_check=TOPK * T - 1, oob_is_err=False).then_inc(scattered[u], 16)


_HOST = {
    "x": lambda a: a["x"],
    "ctxT": lambda a: a["ctx_1024"].reshape(BATCHES * SEQ, D).T,
    "WqT": lambda a: by_dim(a["L0_xattn_Wq"]).T,
    "WkT": lambda a: by_dim(a["L0_xattn_Wk"]).T,
    "WvT": lambda a: a["L0_xattn_Wv"].T,
    "WoT": lambda a: a["L0_xattn_Wo"].T,
    "bq": lambda a: by_dim(a["L0_xattn_bq"].reshape(D, 1)),
    "bk": lambda a: by_dim(a["L0_xattn_bk"].reshape(D, 1)),
    "bv": lambda a: a["L0_xattn_bv"].reshape(1, D),
    "bo": lambda a: a["L0_xattn_bo"].reshape(1, D),
    "gateT": lambda a: a["L0_ffn_gate_w"].T,
    "w1T": lambda a: _stack(a["L0_ffn_fc1_w"].reshape(E, 2, F, D), a["L0_ffn_s_fc1_w"].reshape(2, SHARED, F, D)
                            .transpose(1, 0, 2, 3)).transpose(3, 0, 1, 2).reshape(D, EA, 2 * F),
    "b1": lambda a: _stack(a["L0_ffn_fc1_b"].reshape(E, 2, F), a["L0_ffn_s_fc1_b"].reshape(2, SHARED, F)
                           .transpose(1, 0, 2)).transpose(2, 0, 1),
    "w2T": lambda a: _stack(a["L0_ffn_fc2_w"], a["L0_ffn_s_fc2_w"].reshape(D, SHARED, F).transpose(1, 0, 2))
    .transpose(2, 0, 1),
    "mult": lambda a: _stack(a["L0_ffn_geglu_mult"], a["L0_ffn_s_geglu_mult"].reshape(SHARED, F)).T,
    "b1_row": lambda a: _stack(a["L0_ffn_fc1_b"].reshape(1, -1).T, a["L0_ffn_s_fc1_b"].reshape(-1, 1)[0:2 * F]).T,
    "b2_row": lambda a: _stack(a["L0_ffn_fc2_b"], a["L0_ffn_s_fc2_b"].reshape(1, D)).reshape(1, (E + 1) * D),
}


def by_dim(w):
    return w.reshape(HEADS, HD, -1).transpose(1, 0, 2).reshape(D, -1)


def _stack(a, b):
    return np.concatenate([a, b], axis=0)


def kernel(**inputs):
    import concourse.bacc as bacc
    from concourse.bass_utils import run_bass_kernel_spmd

    given = {k: np.asarray(v) for k, v in inputs.items()}
    nc = bacc.Bacc("TRN2", target_bir_lowering=False, num_devices=1)
    arrays, ins = {}, {}
    for name, lay in _HOST.items():
        arrays[f"in_{name}"] = np.ascontiguousarray(lay(given))
        ins[name] = nc.dram_tensor(f"in_{name}", arrays[f"in_{name}"].shape, F32, kind="ExternalInput").ap()
    out = nc.dram_tensor("out", (BATCHES, SEQ, D), F32, kind="ExternalOutput").ap()
    build(nc, ins, out)
    r = run_bass_kernel_spmd(nc, [arrays], core_ids=[0])
    return r.results[0]["out"]
```

```python
from contextlib import ExitStack

import numpy as np

import concourse.bass as bass
from concourse import mybir

F32 = mybir.dt.float32
BF16 = mybir.dt.bfloat16
I32 = mybir.dt.int32
U32 = mybir.dt.uint32
ACT = mybir.ActivationFunctionType
ALU = mybir.AluOpType
AX = mybir.AxisListType

P = 128
BATCHES, SEQ, D = 8, 256, 128
HEADS = 16
HD = D // HEADS
QT = SEQ // P
TILES = BATCHES * QT
E, TOPK, F, FS = 15, 3, 128, 256
SHARED = FS // F
EA = E + SHARED
SCALE = float(HD) ** -0.5
EPS = 1e-5
MASKED = -3.0e38
BANK = 512
GROUPS = 12
BURSTS = 6
TOPW = E + 1 + 8

T = BATCHES * SEQ
ROW = D + 2
REGION = T + P
UNIT = REGION // P
LAP = 4
UNROLL = 4
SLOT_TILES = -(-(T * TOPK // P + E - 1) // UNROLL) * UNROLL
ROW_GROUPS = SLOT_TILES // UNROLL
CHUNKS = 4
ROUNDS = [(0, 8), (8, 12), (12, 16)]
ROUND_AT = {5: 0, 7: 1}
PLACES_AT = {(6, 11): 0, (8, 4): 1}
DISPATCH_AFTER = {6: (0, 8), 7: (8, 18), 8: (26, 48)}
DISPATCH_BEFORE = {8: (18, 26)}
IOTAS = 9
TABLES = 3
SHARED_AT = {6: [("h", 0)], 8: [("h", 1)], 9: [("y", 0), ("h", 2)], 11: [("y", 1)]}
NOBODY = 1.0e6

Q_ROWS = [(0, 0, 3), (3, 0, 2), (5, 0, 1)]
K_ROWS = [(0, 0, 1), (1, 0, 1), (2, 0, 1), (3, 1, 1), (4, 1, 1), (5, 2, 1)]
QX_ROWS = [(0, 0, 2), (2, 0, 1)]
KX_ROWS = [(0, 0, 1), (1, 0, 1), (2, 1, 1)]
M_ROW = 6 * HD
S_SLOTS = [(0, 2), (2, 4), (4, 6), (6, 8), (8, 10), (10, 11), (11, 12)] + [(12, 12)] * 5


class Batch:

    def __init__(self, c, turn=None):
        self.c, self.turn = c, turn

    def __add__(self, n):
        return Batch(self.c + n, self.turn)

    @property
    def real(self):
        return 0 <= self.c < BATCHES

    @property
    def par(self):
        return self.c % 2

    def val(self, per, k):
        v = per * self.c + k
        return v if self.turn is None else self.turn * (2 * per) + v

    def half(self, per, k):
        v = per * (self.c // 2) + k
        return v if self.turn is None else self.turn * per + v

    def tile(self, width):
        v = self.c * width
        return v if self.turn is None else self.turn * (2 * width) + v


def steps(eng, step):
    for c in range(-3, 1):
        step(Batch(c))
    with eng.Fori(0, 2) as turn:
        step(Batch(1, turn))
        step(Batch(2, turn))
    for c in range(5, BATCHES + 1):
        step(Batch(c))


class Group(Batch):

    def __add__(self, n):
        return Group(self.c + n, self.turn)

    @property
    def real(self):
        return 0 <= self.c < ROW_GROUPS

    def val(self, per, k):
        v = per * self.c + k
        return v if self.turn is None else self.turn * (LAP * per) + v

    def half(self, per, k):
        v = per * (self.c // 2) + k
        return v if self.turn is None else self.turn * (LAP // 2 * per) + v


def group_steps(eng, step, first, end):
    turns = (ROW_GROUPS - 1 - 2) // LAP
    for c in range(first, 2):
        step(Group(c))
    with eng.Fori(0, turns) as turn:
        for c in range(2, 2 + LAP):
            step(Group(c, turn))
    for c in range(2 + LAP * turns, end):
        step(Group(c))


def head_of(r, i, j):
    return 8 * r + 2 * j + i


def build(nc, ins, out):
    with ExitStack() as ctx:
        def sb(name, shape, dt=F32):
            return ctx.enter_context(nc.sbuf_tensor(name, shape, dt))

        def ps(name):
            return ctx.enter_context(nc.psum_tensor(name, [P, BANK], F32))

        def sem(name):
            return ctx.enter_context(nc.semaphore(name))

        s_bank = [ps("s_bank0"), ps("s_bank1")]
        t_bank = [ps("t_bank0"), ps("t_bank1")]
        o_bank = [ps("o_bank0"), ps("o_bank1")]
        m_bank = [ps("m_bank0"), ps("m_bank1")]

        parts_dram = nc.dram_tensor("parts_dram", [2, 2, 3, P, SEQ], BF16).ap()
        slots_dram = nc.dram_tensor("slots_dram", [(E + 1) * REGION, ROW], F32).ap()
        y_dram = nc.dram_tensor("y_dram", [TOPK * T, D], F32).ap()

        ident = sb("ident", [P, P])
        identb = sb("identb", [P, P], BF16)
        mask_s = sb("mask_s", [P, P], BF16)
        mask_t = sb("mask_t", [P, P], BF16)
        half = sb("half", [P, 2])
        eps = sb("eps", [P, 2])
        warm = sb("warm", [P, 2])
        flag = sb("flag", [P, 1])
        wq = sb("wq", [D, D])
        wk = sb("wk", [D, D])
        wv = sb("wv", [D, D])
        wo = sb("wo", [D, D])
        bq = sb("bq", [P, 1])
        bk = sb("bk", [P, 1])
        bv = sb("bv", [P, QT, D])
        bo = sb("bo", [P, QT, D])
        gate = sb("gate", [D, E])
        w1 = sb("w1", [D, EA, 2 * F])
        b1 = sb("b1", [F, EA, 2])
        w2 = sb("w2", [F, EA, D])
        mult = sb("mult", [F, EA])
        b1_row = sb("b1_row", [P, E + 1, 2 * F])
        b2_row = sb("b2_row", [P, E + 1, D])
        before = sb("before", [P, P], BF16)
        upto = sb("upto", [P, P], BF16)
        ones = sb("ones", [P, P], BF16)
        ones32 = sb("ones32", [1, P])
        place0 = sb("place0", [P, E])
        full = sb("full", [P, SEQ // HEADS])
        tile_no = sb("tile_no", [P, SLOT_TILES])
        own = sb("own", [P, 1])
        pad_rows = sb("pad_rows", [P, ROW])

        x_all = sb("x_all", [P, TILES, D])
        x1_all = sb("x1_all", [P, TILES, D])
        x1nT_all = sb("x1nT_all", [D, TILES * P])
        ctxT = [sb(f"ctxT{i}", [D, SEQ]) for i in range(2)]
        stats1 = sb("stats1", [P, QT, 6])
        mv1 = sb("mv1", [P, QT, 2])
        ve1 = sb("ve1", [P, QT])
        rstd1 = sb("rstd1", [P, QT])
        xn = sb("xn", [P, QT, D])
        xnT = sb("xnT", [D, SEQ])
        qk32 = sb("qk32", [P, 2, SEQ])
        rest = sb("rest", [P, 2, SEQ])
        parts = [sb(f"parts{i}", [P, 3, 2, SEQ], BF16) for i in range(2)]
        qk_max = sb("qk_max", [P, 4, HEADS, SEQ], BF16)
        qx = [qk_max[:, i] for i in range(2)]
        kx = [qk_max[:, 2 + i] for i in range(2)]
        qy = [sb(f"qy{i}", [P, HEADS, SEQ], BF16) for i in range(2)]
        ky = [sb(f"ky{i}", [P, HEADS, SEQ], BF16) for i in range(2)]
        negm = sb("negm", [P, QT, HEADS])
        mrest = sb("mrest", [P, QT, HEADS])
        zero32 = sb("zero32", [P, QT, HEADS])
        mparts = sb("mparts", [P, QT, P], BF16)
        mT = sb("mT", [3 * HEADS, SEQ], BF16)
        vaug = [sb(f"vaug{i}", [P, QT, HEADS, 32]) for i in range(2)]
        probs = sb("probs", [P, 4, BANK])
        o_sb = sb("o_sb", [P, BANK])
        rden = sb("rden", [P, QT * 2 * 4, 2])
        on = sb("on", [P, QT, D])
        onT = sb("onT", [D, SEQ])
        stats2 = sb("stats2", [P, QT, 6])
        mv2 = sb("mv2", [P, QT, 2])
        ve2 = sb("ve2", [P, QT])
        rstd2 = sb("rstd2", [P, QT])
        x1n = sb("x1n", [P, QT, D])
        x1nT = sb("x1nT", [D, SEQ])
        logits = sb("logits", [P, TILES, E + 1])

        x_in = sem("x_in")
        x_rest_in = sem("x_rest_in")
        ctx_in = [sem("ctx_in0"), sem("ctx_in1")]
        attn_w_in = sem("attn_w_in")
        w2_in = sem("w2_in")
        ffn_w_in = sem("ffn_w_in")
        parts_out = [sem("parts_out0"), sem("parts_out1")]
        x_load = [sem("x_load0"), sem("x_load1")]
        y_load = [sem("y_load0"), sem("y_load1")]
        m_load = [sem("m_load0"), sem("m_load1")]
        x_zeroed = sem("x_zeroed")
        y_zeroed = sem("y_zeroed")
        v_ones = sem("v_ones")
        const_zero = sem("const_zero")
        consts = sem("consts")
        half_ready = sem("half_ready")
        ky_zero = sem("ky_zero")
        flag_set = sem("flag_set")
        mcut = sem("mcut")
        ln1_stats = sem("ln1_stats")
        ln1_mv = sem("ln1_mv")
        ln1_ve = sem("ln1_ve")
        ln1_rstd = sem("ln1_rstd")
        xn_ready = sem("xn_ready")
        xb_ready = sem("xb_ready")
        xnT_done = sem("xnT_done")
        xnT_evac = sem("xnT_evac")
        qk_done = sem("qk_done")
        qk_evac = sem("qk_evac")
        v_done = sem("v_done")
        v_evac = sem("v_evac")
        hi_ready = sem("hi_ready")
        mid_ready = sem("mid_ready")
        lo_ready = sem("lo_ready")
        rest_ready = sem("rest_ready")
        s_done = sem("s_done")
        s_reduced = sem("s_reduced")
        msplit = sem("msplit")
        mT_done = sem("mT_done")
        mT_evac = sem("mT_evac")
        t_done = sem("t_done")
        exp_done = sem("exp_done")
        av_done = sem("av_done")
        o_evac = sem("o_evac")
        oT_done = sem("oT_done")
        recip_done = sem("recip_done")
        norm_done = sem("norm_done")
        onT_done = sem("onT_done")
        onT_evac = sem("onT_evac")
        wo_done = sem("wo_done")
        x1_ready = sem("x1_ready")
        ln2_stats = sem("ln2_stats")
        ln2_mv = sem("ln2_mv")
        ln2_ve = sem("ln2_ve")
        ln2_rstd = sem("ln2_rstd")
        x1n_ready = sem("x1n_ready")
        x1nT_done = sem("x1nT_done")
        x1nT_evac = sem("x1nT_evac")
        gate_done = sem("gate_done")
        gate_evac = sem("gate_evac")
        x1n_saved = sem("x1n_saved")

        def within(m, first, n, w):
            flat = m[:].rearrange("p h t -> p (h t)").bitcast(F32)
            return flat[:, first:first + n * w].rearrange("p (n w) -> p n w", w=w)

        lmax = sb("lmax", [P, TILES])
        probs_e = sb("probs_e", [P, TILES, TOPW])
        zsum = sb("zsum", [P, TILES])
        zinv = sb("zinv", [P, TILES])
        top8 = sb("top8", [P, TILES, 8])
        marked = sb("marked", [P, TILES, TOPW])
        wsum = sb("wsum", [P, TILES])
        winv = sb("winv", [P, TILES])
        comb = sb("comb", [P, TILES, E])
        rows_all = sb("rows_all", [P, TILES, ROW])
        mask_e = sb("mask_e", [P, TILES, E], BF16)
        place = sb("place", [P, TILES, E])
        top_place = sb("top_place", [P, TILES, 8])
        to_slot = sb("to_slot", [P, TILES, TOPK], I32)
        picked = sb("picked", [P, TILES, TOPK, E])
        weight = sb("weight", [P, TILES, TOPK])
        tile_ge = sb("tile_ge", [E, P // HD])
        n_tiles = sb("n_tiles", [E, 1])
        n_tiles_b = sb("n_tiles_b", [E, 1], BF16)
        skip = sb("skip", [E, 1])
        ends = sb("ends", [E, 1])
        passed = sb("passed", [E, 2, SLOT_TILES], BF16)
        tile_e = sb("tile_e", [P, SLOT_TILES], I32)
        tile_row = sb("tile_row", [P, SLOT_TILES])
        tile_row_i = sb("tile_row_i", [P, SLOT_TILES], I32)
        slot_row = sb("slot_row", [P, SLOT_TILES])
        pad_at = sb("pad_at", [P, 16], I32)
        gelu = within(qy[0], 0, 4, SEQ)
        act_ = within(qy[0], 4 * SEQ, 4, SEQ)
        slots = [within(qy[1], i * UNROLL * ROW, UNROLL, ROW) for i in range(2)]
        hb = within(ky[1], UNROLL * D, UNROLL, 2 * F)
        sxT = [within(ky[0], 0, UNROLL, P), within(ky[1], UNROLL * (D + 2 * F), UNROLL, P)]
        ge = within(ky[0], UNROLL * P, UNROLL, F)
        ae = within(ky[0], 2 * UNROLL * P, UNROLL, F)
        aeT = within(ky[0], 3 * UNROLL * P, UNROLL, P)
        ye = within(ky[1], 0, UNROLL, D)
        which_k = sb("which_k", [P, UNROLL])
        home_f = sb("home_f", [P, SLOT_TILES])
        home = sb("home", [P, UNROLL], I32)
        held = sb("held", [P, SLOT_TILES])
        rank_mark = sb("rank_mark", [P, 4])
        seq = sem("gate_math")
        less_max = sem("less_max")
        exp_gate = sem("exp_gate")
        w2_scaled = sem("w2_scaled")
        iotas = sem("iotas")
        mask_ready = sem("mask_ready")
        ranked = sem("ranked")
        rank_read = sem("rank_read")
        offs_ready = sem("offs_ready")
        tiles_counted = sem("tiles_counted")
        n_ready = sem("n_ready")
        ends_done = sem("ends_done")
        passed_ready = sem("passed_ready")
        tiles_known = sem("tiles_known")
        tables_ready = sem("tables_ready")
        dispatched = sem("dispatched")
        padded = sem("padded")
        sh_h_done = sem("sh_h_done")
        sh_gelu = sem("sh_gelu")
        sh_a = sem("sh_a")
        sh_y_done = sem("sh_y_done")
        sh_added = sem("sh_added")
        slot_in = [[sem(f"slot_in{i}{u}") for u in range(UNROLL)] for i in range(2)]
        x_turned = sem("x_turned")
        sxT_evac = sem("sxT_evac")
        h_done = sem("h_done")
        hb_ready = sem("hb_ready")
        ge_done = sem("ge_done")
        a_done = sem("a_done")
        aT_done = sem("aT_done")
        aT_evac = sem("aT_evac")
        y_done = sem("y_done")
        home_step = sem("home_step")
        y_ready = sem("y_ready")
        y_taken = sem("y_taken")
        scattered = [sem(f"scattered{u}") for u in range(UNROLL)]
        y_in = [sem(f"y_in{c}") for c in range(CHUNKS)]
        combined = sem("combined")
        weights_ready = sem("weights_ready")
        weighed = sem("weighed")
        added = sem("added")
        paired = sem("paired")
        out_done = sem("out_done")
        h_bank = s_bank + t_bank
        y_all = qk_max[:].rearrange("p n h t -> p (n h t)").bitcast(F32).rearrange(
            "p (k t d) -> p k t d", t=TILES, d=D)[:, 0:TOPK]

        def reg_values(src, engine, top, why):
            return nc.values_load_multi_w_load_instructions(src, engines=[engine], min_val=0, max_val=top,
                                                            skip_runtime_bounds_check_because=why)[1]

        def rank_bank(r):
            return m_bank[0] if r == len(ROUNDS) - 1 else s_bank[0]

        class Experts:

            def __init__(self, engine):
                self.engine, self.held = engine, {}

            def of(self, g):
                if (g.c, g.turn is None) not in self.held:
                    self.held[g.c, g.turn is None] = reg_values(
                        tile_e[0:1, bass.ds(g.val(UNROLL, 0), UNROLL)], self.engine, E, "counts at most E ends")
                return self.held[g.c, g.turn is None]

        def rows(dram, par, which, first, n):
            return dram[par, which, first:first + n].rearrange("r (d h) t -> (r d) (h t)", h=HEADS)

        block = ctx.enter_context(nc.Block())

        @block.sync
        def _(sp):
            x_v = ins["x"].rearrange("b (j p) d -> p (b j) d", p=P)
            sp.dma_start(x_all[:, 0:QT, :], x_v[:, 0:QT, :]).then_inc(x_in, 16)
            sp.dma_start(wq[:], ins["WqT"]).then_inc(attn_w_in, 16)
            sp.dma_start(wk[:], ins["WkT"]).then_inc(attn_w_in, 16)
            sp.dma_start(bq[:], ins["bq"]).then_inc(attn_w_in, 16)
            sp.dma_start(bk[:], ins["bk"]).then_inc(attn_w_in, 16)
            sp.dma_start(wv[:], ins["WvT"]).then_inc(attn_w_in, 16)
            for t in range(QT):
                sp.dma_start(bv[:, t, :], ins["bv"].partition_broadcast(P)).then_inc(attn_w_in, 16)
                sp.dma_start(bo[:, t, :], ins["bo"].partition_broadcast(P)).then_inc(attn_w_in, 16)
            sp.dma_start(wo[:], ins["WoT"]).then_inc(attn_w_in, 16)
            sp.dma_start(gate[:], ins["gateT"]).then_inc(attn_w_in, 16)
            sp.dma_start(x_all[:, QT:, :], x_v[:, QT:, :]).then_inc(x_rest_in, 16)

            def store_part(par, r):
                sp.dma_start(parts_dram[par, :, r].rearrange("k p t -> p k t"),
                             parts[par][:, r]).then_inc(parts_out[par], 16)

            def load(dst, which, table, par, done):
                for row, first, n in table:
                    sp.dma_start(dst[row * HD:(row + n) * HD].rearrange("p h t -> p (h t)"),
                                 rows(parts_dram, par, which, first, n)).then_inc(done, 16)

            def step(b):
                if (b + 1).real:
                    c, par = b + 1, (b + 1).par
                    if (b + -1).real:
                        sp.wait_ge(t_done, (b + -1).val(GROUPS, GROUPS))
                    else:
                        sp.wait_ge(y_zeroed, 4)
                    sp.wait_ge(parts_out[par], c.half(48, 48))
                    load(qy[par], 0, Q_ROWS, par, y_load[par])
                    load(ky[par], 1, K_ROWS, par, y_load[par])
                if (b + 3).real:
                    if (b + 1).real:
                        sp.wait_ge(v_done, (b + 1).val(1, 1))
                    sp.dma_start(ctxT[(b + 3).par][:], ins["ctxT"][:, bass.ds((b + 3).tile(SEQ), SEQ)]
                                 ).then_inc(ctx_in[(b + 3).par], 16)
                if (b + 2).real:
                    c, par = b + 2, (b + 2).par
                    sp.wait_ge(hi_ready, c.val(1, 1))
                    store_part(par, 0)
                    sp.wait_ge(mid_ready, c.val(1, 1))
                    store_part(par, 1)
                    sp.wait_ge(parts_out[par], c.half(48, 32))
                    if not b.real:
                        sp.wait_ge(x_zeroed, 2 * (c.c + 1))
                    load(qx[par], 0, QX_ROWS, par, x_load[par])
                    load(kx[par], 1, KX_ROWS, par, x_load[par])
                    sp.wait_ge(lo_ready, c.val(1, 1))
                    store_part(par, 2)
                if b.c == 5:
                    sp.dma_start(w2[:], ins["w2T"]).then_inc(w2_in, 16)
                    sp.dma_start(mult[:], ins["mult"]).then_inc(w2_in, 16)
                    sp.dma_start(w1[:], ins["w1T"]).then_inc(ffn_w_in, 16)
                    sp.dma_start(b1[:], ins["b1"]).then_inc(ffn_w_in, 16)
                if b.c == 6:
                    sp.dma_start(b1_row[:].rearrange("p e f -> p (e f)"),
                                 ins["b1_row"].partition_broadcast(P)).then_inc(ffn_w_in, 16)
                    sp.dma_start(b2_row[:].rearrange("p e f -> p (e f)"),
                                 ins["b2_row"].partition_broadcast(P)).then_inc(ffn_w_in, 16)

            steps(sp, step)

            sp.wait_ge(iotas, IOTAS)
            sp.dma_start(slots_dram[E * REGION:E * REGION + P, :], pad_rows[:]).then_inc(padded, 16)
            sp.wait_ge(tables_ready, 1)
            at = reg_values(pad_at[0:1, 0:E], mybir.EngineType.SP, E * REGION, "a region has room for its rows")
            for e in range(E):
                sp.dma_start(slots_dram[bass.ds(at[e], P), :], pad_rows[:]).then_inc(padded, 16)
            sp.wait_ge(tables_ready, TABLES)
            sp.wait_ge(padded, 16 * (E + 1))
            sp.wait_ge(dispatched, 16 * TILES * TOPK)

            def load_group(g):
                row = reg_values(tile_row_i[0:1, bass.ds(g.val(UNROLL, 0), UNROLL)], mybir.EngineType.SP, E * REGION,
                                 "the last region's first row is the maximum")
                if (g + -2).real:
                    sp.wait_ge(home_step, (g + -2).val(3, 3))
                for u in range(UNROLL):
                    sp.dma_start(slots[g.par][:, u, :], slots_dram[bass.ds(row[u], P), :]).then_inc(slot_in[g.par][u], 16)

            group_steps(sp, load_group, 0, ROW_GROUPS)
            for u in range(UNROLL):
                sp.wait_ge(scattered[u], 16 * ROW_GROUPS)
            y_v = y_dram.rearrange("(k t p) d -> p k t d", k=TOPK, p=P)
            n = TILES // CHUNKS
            for c in range(CHUNKS):
                for k in range(TOPK):
                    sp.dma_start(y_all[:, k, c * n:(c + 1) * n, :], y_v[:, k, c * n:(c + 1) * n, :]).then_inc(y_in[c], 16)
            out_v = out.rearrange("b (j p) d -> p (b j) d", p=P)
            for c in range(CHUNKS):
                sp.wait_ge(combined, c + 1)
                sp.dma_start(out_v[:, c * n:(c + 1) * n, :], x1_all[:, c * n:(c + 1) * n, :]).then_inc(out_done, 16)
            sp.wait_ge(out_done, 16 * CHUNKS)

        @block.tensor
        def _(pe):
            mm = nc.tensor.matmul

            def s_group(b, g):
                bank = s_bank[g % 2]
                n = GROUPS * b.c + g
                if g == 0:
                    pe.wait_ge(x_load[b.par], b.half(80, 80))
                if n >= 2:
                    pe.wait_ge(s_reduced, b.val(GROUPS, g - 1))
                if g < 4:
                    heads, keys, tile = range(4 * g, 4 * g + 4), P, 0
                else:
                    heads, keys, tile = range(2 * (g - 4), 2 * (g - 4) + 2), 2 * P, 1
                view = bank[:].rearrange("p (h k) -> p h k", k=keys)
                mm(view[:, :, keys - P:], identb[:], mask_s[:, None, :].to_broadcast([P, len(heads), P]),
                   start=True, stop=True)
                for k, h in enumerate(heads):
                    last = mm(view[:, k, :], qx[b.par][:, h, tile * P:(tile + 1) * P], kx[b.par][:, h, 0:keys],
                              start=False, stop=True, skip_group_check=True)
                last.then_inc(s_done, 1)

            def t_group(b, g):
                bank = t_bank[g % 2]
                if g == 0:
                    pe.wait_ge(y_load[b.par], b.half(144, 144))
                    pe.wait_ge(m_load[b.par], b.half(16, 16))
                if GROUPS * b.c + g >= 2:
                    pe.wait_ge(exp_done, b.val(GROUPS, g - 1))
                if g < 8:
                    r, i, jj = g // 4, g // 2 % 2, g % 2
                    heads = [head_of(r, i, 2 * jj + k) for k in range(2)]
                    queries, key0 = slice(0, 2 * P), 0
                else:
                    r, i = (g - 8) // 2, g % 2
                    heads = [head_of(r, i, j) for j in range(4)]
                    queries, key0 = slice(P, 2 * P), P
                view = bank[:].rearrange("p (h q) -> p h q", h=len(heads))
                mm(view[:, :, 0:P], identb[:], mask_t[:, None, :].to_broadcast([P, len(heads), P]),
                   start=True, stop=True)
                for k, h in enumerate(heads):
                    last = mm(view[:, k, :], ky[b.par][:, h, key0:key0 + P], qy[b.par][:, h, queries],
                              start=False, stop=True, skip_group_check=True)
                last.then_inc(t_done, 1)

            def av_burst(b, m):
                if m == 0:
                    pe.wait_ge(v_evac, b.val(2, 2))
                pe.wait_ge(exp_done, b.val(GROUPS, 2 * m + 2))
                bank = o_bank[b.par]
                for k in range(4 if m < 4 else 8):
                    if m < 4:
                        r, i, j, kt, q0 = m // 2, m % 2, k, 0, 0
                        src = probs[:, (2 * m + k // 2) % 4, (k % 2) * 2 * P:(k % 2 + 1) * 2 * P]
                    else:
                        r, i, j, kt, q0 = m - 4, k // 4, k % 4, 1, P
                        src = probs[:, (2 * m + i) % 4, j * P:(j + 1) * P]
                    last = mm(bank[32 * j:32 * j + 32, r * SEQ + q0:(r + 1) * SEQ],
                              vaug[b.par][:, kt, head_of(r, i, j), :], src,
                              start=(m == 0), stop=True, skip_group_check=True)
                last.then_inc(av_done, 1)

            def xn_transposes(b):
                pe.wait_ge(xn_ready, b.val(QT, QT))
                if (b + -2).real:
                    pe.wait_ge(mT_evac, (b + -2).val(1, 1))
                for t in range(QT):
                    last = nc.tensor.transpose(m_bank[0][:, t * P:(t + 1) * P], xn[:, t, :], ident[:])
                last.then_inc(xnT_done, 1)

            def qk_proj(b):
                if (b + -2).real:
                    pe.wait_ge(v_evac, (b + -2).val(2, 2))
                pe.wait_ge(xnT_evac, b.val(1, 1))
                pe.wait_ge(ctx_in[b.par], b.half(16, 16))
                mm(m_bank[1][:, 0:SEQ], wq[:], xnT[:], start=True, stop=True)
                mm(m_bank[1][:, SEQ:2 * SEQ], wk[:], ctxT[b.par][:], start=True, stop=True).then_inc(qk_done, 1)

            def v_proj(b):
                if (b + 1).real:
                    pe.wait_ge(qk_evac, (b + 1).val(2, 2))
                else:
                    pe.wait_ge(gate_evac, (b + -3).val(1, 1))
                for t in range(QT):
                    last = mm(m_bank[1][:, t * D:(t + 1) * D], ctxT[b.par][:, t * P:(t + 1) * P], wv[:],
                              start=True, stop=True)
                last.then_inc(v_done, 1)

            def o_transposes(b):
                pe.wait_ge(o_evac, b.val(1, 1))
                if (b + 3).real:
                    pe.wait_ge(xnT_evac, (b + 3).val(1, 1))
                elif (b + 1).real:
                    pe.wait_ge(mT_evac, (b + 1).val(1, 1))
                else:
                    pe.wait_ge(onT_evac, (b + -1).val(1, 1))
                for t in range(QT):
                    for r in range(2):
                        last = nc.tensor.transpose(m_bank[0][:, (2 * t + r) * P:(2 * t + r + 1) * P],
                                                   o_sb[:, r * SEQ + t * P:r * SEQ + (t + 1) * P], ident[:])
                last.then_inc(oT_done, 1)

            def on_transposes(b):
                pe.wait_ge(norm_done, b.val(1, 1))
                for t in range(QT):
                    last = nc.tensor.transpose(m_bank[0][:, t * P:(t + 1) * P], on[:, t, :], ident[:])
                last.then_inc(onT_done, 1)

            def out_proj(b):
                pe.wait_ge(onT_evac, b.val(1, 1))
                if (b + 2).real:
                    pe.wait_ge(v_evac, (b + 2).val(2, 2))
                elif (b + -1).real:
                    pe.wait_ge(gate_evac, (b + -1).val(1, 1))
                for t in range(QT):
                    last = mm(m_bank[1][:, t * D:(t + 1) * D], onT[:, t * P:(t + 1) * P], wo[:],
                              start=True, stop=True)
                last.then_inc(wo_done, 1)

            def m_transposes(b):
                pe.wait_ge(msplit, b.val(1, 1))
                if (b + -2).real:
                    pe.wait_ge(onT_evac, (b + -2).val(1, 1))
                elif (b + 1).real:
                    pe.wait_ge(xnT_evac, (b + 1).val(1, 1))
                dst = m_bank[0][:].bitcast(BF16)
                for t in range(QT):
                    last = nc.tensor.transpose(dst[:, t * P:(t + 1) * P], mparts[:, t, :], identb[:])
                last.then_inc(mT_done, 1)

            def x1n_transposes(b):
                pe.wait_ge(x1n_ready, b.val(QT, QT))
                for t in range(QT):
                    last = nc.tensor.transpose(m_bank[1][:, t * P:(t + 1) * P], x1n[:, t, :], ident[:])
                last.then_inc(x1nT_done, 1)

            def gate_logits(b):
                pe.wait_ge(x1nT_evac, b.val(2, 2))
                for t in range(QT):
                    last = mm(m_bank[1][:, 16 * t:16 * t + E], x1nT[:, t * P:(t + 1) * P], gate[:],
                              start=True, stop=True)
                last.then_inc(gate_done, 1)

            def rank(r):
                t0, t1 = ROUNDS[r]
                view = rank_bank(r)[:, 0:(t1 - t0) * E].rearrange("p (t e) -> p t e", e=E)
                pe.wait_ge(mask_ready, r + 1)
                last = mm(view, before[:], mask_e[:, t0:t1, :], start=True, stop=True)
                for t in range(t1 - 1):
                    lo = max(t + 1, t0)
                    last = mm(view[:, lo - t0:, :], ones[:], mask_e[:, t:t + 1, :].to_broadcast([P, t1 - lo, E]),
                              start=False, stop=True, skip_group_check=True)
                last.then_inc(ranked, 1)

            def shared(what, c):
                if what == "h":
                    if c == 0:
                        pe.wait_ge(ffn_w_in, 16 * 4)
                        pe.wait_ge(w2_scaled, 1)
                        pe.wait_ge(rank_read, len(ROUNDS) - 1)
                        pe.wait_ge(exp_done, GROUPS * BATCHES)
                    if c >= 2:
                        pe.wait_ge(sh_a, SHARED * (c - 1))
                    xc = x1nT_all[:, c * SEQ:(c + 1) * SEQ]
                    for h in range(SHARED):
                        bank = h_bank[c % 2 * SHARED + h]
                        mm(bank[:, 0:SEQ], w1[:, E + h, 0:F], xc, start=True, stop=True)
                        mm(bank[:, SEQ:], w1[:, E + h, F:], xc, start=True, stop=True).then_inc(sh_h_done, 1)
                else:
                    pe.wait_ge(sh_a, SHARED * (c + 1))
                    if c:
                        pe.wait_ge(sh_added, c)
                    for t in range(QT):
                        yb = o_bank[0][:, t * P:(t + 1) * P]
                        mm(yb, ones32[:], b2_row[0:1, E, :], start=True, stop=False)
                        for h in range(SHARED):
                            last = mm(yb, act_[:, c % 2 * SHARED + h, t * P:(t + 1) * P], w2[:, E + h, :],
                                      start=False, stop=(h == SHARED - 1))
                    last.then_inc(sh_y_done, 1)

            pe.wait_ge(consts, 1)

            def step(b):
                for slot in range(GROUPS):
                    if (b + 1).real:
                        for g in range(*S_SLOTS[slot]):
                            s_group(b + 1, g)
                    if b.real:
                        t_group(b, slot)
                    if slot == 0 and (b + 2).real:
                        xn_transposes(b + 2)
                    if slot == 2 and b.c == -2:
                        pe.wait_ge(attn_w_in, 16 * 11)
                        pe.wait_ge(consts, 4)
                    if slot == 2 and (b + 2).real:
                        qk_proj(b + 2)
                    if slot == 3 and (b + -1).real:
                        o_transposes(b + -1)
                    if slot == 4 and (b + 1).real:
                        v_proj(b + 1)
                    if slot == 6 and (b + -1).real:
                        on_transposes(b + -1)
                    if slot == 7 and (b + -1).real:
                        out_proj(b + -1)
                    if slot == 9 and (b + 1).real:
                        m_transposes(b + 1)
                    if slot == 10 and (b + -1).real:
                        x1n_transposes(b + -1)
                    if slot == 11 and (b + -1).real:
                        gate_logits(b + -1)
                    if (b.c, slot) in PLACES_AT:
                        rank(PLACES_AT[b.c, slot])
                    if b.c == BATCHES:
                        for what, c in SHARED_AT.get(slot, []):
                            shared(what, c)
                    if slot == 1 and (b + -1).real:
                        av_burst(b + -1, BURSTS - 1)
                    if slot % 2 and slot >= 3 and b.real:
                        av_burst(b, (slot - 3) // 2)

            steps(pe, step)

            shared("h", 3)
            rank(len(ROUNDS) - 1)
            for t in range(TILES):
                mm(m_bank[1][0:E, 0:16], mask_e[:, t, :], ones[:, 0:16], start=(t == 0), stop=(t == TILES - 1))
            for t in range(TILES):
                last = mm(m_bank[1][:, 16:16 + E], ones[:], mask_e[:, t, :], start=False, stop=True,
                          skip_group_check=True)
            last.then_inc(tiles_counted, 1)
            shared("y", 2)
            shared("h", 4)
            shared("y", 3)
            pe.wait_ge(n_ready, 1)
            mm(m_bank[0][0:E, 0:16], upto[0:E, 0:E], n_tiles_b[:].to_broadcast([E, 16]), start=True, stop=True
               ).then_inc(ends_done, 1)
            shared("y", 4)
            pe.wait_ge(passed_ready, 1)
            mm(o_bank[1][:, 0:2 * SLOT_TILES], ones[0:E, :], passed[:].rearrange("p a j -> p (a j)"),
               start=True, stop=True).then_inc(tiles_known, 1)
            for c in range(5, BATCHES):
                shared("h", c)
                if c > 5:
                    shared("y", c - 1)
            shared("y", BATCHES - 1)

            pe.wait_ge(sh_added, BATCHES)
            pe.wait_ge(tables_ready, TABLES)

            experts = Experts(mybir.EngineType.PE)

            def step(g):
                now, prev, nxt = g, g + -1, g + 1

                def turn_x(u):
                    if nxt.real:
                        pe.wait_ge(slot_in[nxt.par][u], nxt.half(16, 16))
                        nc.tensor.transpose(m_bank[0][:, u * P:(u + 1) * P], slots[nxt.par][:, u, 0:D], ident[:]
                                            ).then_inc(x_turned, 1)

                def fc1(u):
                    if now.real:
                        pe.wait_ge(sxT_evac, now.val(1, 1))
                        if prev.real:
                            pe.wait_ge(hb_ready, prev.val(UNROLL, u + 1))
                        mm(h_bank[u][:, 0:2 * F], sxT[now.par][:, u, :], w1[:, bass.ds(experts.of(now)[u], 1), :].rearrange("p o f -> p (o f)"),
                           start=True, stop=True).then_inc(h_done, 1)

                def turn_a(u):
                    if prev.real:
                        pe.wait_ge(a_done, prev.val(UNROLL, u + 1))
                        nc.tensor.transpose(m_bank[1][:, (u % 2) * P:(u % 2 + 1) * P], ae[:, u, :], ident[:]
                                            ).then_inc(aT_done, 1)

                def fc2(u):
                    if prev.real:
                        pe.wait_ge(aT_evac, prev.val(2, u // 2 + 1))
                        if (prev + -1).real and u % 2 == 0:
                            pe.wait_ge(y_taken, (prev + -1).val(UNROLL, u + 2))
                        mm(o_bank[u // 2][:, (u % 2) * D:(u % 2 + 1) * D], aeT[:, u, :],
                           w2[:, bass.ds(experts.of(prev)[u], 1), :].rearrange("p o f -> p (o f)"), start=True, stop=True
                           ).then_inc(y_done, 1)

                fc1(0)
                turn_a(0)
                turn_a(1)
                fc1(1)
                for u in range(UNROLL):
                    turn_x(u)
                if prev.real:
                    experts.of(prev)
                fc1(2)
                fc2(0)
                fc2(1)
                turn_a(2)
                turn_a(3)
                fc1(3)
                if nxt.real and (now.turn is None or now.c < 1 + LAP):
                    experts.of(nxt)
                fc2(2)
                fc2(3)

            group_steps(pe, step, -1, ROW_GROUPS + 1)

        @block.scalar
        def _(act):
            act.wait_ge(half_ready, 1)
            nc.scalar.activation(warm[:], half[:], ACT.Exp)

            def shared_gelu(c):
                if c >= 2:
                    act.wait_ge(sh_a, SHARED * (c - 1))
                for h in range(SHARED):
                    n = c % 2 * SHARED + h
                    act.wait_ge(sh_h_done, SHARED * c + h + 1)
                    nc.scalar.activation(gelu[:, n, :], h_bank[n][:, SEQ:], ACT.Gelu,
                                         bias=b1[:, E + h, 1:2]).then_inc(sh_gelu, 1)

            def exp_round(r):
                t0, t1 = ROUNDS[r]
                act.wait_ge(less_max, r + 1)
                nc.scalar.activation(probs_e[:, t0:t1, 0:E], probs_e[:, t0:t1, 0:E], ACT.Exp).then_inc(exp_gate, 1)

            def step(b):
                for slot in range(GROUPS):
                    if b.real:
                        g = slot
                        act.wait_ge(t_done, b.val(GROUPS, g + 1))
                        if g >= 4:
                            act.wait_ge(av_done, b.val(BURSTS, (g - 4) // 2 + 1))
                        elif (b + -1).real:
                            act.wait_ge(av_done, b.val(BURSTS, (g - 4) // 2 + 1))
                        nc.scalar.activation(probs[:, g % 4, :], t_bank[g % 2][:], ACT.Exp,
                                             scale=SCALE).then_inc(exp_done, 1)
                    if slot == 8 and b.c in ROUND_AT:
                        exp_round(ROUND_AT[b.c])
                    if slot == 0 and (b + 2).real:
                        act.wait_ge(xnT_done, (b + 2).val(1, 1))
                        if (b + 1).real:
                            act.wait_ge(qk_done, (b + 1).val(1, 1))
                        nc.scalar.activation(xnT[:], m_bank[0][:, 0:SEQ], ACT.Identity).then_inc(xnT_evac, 1)
                    if slot == 2 and (b + -1).real:
                        act.wait_ge(av_done, (b + -1).val(BURSTS, BURSTS))
                        nc.scalar.activation(o_sb[:], o_bank[(b + -1).par][:], ACT.Identity).then_inc(o_evac, 1)
                    if slot == 2 and b.c == -2:
                        act.wait_ge(attn_w_in, 16 * 11)
                    if slot == 2 and (b + 2).real:
                        act.wait_ge(qk_done, (b + 2).val(1, 1))
                        if (b + 1).real:
                            act.wait_ge(rest_ready, (b + 1).val(1, 1))
                        for k, bias in enumerate((bq, bk)):
                            nc.scalar.activation(qk32[:, k, :], m_bank[1][:, k * SEQ:(k + 1) * SEQ], ACT.Identity,
                                                 bias=bias[:]).then_inc(qk_evac, 1)
                    if slot == 6 and (b + -1).real:
                        act.wait_ge(onT_done, (b + -1).val(1, 1))
                        nc.scalar.activation(onT[:], m_bank[0][:, 0:SEQ], ACT.Identity).then_inc(onT_evac, 1)
                    if slot == 9 and (b + 1).real:
                        act.wait_ge(mT_done, (b + 1).val(1, 1))
                        if b.real:
                            act.wait_ge(m_load[b.par], b.half(16, 16))
                        nc.scalar.activation(mT[:], m_bank[0][:].bitcast(BF16)[0:3 * HEADS, 0:SEQ],
                                             ACT.Identity).then_inc(mT_evac, 1)
                        act.wait_ge(mT_evac, (b + 1).val(1, 1))
                        if (b + -1).real:
                            act.wait_ge(t_done, (b + -1).val(GROUPS, GROUPS))
                        else:
                            act.wait_ge(y_zeroed, 4)
                        act.dma_start(qy[(b + 1).par][M_ROW:M_ROW + 3].rearrange("p h t -> p (h t)"),
                                      mT[:]).then_inc(m_load[(b + 1).par], 16)
                    if slot == 10 and (b + -1).real:
                        act.wait_ge(x1nT_done, (b + -1).val(1, 1))
                        for dst in (x1nT[:], x1nT_all[:, bass.ds((b + -1).tile(SEQ), SEQ)]):
                            nc.scalar.activation(dst, m_bank[1][:, 0:SEQ], ACT.Identity).then_inc(x1nT_evac, 1)
                        nc.scalar.activation(rows_all[:, bass.ds((b + -1).tile(QT), QT), 0:D], x1n[:],
                                             ACT.Identity).then_inc(x1n_saved, 1)
                    if b.c == BATCHES:
                        for what, c in SHARED_AT.get(slot, []):
                            if what == "h":
                                shared_gelu(c)

            steps(act, step)

            exp_round(len(ROUNDS) - 1)
            for c in range(3, BATCHES):
                shared_gelu(c)

            def step(g):
                now, prev, nxt = g, g + -1, g + 1

                def evac_x():
                    if nxt.real:
                        act.wait_ge(x_turned, nxt.val(UNROLL, UNROLL))
                        nc.scalar.activation(sxT[nxt.par], m_bank[0][:].rearrange("p (u q) -> p u q", u=UNROLL),
                                             ACT.Identity).then_inc(sxT_evac, 1)

                def gelu_e(u):
                    if now.real:
                        act.wait_ge(hb_ready, now.val(UNROLL, u + 1))
                        nc.scalar.activation(ge[:, u, :], hb[:, u, F:], ACT.Gelu).then_inc(ge_done, 1)

                def evac_a(k):
                    if prev.real:
                        act.wait_ge(aT_done, prev.val(UNROLL, 2 * k + 2))
                        if (prev + -1).real:
                            act.wait_ge(y_done, (prev + -1).val(UNROLL, 2 * k + 2))
                        nc.scalar.activation(aeT[:, 2 * k:2 * k + 2, :],
                                             m_bank[1][:, 0:2 * P].rearrange("p (u q) -> p u q", u=2),
                                             ACT.Identity).then_inc(aT_evac, 1)

                evac_a(0)
                gelu_e(0)
                evac_a(1)
                gelu_e(1)
                evac_x()
                gelu_e(2)
                gelu_e(3)

            group_steps(act, step, -1, ROW_GROUPS + 1)

            n = TILES // CHUNKS
            act.wait_ge(weights_ready, len(ROUNDS))
            for c in range(CHUNKS):
                act.wait_ge(y_in[c], 16 * TOPK)
                for t in range(c * n, (c + 1) * n):
                    for k in range(1, TOPK if t > c * n else TOPK - 1):
                        nc.scalar.activation(y_all[:, k, t, :], y_all[:, k, t, :], ACT.Copy,
                                             scale=weight[:, t, k:k + 1]).then_inc(weighed, 1)

        @block.vector
        def _(dve):
            ones_pair = float(np.uint32(0x3F803F80).view(np.float32))

            def clear_k(i):
                flat = ky[i][:].rearrange("p h t -> p (h t)").bitcast(F32)
                nc.vector.memset(flat, 0.0).then_inc(ky_zero, 1)
                dve.wait_ge(ky_zero, i + 1)
                nc.vector.memset(flat[32:64], ones_pair).then_inc(y_zeroed, 1)

            def reduce(b, g):
                dve.wait_ge(s_done, b.val(GROUPS, g + 1))
                if g == 0 and (b + -1).real:
                    dve.wait_ge(msplit, (b + -1).val(1, 1))
                if g < 4:
                    dst, keys = negm[:, 0, 4 * g:4 * g + 4], P
                else:
                    dst, keys = negm[:, 1, 2 * (g - 4):2 * (g - 4) + 2], 2 * P
                nc.vector.tensor_reduce(dst, s_bank[g % 2][:].rearrange("p (h k) -> p h k", k=keys), AX.X, ALU.max,
                                        negate=True).then_inc(s_reduced, 1)

            def held_by(sem_, value):
                dve.wait_ge(sem_, value)
                nc.vector.memset(flag[:], 0.0).then_inc(flag_set, 1)

            def layer_norm_stats(src, stats, mv, s_stats, s_mv, b, guard):
                held_by(*guard)
                for t in range(QT):
                    nc.vector.bn_stats(stats[:, t, :], src[t]).then_inc(s_stats, 1)
                held_by(s_stats, b.val(QT, QT))
                for t in range(QT):
                    nc.vector.bn_aggr(mv[:, t, :], stats[:, t, :]).then_inc(s_mv, 1)

            def tiles_of(arr, b):
                return [arr[:, bass.ds(b.tile(QT) + t, 1), :].rearrange("p o d -> p (o d)") for t in range(QT)]

            sq = [0]

            def chained(ins_):
                ins_.then_inc(seq, 1)
                sq[0] += 1
                dve.wait_ge(seq, sq[0])

            def shared(what, c):
                if what == "h":
                    for h in range(SHARED):
                        n = c % 2 * SHARED + h
                        dve.wait_ge(sh_gelu, SHARED * c + h + 1)
                        nc.vector.scalar_tensor_tensor(out=act_[:, n, :], in0=h_bank[n][:, 0:SEQ],
                                                       scalar=b1[:, E + h, 0:1], in1=gelu[:, n, :], op0=ALU.add,
                                                       op1=ALU.mult).then_inc(sh_a, 1)
                else:
                    dve.wait_ge(sh_y_done, c + 1)
                    tile = x1_all[:, c * QT:(c + 1) * QT, :]
                    nc.vector.tensor_tensor(tile, o_bank[0][:, 0:QT * D].rearrange("p (t d) -> p t d", d=D), tile,
                                            ALU.add).then_inc(sh_added, 1)

            def choose(r, part):
                t0, t1 = ROUNDS[r]
                n = t1 - t0
                ts = slice(t0, t1)
                pe_, lg, top = probs_e[:, ts, 0:E], logits[:, ts, 0:E], top8[:, ts]

                def wide(v, w=E):
                    return v[:, ts, None].to_broadcast([P, n, w])

                if part == 0:
                    dve.wait_ge(gate_evac, t1 // QT)
                    chained(nc.vector.tensor_reduce(lmax[:, ts], lg, AX.X, ALU.max))
                    nc.vector.tensor_tensor(pe_, lg, wide(lmax), ALU.subtract).then_inc(less_max, 1)
                if part == 1:
                    dve.wait_ge(exp_gate, r + 1)
                    chained(nc.vector.tensor_reduce(zsum[:, ts], pe_, AX.X, ALU.add))
                    chained(nc.vector.reciprocal(zinv[:, ts], zsum[:, ts]))
                    chained(nc.vector.tensor_tensor(pe_, pe_, wide(zinv), ALU.mult))
                    for t in range(t0, t1):
                        last = nc.vector.max(top8[:, t, :], probs_e[:, t, :])
                    chained(last)
                    chained(nc.vector.memset(top[:, :, TOPK:], -1.0))
                    for t in range(t0, t1):
                        last = nc.vector.match_replace(marked[:, t, :], top8[:, t, :], probs_e[:, t, :], -2.0)
                    chained(last)
                    nc.vector.tensor_scalar(mask_e[:, ts, :], marked[:, ts, 0:E], -2.0, None, ALU.is_equal
                                            ).then_inc(mask_ready, 1)
                    dve.wait_ge(mask_ready, r + 1)
                    chained(nc.vector.tensor_scalar(marked[:, ts, :], marked[:, ts, :], -2.0, None, ALU.is_equal))
                    chained(nc.vector.tensor_tensor(pe_, marked[:, ts, 0:E], pe_, ALU.mult))
                    chained(nc.vector.tensor_reduce(wsum[:, ts], pe_, AX.X, ALU.add))
                    chained(nc.vector.tensor_scalar(wsum[:, ts], wsum[:, ts], 1e-20, None, ALU.add))
                    chained(nc.vector.reciprocal(winv[:, ts], wsum[:, ts]))
                    nc.vector.tensor_tensor(comb[:, ts, :], pe_, wide(winv), ALU.mult)
                if part == 2:
                    dve.wait_ge(ranked, r + 1)
                    dve.wait_ge(iotas, IOTAS)
                    chained(nc.vector.tensor_tensor(
                        place[:, ts, :], rank_bank(r)[:, 0:n * E].rearrange("p (t e) -> p t e", e=E),
                        place0[:, None, :].to_broadcast([P, n, E]), ALU.add))
                    nc.vector.memset(rank_mark[:, r:r + 1], 0.0).then_inc(rank_read, 1)
                    chained(nc.vector.tensor_tensor(place[:, ts, :], place[:, ts, :], marked[:, ts, 0:E], ALU.mult))
                    for t in range(t0, t1):
                        last = nc.vector.max(top_place[:, t, :], place[:, t, :])
                    chained(last)
                    nc.vector.tensor_scalar(rows_all[:, ts, D + 1:], top_place[:, ts, 1:2], -1.0, None, ALU.add)
                    nc.vector.tensor_scalar(to_slot[:, ts, :], top_place[:, ts, 0:TOPK], -1.0, None, ALU.add
                                            ).then_inc(offs_ready, 1)
                if part == 3:
                    chained(nc.vector.tensor_tensor(
                        picked[:, ts], place[:, ts, None, :].to_broadcast([P, n, TOPK, E]),
                        top_place[:, ts, 0:TOPK, None].to_broadcast([P, n, TOPK, E]), ALU.is_equal))
                    chained(nc.vector.tensor_tensor(
                        picked[:, ts], picked[:, ts], comb[:, ts, None, :].to_broadcast([P, n, TOPK, E]), ALU.mult))
                    nc.vector.tensor_reduce(weight[:, ts, :], picked[:, ts], AX.X, ALU.add).then_inc(weights_ready, 1)

            def step(b):
                for slot in range(GROUPS):
                    if (b + 1).real:
                        for g in range(*S_SLOTS[slot]):
                            reduce(b + 1, g)
                    if slot == 3 and (b + 2).real:
                        par = (b + 2).par
                        dve.wait_ge(qk_evac, (b + 2).val(2, 2))
                        if b.real:
                            dve.wait_ge(parts_out[par], b.half(48, 48))
                        nc.vector.tensor_copy(parts[par][:, 0], qk32[:]).then_inc(hi_ready, 1)
                    if slot == 4 and (b + -1).real:
                        c = b + -1
                        dve.wait_ge(oT_done, c.val(1, 1))
                        view = m_bank[0][:].rearrange("p (g w) -> p g w", w=32)
                        nc.vector.reciprocal(rden[:], view[:, :, 2 * HD:4 * HD:HD]).then_inc(recip_done, 1)
                        dve.wait_ge(recip_done, c.val(1, 1))
                        nc.vector.tensor_tensor(
                            on[:].rearrange("p t (g i d) -> p (t g) i d", i=2, d=HD),
                            view[:, :, 0:2 * HD].rearrange("p g (i d) -> p g i d", d=HD),
                            rden[:, :, :, None].to_broadcast([P, QT * 8, 2, HD]), ALU.mult).then_inc(norm_done, 1)
                    if slot == 5 and (b + 1).real:
                        c = b + 1
                        dve.wait_ge(v_done, c.val(1, 1))
                        if (b + -1).real:
                            dve.wait_ge(av_done, (b + -1).val(BURSTS, BURSTS))
                        else:
                            dve.wait_ge(v_ones, 6)
                        for i in range(2):
                            nc.vector.tensor_tensor(
                                vaug[c.par][:].rearrange("p t (g i) w -> p (t g) (i w)", i=2)[:, :, i * 40:i * 40 + HD],
                                m_bank[1][:, 0:QT * D].rearrange("p (g i d) -> p g i d", i=2, d=HD)[:, :, i, :],
                                bv[:].rearrange("p t (g i d) -> p (t g) i d", i=2, d=HD)[:, :, i, :],
                                ALU.add).then_inc(v_evac, 1)
                    if slot == 6 and (b + 2).real:
                        par = (b + 2).par
                        dve.wait_ge(rest_ready, (b + 2).val(1, 1))
                        nc.vector.tensor_copy(parts[par][:, 1], rest[:]).then_inc(mid_ready, 1)
                    if slot == 7 and (b + 3).real:
                        c = b + 3
                        first = (x_in, 16) if c.c == 0 else (x_rest_in, 16)
                        layer_norm_stats(tiles_of(x_all, c), stats1, mv1, ln1_stats, ln1_mv, c, first)
                    if slot == 9 and (b + -1).real:
                        c = b + -1
                        dve.wait_ge(wo_done, c.val(1, 1))
                        dve.wait_ge(xb_ready, c.val(1, 1))
                        nc.vector.tensor_tensor(
                            x1_all[:, bass.ds(c.tile(QT), QT), :], m_bank[1][:, 0:QT * D].rearrange("p (t d) -> p t d", d=D),
                            x_all[:, bass.ds(c.tile(QT), QT), :], ALU.add).then_inc(x1_ready, 1)
                        layer_norm_stats(tiles_of(x1_all, c), stats2, mv2, ln2_stats, ln2_mv, c,
                                         (x1_ready, c.val(1, 1)))
                    if slot == 9 and (b + 3).real:
                        c = b + 3
                        dve.wait_ge(ln1_rstd, c.val(1, 1))
                        if (b + 2).real:
                            dve.wait_ge(xnT_done, (b + 2).val(1, 1))
                        for t, src in enumerate(tiles_of(x_all, c)):
                            nc.vector.tensor_scalar(xn[:, t, :], src, mv1[:, t, 0:1], rstd1[:, t:t + 1],
                                                    ALU.subtract, ALU.mult).then_inc(xn_ready, 1)
                    if slot == 10 and (b + -1).real:
                        c = b + -1
                        dve.wait_ge(ln2_rstd, c.val(1, 1))
                        if (b + -2).real:
                            dve.wait_ge(x1n_saved, (b + -2).val(1, 1))
                        for t, src in enumerate(tiles_of(x1_all, c)):
                            nc.vector.tensor_scalar(x1n[:, t, :], src, mv2[:, t, 0:1], rstd2[:, t:t + 1],
                                                    ALU.subtract, ALU.mult).then_inc(x1n_ready, 1)
                    if slot == 11 and (b + -1).real:
                        c = b + -1
                        dve.wait_ge(gate_done, c.val(1, 1))
                        nc.vector.tensor_copy(logits[:, bass.ds(c.tile(QT), QT), 0:E],
                                              m_bank[1][:, 0:32].rearrange("p (t e) -> p t e", e=16)[:, :, 0:E]
                                              ).then_inc(gate_evac, 1)
                    if slot == 11 and b.c == -2:
                        clear_k(0)
                        clear_k(1)
                        nc.vector.memset(probs_e[:], -1.0).then_inc(ky_zero, 1)
                    if b.c in ROUND_AT and slot in (7, 11):
                        choose(ROUND_AT[b.c], (slot - 7) // 4)
                    if (b.c, slot) in PLACES_AT:
                        choose(PLACES_AT[b.c, slot], 2)
                        choose(PLACES_AT[b.c, slot], 3)
                    if b.c == BATCHES:
                        for what, c in SHARED_AT.get(slot, []):
                            shared(what, c)

            steps(dve, step)

            choose(len(ROUNDS) - 1, 0)
            choose(len(ROUNDS) - 1, 1)
            choose(len(ROUNDS) - 1, 2)

            dve.wait_ge(tiles_counted, 1)
            chained(nc.vector.tensor_tensor(tile_ge[:], m_bank[1][0:E, 0:16], full[0:E, :], ALU.is_gt))
            chained(nc.vector.tensor_reduce(n_tiles[:], tile_ge[:], AX.X, ALU.add))
            nc.vector.tensor_copy(n_tiles_b[:], n_tiles[:]).then_inc(n_ready, 1)
            nc.vector.tensor_scalar(skip[:], n_tiles[:], -1.0, float(UNIT), ALU.mult, ALU.add)
            nc.vector.scalar_tensor_tensor(out=pad_at[:, 0:E], in0=m_bank[1][:, 16:16 + E], scalar=-1.0, in1=place0[:],
                                           op0=ALU.add, op1=ALU.add).then_inc(tables_ready, 1)
            shared("h", 3)
            shared("y", 2)
            dve.wait_ge(ends_done, 1)
            chained(nc.vector.tensor_copy(ends[:], m_bank[0][0:E, 0:1]))
            nc.vector.tensor_scalar(passed[:, 0, :], tile_no[0:E, :], ends[:], None, ALU.is_ge)
            nc.vector.tensor_scalar(passed[:, 1, :], tile_no[0:E, :], ends[:], skip[:], ALU.is_ge, ALU.mult
                                    ).then_inc(passed_ready, 1)
            shared("y", 3)
            shared("h", 4)
            shared("y", 4)
            dve.wait_ge(tiles_known, 1)
            nc.vector.tensor_copy(tile_e[:], o_bank[1][:, 0:SLOT_TILES])
            chained(nc.vector.tensor_tensor(tile_row[:], o_bank[1][:, SLOT_TILES:2 * SLOT_TILES], tile_no[:], ALU.add))
            chained(nc.vector.tensor_scalar(tile_row[:], tile_row[:], float(E * UNIT), float(P), ALU.min, ALU.mult))
            nc.vector.tensor_copy(tile_row_i[:], tile_row[:]).then_inc(tables_ready, 1)
            nc.vector.tensor_scalar(slot_row[:], tile_row[:], own[:], None, ALU.add).then_inc(tables_ready, 1)
            for c in range(5, BATCHES):
                shared("h", c)
                if c > 5:
                    shared("y", c - 1)
            choose(len(ROUNDS) - 1, 3)
            shared("y", BATCHES - 1)

            experts = Experts(mybir.EngineType.DVE)

            def step(g):
                now, prev, nxt = g, g + -1, g + 1

                def bias1(u):
                    if now.real:
                        dve.wait_ge(h_done, now.val(UNROLL, u + 1))
                        if prev.real and u == 0:
                            dve.wait_ge(a_done, prev.val(UNROLL, UNROLL))
                        nc.vector.tensor_tensor(hb[:, u, :], h_bank[u][:, 0:2 * F],
                                                b1_row[:, bass.ds(experts.of(now)[u], 1), :].rearrange("p o f -> p (o f)"),
                                                ALU.add).then_inc(hb_ready, 1)

                def geglu(u):
                    if now.real:
                        dve.wait_ge(ge_done, now.val(UNROLL, u + 1))
                        if prev.real:
                            dve.wait_ge(aT_done, prev.val(UNROLL, u + 1))
                        nc.vector.tensor_tensor(ae[:, u, :], hb[:, u, 0:F], ge[:, u, :], ALU.mult).then_inc(a_done, 1)

                def bias2(u):
                    if prev.real:
                        dve.wait_ge(y_done, prev.val(UNROLL, u // 2 * 2 + 2))
                        if (prev + -1).real:
                            dve.wait_ge(scattered[u], prev.val(16, 0))
                        nc.vector.tensor_tensor(ye[:, u, :], o_bank[u // 2][:, (u % 2) * D:(u % 2 + 1) * D],
                                                b2_row[:, bass.ds(experts.of(prev)[u], 1), :].rearrange("p o f -> p (o f)"),
                                                ALU.add).then_inc(y_taken, 1)
                        nc.vector.tensor_copy(home[:, u:u + 1], home_f[:, bass.ds(prev.val(UNROLL, u), 1)]
                                              ).then_inc(y_ready, 1)

                def home_op(k):
                    if not nxt.real:
                        return
                    at = bass.ds(nxt.val(UNROLL, 0), UNROLL)
                    if k == 0:
                        dve.wait_ge(x_turned, nxt.val(UNROLL, UNROLL))
                        if now.real:
                            dve.wait_ge(home_step, now.val(3, 3))
                        op = nc.vector.tensor_tensor(which_k[:], slots[nxt.par][:, :, D + 1], slot_row[:, at], ALU.subtract)
                    elif k == 1:
                        dve.wait_ge(home_step, nxt.val(3, 1))
                        op = nc.vector.tensor_scalar(which_k[:], which_k[:], 1.0, -1.0, ALU.min, ALU.max)
                    else:
                        dve.wait_ge(home_step, nxt.val(3, 2))
                        op = nc.vector.scalar_tensor_tensor(out=home_f[:, at], in0=which_k[:], scalar=float(T),
                                                            in1=slots[nxt.par][:, :, D], op0=ALU.mult, op1=ALU.add)
                    op.then_inc(home_step, 1)

                bias1(0)
                bias1(1)
                home_op(0)
                geglu(0)
                bias1(2)
                home_op(1)
                bias2(0)
                home_op(2)
                bias2(1)
                geglu(1)
                geglu(2)
                bias1(3)
                if nxt.real and (now.turn is None or now.c < 1 + LAP):
                    experts.of(nxt)
                bias2(2)
                bias2(3)
                geglu(3)

            group_steps(dve, step, -1, ROW_GROUPS + 1)

            n = TILES // CHUNKS
            for c in range(CHUNKS):
                ts = slice(c * n, (c + 1) * n)
                dve.wait_ge(y_in[c], 16 * TOPK)
                for t in range(c * n, (c + 1) * n):
                    nc.vector.scalar_tensor_tensor(out=x1_all[:, t, :], in0=y_all[:, 0, t, :],
                                                   scalar=weight[:, t, 0:1], in1=x1_all[:, t, :],
                                                   op0=ALU.mult, op1=ALU.add).then_inc(added, 1)
                t = c * n
                dve.wait_ge(added, (n + 1) * c + 1)
                nc.vector.scalar_tensor_tensor(out=x1_all[:, t, :], in0=y_all[:, 2, t, :], scalar=weight[:, t, 2:3],
                                               in1=x1_all[:, t, :], op0=ALU.mult, op1=ALU.add).then_inc(added, 1)
                dve.wait_ge(paired, c + 1)
                dve.wait_ge(added, (n + 1) * (c + 1))
                nc.vector.tensor_tensor(x1_all[:, ts, :], x1_all[:, ts, :], y_all[:, 1, ts, :], ALU.add
                                        ).then_inc(combined, 1)

        @block.gpsimd
        def _(pool):
            g = nc.gpsimd
            for k, m in enumerate((ident, identb)):
                g.memset(m[:], 0.0).then_inc(const_zero, 1)
                pool.wait_ge(const_zero, k + 1)
                g.affine_select(out=m[:], in_=m[:], compare_op=ALU.not_equal, fill=1.0, base=0,
                                pattern=[[-1, P]], channel_multiplier=1).then_inc(consts, 1)
            for k, (m, step_, mult_) in enumerate(((mask_s, -1, 1), (mask_t, 1, -1))):
                g.memset(m[:], 0.0).then_inc(const_zero, 1)
                pool.wait_ge(const_zero, k + 3)
                g.affine_select(out=m[:], in_=m[:], compare_op=ALU.is_ge, fill=MASKED, base=0,
                                pattern=[[step_, P]], channel_multiplier=mult_).then_inc(consts, 1)
            g.memset(half[:], -0.5).then_inc(half_ready, 1)
            g.memset(eps[:], EPS).then_inc(half_ready, 1)
            g.memset(zero32[:], 0.0).then_inc(half_ready, 1)
            g.memset(mparts[:], 0.0).then_inc(half_ready, 1)

            def zero_x(par, k):
                m = (qx, kx)[k][par]
                g.memset(m.rearrange("p h t -> p (h t)").bitcast(F32), 0.0).then_inc(x_zeroed, 1)

            zero_x(0, 0)
            pool.wait_ge(half_ready, 4)

            def rstd(b, mv, ve, out_, s_mv, s_ve, s_out):
                pool.wait_ge(s_mv, b.val(QT, QT))
                g.tensor_tensor(ve[:], mv[:, :, 1], eps[:], ALU.add).then_inc(s_ve, 1)
                pool.wait_ge(s_ve, b.val(1, 1))
                g.tensor_tensor(out_[:], ve[:], half[:], ALU.pow).then_inc(s_out, 1)

            def dispatch(first, end):
                for n in range(first, end):
                    t, k = divmod(n, TOPK)
                    for r, (t0, _) in enumerate(ROUNDS):
                        if n == t0 * TOPK or (n == first and t >= t0):
                            pool.wait_ge(offs_ready, r + 1)
                            pool.wait_ge(x1n_saved, ROUNDS[r][1] // QT)
                    g.indirect_dma_start(out=slots_dram, out_offset=bass.IndirectOffsetOnAxis(
                        ap=to_slot[:, t, k:k + 1].bitcast(U32), axis=0), in_=rows_all[:, t, :],
                        in_offset=None).then_inc(dispatched, 16)

            def cut(r):
                return mparts[:, :, r * HEADS:(r + 1) * HEADS]

            def step(b):
                if b.c == -1:
                    pool.wait_ge(attn_w_in, 16 * 11)
                if (b + 2).real:
                    c = b + 2
                    par = c.par
                    if (b + 1).real:
                        pool.wait_ge(lo_ready, (b + 1).val(1, 1))
                    pool.wait_ge(hi_ready, c.val(1, 1))
                    g.tensor_tensor(rest[:], qk32[:], parts[par][:, 0], ALU.subtract).then_inc(rest_ready, 1)
                if (b + 1).real:
                    c = b + 1
                    pool.wait_ge(s_reduced, c.val(GROUPS, GROUPS))
                    if b.real:
                        pool.wait_ge(mT_done, b.val(1, 1))
                    g.tensor_tensor(cut(0), negm[:], zero32[:], ALU.add).then_inc(mcut, 1)
                    pool.wait_ge(mcut, c.val(3, 1))
                    g.tensor_tensor(mrest[:], negm[:], cut(0), ALU.subtract).then_inc(mcut, 1)
                    pool.wait_ge(mcut, c.val(3, 2))
                    g.tensor_tensor(cut(1), mrest[:], zero32[:], ALU.add).then_inc(mcut, 1)
                    pool.wait_ge(mcut, c.val(3, 3))
                    g.tensor_tensor(cut(2), mrest[:], cut(1), ALU.subtract).then_inc(msplit, 1)
                if (b + 3).real:
                    c = b + 3
                    rstd(c, mv1, ve1, rstd1, ln1_mv, ln1_ve, ln1_rstd)
                if b.c in DISPATCH_BEFORE:
                    dispatch(*DISPATCH_BEFORE[b.c])
                if (b + -1).real:
                    rstd(b + -1, mv2, ve2, rstd2, ln2_mv, ln2_ve, ln2_rstd)
                if (b + 2).real:
                    c = b + 2
                    par = c.par
                    pool.wait_ge(mid_ready, c.val(1, 1))
                    g.tensor_tensor(parts[par][:, 2], rest[:], parts[par][:, 1], ALU.subtract).then_inc(lo_ready, 1)
                if (b + 1).real:
                    c = b + 1
                    xs = x_all[:, bass.ds(c.tile(QT), QT), :]
                    pool.wait_ge(xn_ready, c.val(QT, QT))
                    g.tensor_tensor(xs, xs, bo[:], ALU.add).then_inc(xb_ready, 1)
                if b.c in DISPATCH_AFTER:
                    dispatch(*DISPATCH_AFTER[b.c])
                if b.c == 5:
                    pool.wait_ge(w2_in, 16 * 2)
                    g.tensor_tensor(w2[:], w2[:], mult[:, :, None].to_broadcast([F, EA, D]), ALU.mult).then_inc(w2_scaled, 1)
                if b.c == -3:
                    zero_x(0, 1)
                if b.c == -2:
                    zero_x(1, 0)
                    zero_x(1, 1)
                    for i in range(2):
                        g.memset(qy[i][:].rearrange("p h t -> p (h t)").bitcast(F32), 0.0).then_inc(y_zeroed, 1)
                        g.memset(vaug[i][:], 0.0).then_inc(v_ones, 1)
                    pool.wait_ge(v_ones, 2)
                    for i in range(2):
                        for k in range(2):
                            v = vaug[i][:].rearrange("p t (g i) w -> p (t g) (i w)", i=2)
                            g.memset(v[:, :, k * 40 + 2 * HD:k * 40 + 2 * HD + 1], 1.0).then_inc(v_ones, 1)
                if b.c == 0:
                    kw = dict(allow_small_or_imprecise_dtypes=True)
                    g.memset(ones[:], 1.0).then_inc(iotas, 1)
                    g.memset(ones32[:], 1.0).then_inc(iotas, 1)
                    for k, (m, first) in enumerate(((before, -1), (upto, 0))):
                        g.memset(m[:], 1.0).then_inc(const_zero, 1)
                        pool.wait_ge(const_zero, k + 5)
                        g.affine_select(out=m[:], in_=m[:], compare_op=ALU.is_ge, fill=0.0, base=first,
                                        pattern=[[1, P]], channel_multiplier=-1).then_inc(iotas, 1)
                    g.iota(place0[:], pattern=[[REGION, E]], base=1, channel_multiplier=0, **kw).then_inc(iotas, 1)
                    g.iota(full[:], pattern=[[P, SEQ // HEADS]], base=0, channel_multiplier=0, **kw).then_inc(iotas, 1)
                    g.iota(tile_no[:], pattern=[[1, SLOT_TILES]], base=0, channel_multiplier=0, **kw).then_inc(iotas, 1)
                    g.iota(own[:], pattern=[[1, 1]], base=0, channel_multiplier=1, **kw).then_inc(iotas, 1)
                    g.iota(rows_all[:, :, D], pattern=[[P, TILES]], base=T, channel_multiplier=1, **kw).then_inc(const_zero, 1)
                    g.memset(pad_rows[:], 0.0).then_inc(const_zero, 1)
                    pool.wait_ge(const_zero, 8)
                    g.memset(pad_rows[:, D:D + 1], NOBODY).then_inc(iotas, 1)

            steps(pool, step)

            with pool.Fori(0, ROW_GROUPS) as i:
                for u in range(UNROLL):
                    if u % 2 == 0:
                        pool.wait_ge(y_ready, UNROLL * i + u + 2)
                        g.tensor_tensor(held[:, bass.ds(UNROLL * i + u, 1)], own[:], own[:], ALU.add)
                    g.indirect_dma_start(out=y_dram, out_offset=bass.IndirectOffsetOnAxis(
                        ap=home[:, u:u + 1].bitcast(U32), axis=0), in_=ye[:, u, :], in_offset=None,
                        bounds_check=TOPK * T - 1, oob_is_err=False).then_inc(scattered[u], 16)
            n = TILES // CHUNKS
            for c in range(CHUNKS):
                ts = slice(c * n + 1, (c + 1) * n)
                pool.wait_ge(weighed, (2 * n - 1) * (c + 1))
                g.tensor_tensor(y_all[:, 1, ts, :], y_all[:, 1, ts, :], y_all[:, 2, ts, :], ALU.add).then_inc(paired, 1)


_HOST = {
    "x": lambda a: a["x"],
    "ctxT": lambda a: a["ctx_1024"].reshape(BATCHES * SEQ, D).T,
    "WqT": lambda a: by_dim(a["L0_xattn_Wq"]).T,
    "WkT": lambda a: by_dim(a["L0_xattn_Wk"]).T,
    "WvT": lambda a: a["L0_xattn_Wv"].T,
    "WoT": lambda a: a["L0_xattn_Wo"].T,
    "bq": lambda a: by_dim(a["L0_xattn_bq"].reshape(D, 1)),
    "bk": lambda a: by_dim(a["L0_xattn_bk"].reshape(D, 1)),
    "bv": lambda a: a["L0_xattn_bv"].reshape(1, D),
    "bo": lambda a: a["L0_xattn_bo"].reshape(1, D),
    "gateT": lambda a: a["L0_ffn_gate_w"].T,
    "w1T": lambda a: _stack(a["L0_ffn_fc1_w"].reshape(E, 2, F, D), a["L0_ffn_s_fc1_w"].reshape(2, SHARED, F, D)
                            .transpose(1, 0, 2, 3)).transpose(3, 0, 1, 2).reshape(D, EA, 2 * F),
    "b1": lambda a: _stack(a["L0_ffn_fc1_b"].reshape(E, 2, F), a["L0_ffn_s_fc1_b"].reshape(2, SHARED, F)
                           .transpose(1, 0, 2)).transpose(2, 0, 1),
    "w2T": lambda a: _stack(a["L0_ffn_fc2_w"], a["L0_ffn_s_fc2_w"].reshape(D, SHARED, F).transpose(1, 0, 2))
    .transpose(2, 0, 1),
    "mult": lambda a: _stack(a["L0_ffn_geglu_mult"], a["L0_ffn_s_geglu_mult"].reshape(SHARED, F)).T,
    "b1_row": lambda a: _stack(a["L0_ffn_fc1_b"].reshape(1, -1).T, a["L0_ffn_s_fc1_b"].reshape(-1, 1)[0:2 * F]).T,
    "b2_row": lambda a: _stack(a["L0_ffn_fc2_b"], a["L0_ffn_s_fc2_b"].reshape(1, D)).reshape(1, (E + 1) * D),
}


def by_dim(w):
    return w.reshape(HEADS, HD, -1).transpose(1, 0, 2).reshape(D, -1)


def _stack(a, b):
    return np.concatenate([a, b], axis=0)


def kernel(**inputs):
    import concourse.bacc as bacc
    from concourse.bass_utils import run_bass_kernel_spmd

    given = {k: np.asarray(v) for k, v in inputs.items()}
    nc = bacc.Bacc("TRN2", target_bir_lowering=False, num_devices=1)
    arrays, ins = {}, {}
    for name, lay in _HOST.items():
        arrays[f"in_{name}"] = np.ascontiguousarray(lay(given))
        ins[name] = nc.dram_tensor(f"in_{name}", arrays[f"in_{name}"].shape, F32, kind="ExternalInput").ap()
    out = nc.dram_tensor("out", (BATCHES, SEQ, D), F32, kind="ExternalOutput").ap()
    build(nc, ins, out)
    r = run_bass_kernel_spmd(nc, [arrays], core_ids=[0])
    return r.results[0]["out"]
```
